# Optimizing a Trainium2 kernel written in Bass

```python
import numpy as np
import jax
import jax.numpy as jnp

def _softmax(x, axis=-1):
    return jax.nn.softmax(x, axis=axis)

def _gelu(x):
    return jax.nn.gelu(x, approximate=True)

def _silu(x):
    return jax.nn.silu(x)

def _sigmoid(x):
    return jax.nn.sigmoid(x)

def _layernorm(x, axis=-1, eps=1e-05):
    m = jnp.mean(x, axis=axis, keepdims=True)
    v = jnp.var(x, axis=axis, keepdims=True)
    return (x - m) / jnp.sqrt(v + eps)

def _scatter_add(tgt, idx, src, axis=0):
    return tgt.at[idx].add(src)

def _segment_sum(src, seg, n):
    return jax.ops.segment_sum(src, seg, n)
kernel_name = 'mk_decoder_preln_d2_seqx_r8_f4d27d'

def setup_inputs(seed: int=0):
    np.random.seed(seed)
    _w = jnp.asarray

    def _rec_inputs():
        import jax
        import jax.numpy as jnp
        _rk = jax.random.key(seed)
        x = -0.0003929 + 0.9999 * jax.random.normal(jax.random.fold_in(_rk, 1), (128, 64, 128), jnp.float32)
        _lenS = 64 - jax.random.randint(jax.random.fold_in(_rk, 7), (128,), 0, max(1, 64 // 4) + 1, jnp.int32)
        _lenS2 = 64 - jax.random.randint(jax.random.fold_in(_rk, 8), (128,), 0, max(1, 64 // 4) + 1, jnp.int32)
        _ctx_1024P = jax.random.normal(jax.random.fold_in(_rk, 11), (128, 16, 128), jnp.float32)
        _ctx_1024c = jax.random.dirichlet(jax.random.fold_in(_rk, 511), 0.3 * jnp.ones((16,), jnp.float32), (128, 64))
        _ctx_1024t = jnp.einsum('bsk,bkd->bsd', _ctx_1024c, _ctx_1024P)
        _ctx_1024t = _ctx_1024t * jax.lax.rsqrt(jnp.mean(jnp.square(_ctx_1024t)) + 1e-12) * 0.953939
        ctx_1024 = 2.81802e-05 + 1.00001 * (_ctx_1024t + 0.3 * jax.random.normal(jax.random.fold_in(_rk, 611), (128, 64, 128), jnp.float32))
        itok_BxS_0_7 = jax.random.randint(jax.random.fold_in(_rk, 12), (128, 64), 0, 8, jnp.int32)
        itok_BxS_0_4092 = jax.random.randint(jax.random.fold_in(_rk, 13), (128, 64), 0, 4093, jnp.int32)
        _validS = jnp.arange(64)[None, :] < _lenS[:, None]
        _validS2 = jnp.arange(64)[None, :] < _lenS2[:, None]
        _causal = jnp.tril(jnp.ones((64, 64), dtype=bool))
        mask_Bx1xSxS2_ff0 = jnp.where(jnp.ones((128, 1, 64, 64), dtype=bool), 0.0, -1000000000.0).astype(jnp.float32)
        return (x, ctx_1024, itok_BxS_0_7, itok_BxS_0_4092, mask_Bx1xSxS2_ff0)
    x, ctx_1024, itok_BxS_0_7, itok_BxS_0_4092, mask_Bx1xSxS2_ff0 = _rec_inputs()

    def _L0_attn_setup():
        import jax, jax.numpy as jnp
        import numpy as np
        D_MODEL = 128
        D_STATE = 16
        D_CONV = 3
        EXPAND = 2
        MLP_RATIO = 4
        HEADDIM = 64
        D_INNER = EXPAND * D_MODEL
        NHEADS = D_INNER // HEADDIM
        CONV_DIM = D_INNER + 2 * D_STATE
        D_IN_PROJ = 2 * D_INNER + 2 * D_STATE + NHEADS

        def rmsnorm(x, w, eps=1e-06):
            return x * jax.lax.rsqrt(jnp.mean(x * x, axis=-1, keepdims=True) + eps) * w

        def silu(x):
            return x * jax.nn.sigmoid(x)

        def causal_depthwise_conv(x, w, b):
            B, L, C = x.shape
            K = w.shape[1]
            xp = jnp.pad(x, ((0, 0), (K - 1, 0), (0, 0)))
            out = b
            for k in range(K):
                out = out + w[:, k] * xp[:, k:k + L, :]
            return out

        def mamba2(h, W_in, conv_w, conv_b, dt_bias, A_log, D, norm_gate_w, W_out):
            B, L, _ = h.shape
            zxbcdt = h @ W_in
            z = zxbcdt[..., :D_INNER]
            xBC = zxbcdt[..., D_INNER:D_INNER + CONV_DIM]
            dt = jax.nn.softplus(zxbcdt[..., D_INNER + CONV_DIM:] + dt_bias)
            xBC = silu(causal_depthwise_conv(xBC, conv_w, conv_b))
            x = xBC[..., :D_INNER].reshape(B, L, NHEADS, HEADDIM)
            Bmat = xBC[..., D_INNER:D_INNER + D_STATE]
            Cmat = xBC[..., D_INNER + D_STATE:]
            A = -jnp.exp(A_log)
            dA = jnp.exp(dt * A)
            dBx = jnp.einsum('blhp,bln,blh->blhpn', x, Bmat, dt)

            def step(state, inp):
                dA_t, dBx_t = inp
                state = state * dA_t[:, :, None, None] + dBx_t
                return (state, state)
            s0 = jnp.zeros((B, NHEADS, HEADDIM, D_STATE), dtype=h.dtype)
            _, states = jax.lax.scan(step, s0, (jnp.moveaxis(dA, 1, 0), jnp.moveaxis(dBx, 1, 0)))
            y = jnp.einsum('lbhpn,bln->blhp', states, Cmat)
            y = y + D[None, None, :, None] * x
            y = y.reshape(B, L, D_INNER)
            y = rmsnorm(y * silu(z), norm_gate_w, eps=1e-05)
            return y @ W_out
        key = jax.random.key(seed)
        ks = jax.random.split(key, 12)
        f = jnp.float32
        d = {}
        d['x'] = jax.random.normal(ks[0], (2, 256, D_MODEL), dtype=f)
        d['norm1_w'] = jnp.ones((D_MODEL,), f)
        d['W_in'] = jax.random.normal(ks[1], (D_MODEL, D_IN_PROJ), f) * D_MODEL ** (-0.5)
        d['conv_w'] = jax.random.normal(ks[2], (CONV_DIM, D_CONV), f) * 0.2
        d['conv_b'] = jnp.zeros((CONV_DIM,), f)
        d['dt_bias'] = jnp.log(jnp.expm1(jax.random.uniform(ks[3], (NHEADS,), f, 0.001, 0.1)))
        d['A_log'] = jnp.log(jax.random.uniform(ks[4], (NHEADS,), f, 1.0, 16.0))
        d['D'] = jnp.ones((NHEADS,), f)
        d['norm_gate_w'] = jnp.ones((D_INNER,), f)
        d['W_out'] = jax.random.normal(ks[5], (D_INNER, D_MODEL), f) * D_INNER ** (-0.5)
        d['norm2_w'] = jnp.ones((D_MODEL,), f)
        d['mlp_w1'] = jax.random.normal(ks[6], (D_MODEL, D_MODEL * MLP_RATIO), f) * D_MODEL ** (-0.5)
        d['mlp_b1'] = jnp.zeros((D_MODEL * MLP_RATIO,), f)
        d['mlp_w2'] = jax.random.normal(ks[7], (D_MODEL * MLP_RATIO, D_MODEL), f) * (D_MODEL * MLP_RATIO) ** (-0.5)
        d['mlp_b2'] = jnp.zeros((D_MODEL,), f)
        return d
    _L0_attn_all = _L0_attn_setup()
    _L0_attn_in = {k: v for k, v in _L0_attn_all.items() if k in ('norm1_w', 'W_in', 'conv_w', 'conv_b', 'dt_bias', 'A_log', 'D', 'norm_gate_w', 'W_out', 'norm2_w', 'mlp_w1', 'mlp_b1', 'mlp_w2', 'mlp_b2')}
    del _L0_attn_all

    def _L0_xattn_setup():
        import math
        import jax, jax.numpy as jnp
        import numpy as np
        B, T, L, H = (4, 512, 512, 128)

        def _forward(hidden_states, advisor_states, advisor_ids, pointer_ids, Wqj, Wkj, Wvj, Wqi, Wki, Wvi, Wout, gain, council_weights):
            b, t, h = hidden_states.shape
            l = advisor_states.shape[1]
            inv_sqrt_h = 1.0 / math.sqrt(float(h))
            p = pointer_ids[:, :, None]
            indices = jnp.clip(jnp.concatenate([p, p + 1, p + 2], axis=-1), 0, l - 1)
            win_states = jax.vmap(lambda a, idx: a[idx])(advisor_states, indices)
            win_ids = jax.vmap(lambda a, idx: a[idx])(advisor_ids, indices)
            qj = hidden_states @ Wqj.T
            kj = win_states @ Wkj.T
            vj = win_states @ Wvj.T
            sj = jnp.einsum('bth,btwh->btw', qj, kj) * inv_sqrt_h
            l_rel, l_v1, l_v2 = (sj[:, :, 0], sj[:, :, 1], sj[:, :, 2])
            rel_ids = win_ids[:, :, 0]
            is_and = (rel_ids == 0).astype(sj.dtype)
            is_or = (rel_ids == 1).astype(sj.dtype)
            is_not = (rel_ids == 2).astype(sj.dtype)
            is_implies = (rel_ids == 3).astype(sj.dtype)
            is_xor = (rel_ids == 4).astype(sj.dtype)
            l_new = is_and * (l_v1 + l_v2) + is_or * jnp.maximum(l_v1, l_v2) + is_not * -l_v1 + is_implies * jnp.maximum(-l_v1, l_v2) + is_xor * jnp.abs(l_v1 - l_v2)
            mask_any = jnp.clip(is_and + is_or + is_not + is_implies + is_xor, 0.0, 1.0)
            l_final = mask_any * l_new + (1.0 - mask_any) * l_rel
            sj = jnp.stack([l_final, l_v1, l_v2], axis=-1)
            aj = jax.nn.softmax(sj, axis=-1)
            cj = jnp.einsum('btw,btwh->bth', aj, vj)
            qi = hidden_states @ Wqi.T
            ki = win_states @ Wki.T
            vi = win_states @ Wvi.T
            si = jnp.einsum('bth,btwh->btw', qi, ki) * inv_sqrt_h
            ai = jax.nn.softmax(si, axis=-1)
            ci = jnp.einsum('btw,btwh->bth', ai, vi)
            w = jax.nn.softmax(council_weights, axis=0)
            context = w[0] * cj + w[1] * ci
            return context @ Wout.T * gain
        key = jax.random.key(seed)
        ks = jax.random.split(key, 12)
        inp = {'hidden_states': jax.random.normal(ks[0], (B, T, H), jnp.float32), 'advisor_states': jax.random.normal(ks[1], (B, L, H), jnp.float32), 'advisor_ids': jax.random.randint(ks[2], (B, L), 0, 8, jnp.int32), 'pointer_ids': jax.random.randint(ks[3], (B, T), 0, L - 2, jnp.int32)}
        s = 1.0 / math.sqrt(H)
        names = ['Wqj', 'Wkj', 'Wvj', 'Wqi', 'Wki', 'Wvi', 'Wout']
        for i, n in enumerate(names):
            inp[n] = jax.random.normal(ks[4 + i], (H, H), jnp.float32) * s
        inp['gain'] = jnp.asarray(0.1, jnp.float32)
        inp['council_weights'] = jnp.ones((2,), jnp.float32)
        return inp
    _L0_xattn_all = _L0_xattn_setup()
    _L0_xattn_in = {k: v for k, v in _L0_xattn_all.items() if k in ('Wqj', 'Wkj', 'Wvj', 'Wqi', 'Wki', 'Wvi', 'Wout', 'gain', 'council_weights')}
    del _L0_xattn_all

    def _L0_ffn_setup():
        import jax, jax.numpy as jnp
        import numpy as np
        QB = 127.0
        EPS = 1e-05

        def _ste(x, q):
            return x + jax.lax.stop_gradient(q - x)

        def bitlinear(x, W, b):
            w_scale = jnp.clip(jnp.mean(jnp.abs(W)), EPS, None)
            Wq = _ste(W, jnp.clip(jnp.round(W / w_scale), -1.0, 1.0) * w_scale)
            x_scale = jnp.clip(jnp.max(jnp.abs(x), axis=-1, keepdims=True), EPS, None)
            xq = _ste(x, jnp.clip(jnp.round(x * (QB / x_scale)), -QB - 1.0, QB) * (x_scale / QB))
            return jnp.einsum('bnd,hd->bnh', xq, Wq) + b
        key = jax.random.key(seed)
        k0, k1, k2 = jax.random.split(key, 3)
        B, N, D = (8, 512, 128)
        H = int(D * 4.0)
        x = jax.random.normal(k0, (B, N, D), dtype=jnp.float32)
        W1 = jax.random.normal(k1, (H, D), dtype=jnp.float32) * 0.02
        b1 = jnp.zeros((H,), dtype=jnp.float32)
        W2 = jax.random.normal(k2, (D, H), dtype=jnp.float32) * 0.02
        b2 = jnp.zeros((D,), dtype=jnp.float32)
        return {'x': x, 'W1': W1, 'b1': b1, 'W2': W2, 'b2': b2}
    _L0_ffn_all = _L0_ffn_setup()
    _L0_ffn_in = {k: v for k, v in _L0_ffn_all.items() if k in ('W1', 'b1', 'W2', 'b2')}
    del _L0_ffn_all

    def _L1_attn_setup():
        import jax, jax.numpy as jnp
        import numpy as np
        import math
        D_MODEL = 128
        NUM_HEADS = 16
        HEAD_DIM = D_MODEL // NUM_HEADS
        B, S = (2, 256)

        def _causal_attn(q, k, v):
            scale = 1.0 / math.sqrt(q.shape[-1])
            scores = jnp.einsum('bthd,bshd->bhts', q, k) * scale
            t = q.shape[1]
            mask = jnp.tril(jnp.ones((t, t), dtype=bool))
            scores = jnp.where(mask, scores, -jnp.inf)
            attn = jax.nn.softmax(scores, axis=-1)
            return jnp.einsum('bhts,bshd->bthd', attn, v)
        key = jax.random.key(seed)
        ks = jax.random.split(key, 7)
        sc = 0.02
        return {'x': jax.random.normal(ks[0], (B, S, D_MODEL), dtype=jnp.float32), 'Wqkv_w': jax.random.normal(ks[1], (3 * D_MODEL, D_MODEL), dtype=jnp.float32) * sc, 'Wqkv_b': jnp.zeros((3 * D_MODEL,), dtype=jnp.float32), 'conv_w': jax.random.normal(ks[2], (D_MODEL, D_MODEL, 3), dtype=jnp.float32) * sc, 'conv_b': jnp.zeros((D_MODEL,), dtype=jnp.float32), 'out_w': jax.random.normal(ks[3], (D_MODEL, D_MODEL), dtype=jnp.float32) * sc, 'out_b': jnp.zeros((D_MODEL,), dtype=jnp.float32)}
    _L1_attn_all = _L1_attn_setup()
    _L1_attn_in = {k: v for k, v in _L1_attn_all.items() if k in ('Wqkv_w', 'Wqkv_b', 'conv_w', 'conv_b', 'out_w', 'out_b')}
    del _L1_attn_all

    def _L1_xattn_setup():
        import jax, jax.numpy as jnp
        import numpy as np
        HIDDEN = 128
        NUM_HEADS = 16
        DEPTH = HIDDEN // NUM_HEADS
        B, F, T = (2, 256, 256)
        key = jax.random.key(seed)
        ks = jax.random.split(key, 6)
        scale = 1.0 / np.sqrt(HIDDEN)
        return {'query_input': jax.random.normal(ks[0], (B, F, HIDDEN), dtype=jnp.float32), 'source_input': jax.random.normal(ks[1], (B, T, HIDDEN), dtype=jnp.float32), 'bias': jnp.zeros((B, 1, F, T), dtype=jnp.float32), 'wq': jax.random.normal(ks[2], (HIDDEN, NUM_HEADS, DEPTH), dtype=jnp.float32) * scale, 'wk': jax.random.normal(ks[3], (HIDDEN, NUM_HEADS, DEPTH), dtype=jnp.float32) * scale, 'wv': jax.random.normal(ks[4], (HIDDEN, NUM_HEADS, DEPTH), dtype=jnp.float32) * scale, 'wo': jax.random.normal(ks[5], (NUM_HEADS, DEPTH, HIDDEN), dtype=jnp.float32) * scale}
    _L1_xattn_all = _L1_xattn_setup()
    _L1_xattn_in = {k: v for k, v in _L1_xattn_all.items() if k in ('wq', 'wk', 'wv', 'wo')}
    del _L1_xattn_all

    def _L1_ffn_setup():
        import jax, jax.numpy as jnp
        import numpy as np
        TOP_K = 2
        N_EXPERTS = 8
        key = jax.random.key(seed)
        k_x, k_g, k_w1, k_w2 = jax.random.split(key, 4)
        B, S, d_in, d_hid, d_out, E = (8, 256, 128, 256, 128, N_EXPERTS)
        s_gate = float(np.sqrt(6.0 / (d_in + E)))
        s_w1 = float(np.sqrt(6.0 / (d_in + d_hid)))
        s_w2 = float(np.sqrt(6.0 / (d_hid + d_out)))
        x = jax.random.normal(k_x, (B, S, d_in), dtype=jnp.float32)
        gate_W = jax.random.uniform(k_g, (d_in, E), jnp.float32, -s_gate, s_gate)
        W1 = jax.random.uniform(k_w1, (E, d_in, d_hid), jnp.float32, -s_w1, s_w1)
        b1 = jnp.zeros((E, d_hid), jnp.float32)
        W2 = jax.random.uniform(k_w2, (E, d_hid, d_out), jnp.float32, -s_w2, s_w2)
        b2 = jnp.zeros((E, d_out), jnp.float32)
        return {'x': x, 'gate_W': gate_W, 'W1': W1, 'b1': b1, 'W2': W2, 'b2': b2}
    _L1_ffn_all = _L1_ffn_setup()
    _L1_ffn_in = {k: v for k, v in _L1_ffn_all.items() if k in ('gate_W', 'W1', 'b1', 'W2', 'b2')}
    del _L1_ffn_all
    return {'x': x, 'ctx_1024': ctx_1024, 'itok_BxS_0_7': itok_BxS_0_7, 'itok_BxS_0_4092': itok_BxS_0_4092, 'mask_Bx1xSxS2_ff0': mask_Bx1xSxS2_ff0, 'L0_attn_norm1_w': _L0_attn_in['norm1_w'], 'L0_attn_W_in': _L0_attn_in['W_in'], 'L0_attn_conv_w': _L0_attn_in['conv_w'], 'L0_attn_conv_b': _L0_attn_in['conv_b'], 'L0_attn_dt_bias': _L0_attn_in['dt_bias'], 'L0_attn_A_log': _L0_attn_in['A_log'], 'L0_attn_D': _L0_attn_in['D'], 'L0_attn_norm_gate_w': _L0_attn_in['norm_gate_w'], 'L0_attn_W_out': _L0_attn_in['W_out'], 'L0_attn_norm2_w': _L0_attn_in['norm2_w'], 'L0_attn_mlp_w1': _L0_attn_in['mlp_w1'], 'L0_attn_mlp_b1': _L0_attn_in['mlp_b1'], 'L0_attn_mlp_w2': _L0_attn_in['mlp_w2'], 'L0_attn_mlp_b2': _L0_attn_in['mlp_b2'], 'L0_xattn_Wqj': _L0_xattn_in['Wqj'], 'L0_xattn_Wkj': _L0_xattn_in['Wkj'], 'L0_xattn_Wvj': _L0_xattn_in['Wvj'], 'L0_xattn_Wqi': _L0_xattn_in['Wqi'], 'L0_xattn_Wki': _L0_xattn_in['Wki'], 'L0_xattn_Wvi': _L0_xattn_in['Wvi'], 'L0_xattn_Wout': _L0_xattn_in['Wout'], 'L0_xattn_gain': _L0_xattn_in['gain'], 'L0_xattn_council_weights': _L0_xattn_in['council_weights'], 'L0_ffn_W1': _L0_ffn_in['W1'], 'L0_ffn_b1': _L0_ffn_in['b1'], 'L0_ffn_W2': _L0_ffn_in['W2'], 'L0_ffn_b2': _L0_ffn_in['b2'], 'L1_attn_Wqkv_w': _L1_attn_in['Wqkv_w'], 'L1_attn_Wqkv_b': _L1_attn_in['Wqkv_b'], 'L1_attn_conv_w': _L1_attn_in['conv_w'], 'L1_attn_conv_b': _L1_attn_in['conv_b'], 'L1_attn_out_w': _L1_attn_in['out_w'], 'L1_attn_out_b': _L1_attn_in['out_b'], 'L1_xattn_wq': _L1_xattn_in['wq'], 'L1_xattn_wk': _L1_xattn_in['wk'], 'L1_xattn_wv': _L1_xattn_in['wv'], 'L1_xattn_wo': _L1_xattn_in['wo'], 'L1_ffn_gate_W': _L1_ffn_in['gate_W'], 'L1_ffn_W1': _L1_ffn_in['W1'], 'L1_ffn_b1': _L1_ffn_in['b1'], 'L1_ffn_W2': _L1_ffn_in['W2'], 'L1_ffn_b2': _L1_ffn_in['b2']}

def reference(x, ctx_1024, itok_BxS_0_7, itok_BxS_0_4092, mask_Bx1xSxS2_ff0, L0_attn_norm1_w, L0_attn_W_in, L0_attn_conv_w, L0_attn_conv_b, L0_attn_dt_bias, L0_attn_A_log, L0_attn_D, L0_attn_norm_gate_w, L0_attn_W_out, L0_attn_norm2_w, L0_attn_mlp_w1, L0_attn_mlp_b1, L0_attn_mlp_w2, L0_attn_mlp_b2, L0_xattn_Wqj, L0_xattn_Wkj, L0_xattn_Wvj, L0_xattn_Wqi, L0_xattn_Wki, L0_xattn_Wvi, L0_xattn_Wout, L0_xattn_gain, L0_xattn_council_weights, L0_ffn_W1, L0_ffn_b1, L0_ffn_W2, L0_ffn_b2, L1_attn_Wqkv_w, L1_attn_Wqkv_b, L1_attn_conv_w, L1_attn_conv_b, L1_attn_out_w, L1_attn_out_b, L1_xattn_wq, L1_xattn_wk, L1_xattn_wv, L1_xattn_wo, L1_ffn_gate_W, L1_ffn_W1, L1_ffn_b1, L1_ffn_W2, L1_ffn_b2):
    import jax
    import jax.numpy as jnp

    def _L0_attn_ref(x, norm1_w, W_in, conv_w, conv_b, dt_bias, A_log, D, norm_gate_w, W_out, norm2_w, mlp_w1, mlp_b1, mlp_w2, mlp_b2):
        import jax, jax.numpy as jnp
        import numpy as np
        D_MODEL = 128
        D_STATE = 16
        D_CONV = 3
        EXPAND = 2
        MLP_RATIO = 4
        HEADDIM = 64
        D_INNER = EXPAND * D_MODEL
        NHEADS = D_INNER // HEADDIM
        CONV_DIM = D_INNER + 2 * D_STATE
        D_IN_PROJ = 2 * D_INNER + 2 * D_STATE + NHEADS

        def rmsnorm(x, w, eps=1e-06):
            return x * jax.lax.rsqrt(jnp.mean(x * x, axis=-1, keepdims=True) + eps) * w

        def silu(x):
            return x * jax.nn.sigmoid(x)

        def causal_depthwise_conv(x, w, b):
            B, L, C = x.shape
            K = w.shape[1]
            xp = jnp.pad(x, ((0, 0), (K - 1, 0), (0, 0)))
            out = b
            for k in range(K):
                out = out + w[:, k] * xp[:, k:k + L, :]
            return out

        def mamba2(h, W_in, conv_w, conv_b, dt_bias, A_log, D, norm_gate_w, W_out):
            B, L, _ = h.shape
            zxbcdt = h @ W_in
            z = zxbcdt[..., :D_INNER]
            xBC = zxbcdt[..., D_INNER:D_INNER + CONV_DIM]
            dt = jax.nn.softplus(zxbcdt[..., D_INNER + CONV_DIM:] + dt_bias)
            xBC = silu(causal_depthwise_conv(xBC, conv_w, conv_b))
            x = xBC[..., :D_INNER].reshape(B, L, NHEADS, HEADDIM)
            Bmat = xBC[..., D_INNER:D_INNER + D_STATE]
            Cmat = xBC[..., D_INNER + D_STATE:]
            A = -jnp.exp(A_log)
            dA = jnp.exp(dt * A)
            dBx = jnp.einsum('blhp,bln,blh->blhpn', x, Bmat, dt)

            def step(state, inp):
                dA_t, dBx_t = inp
                state = state * dA_t[:, :, None, None] + dBx_t
                return (state, state)
            s0 = jnp.zeros((B, NHEADS, HEADDIM, D_STATE), dtype=h.dtype)
            _, states = jax.lax.scan(step, s0, (jnp.moveaxis(dA, 1, 0), jnp.moveaxis(dBx, 1, 0)))
            y = jnp.einsum('lbhpn,bln->blhp', states, Cmat)
            y = y + D[None, None, :, None] * x
            y = y.reshape(B, L, D_INNER)
            y = rmsnorm(y * silu(z), norm_gate_w, eps=1e-05)
            return y @ W_out
        h = rmsnorm(x, norm1_w)
        h = mamba2(h, W_in, conv_w, conv_b, dt_bias, A_log, D, norm_gate_w, W_out)
        x = x + h
        h = rmsnorm(x, norm2_w)
        h = silu(h @ mlp_w1 + mlp_b1) @ mlp_w2 + mlp_b2
        return x + h

    def _L0_xattn_ref(hidden_states, advisor_states, advisor_ids, pointer_ids, Wqj, Wkj, Wvj, Wqi, Wki, Wvi, Wout, gain, council_weights):
        import math
        import jax, jax.numpy as jnp
        import numpy as np
        B, T, L, H = (4, 512, 512, 128)

        def _forward(hidden_states, advisor_states, advisor_ids, pointer_ids, Wqj, Wkj, Wvj, Wqi, Wki, Wvi, Wout, gain, council_weights):
            b, t, h = hidden_states.shape
            l = advisor_states.shape[1]
            inv_sqrt_h = 1.0 / math.sqrt(float(h))
            p = pointer_ids[:, :, None]
            indices = jnp.clip(jnp.concatenate([p, p + 1, p + 2], axis=-1), 0, l - 1)
            win_states = jax.vmap(lambda a, idx: a[idx])(advisor_states, indices)
            win_ids = jax.vmap(lambda a, idx: a[idx])(advisor_ids, indices)
            qj = hidden_states @ Wqj.T
            kj = win_states @ Wkj.T
            vj = win_states @ Wvj.T
            sj = jnp.einsum('bth,btwh->btw', qj, kj) * inv_sqrt_h
            l_rel, l_v1, l_v2 = (sj[:, :, 0], sj[:, :, 1], sj[:, :, 2])
            rel_ids = win_ids[:, :, 0]
            is_and = (rel_ids == 0).astype(sj.dtype)
            is_or = (rel_ids == 1).astype(sj.dtype)
            is_not = (rel_ids == 2).astype(sj.dtype)
            is_implies = (rel_ids == 3).astype(sj.dtype)
            is_xor = (rel_ids == 4).astype(sj.dtype)
            l_new = is_and * (l_v1 + l_v2) + is_or * jnp.maximum(l_v1, l_v2) + is_not * -l_v1 + is_implies * jnp.maximum(-l_v1, l_v2) + is_xor * jnp.abs(l_v1 - l_v2)
            mask_any = jnp.clip(is_and + is_or + is_not + is_implies + is_xor, 0.0, 1.0)
            l_final = mask_any * l_new + (1.0 - mask_any) * l_rel
            sj = jnp.stack([l_final, l_v1, l_v2], axis=-1)
            aj = jax.nn.softmax(sj, axis=-1)
            cj = jnp.einsum('btw,btwh->bth', aj, vj)
            qi = hidden_states @ Wqi.T
            ki = win_states @ Wki.T
            vi = win_states @ Wvi.T
            si = jnp.einsum('bth,btwh->btw', qi, ki) * inv_sqrt_h
            ai = jax.nn.softmax(si, axis=-1)
            ci = jnp.einsum('btw,btwh->bth', ai, vi)
            w = jax.nn.softmax(council_weights, axis=0)
            context = w[0] * cj + w[1] * ci
            return context @ Wout.T * gain
        return _forward(hidden_states, advisor_states, advisor_ids, pointer_ids, Wqj, Wkj, Wvj, Wqi, Wki, Wvi, Wout, gain, council_weights)

    def _L0_ffn_ref(x, W1, b1, W2, b2):
        import jax, jax.numpy as jnp
        import numpy as np
        QB = 127.0
        EPS = 1e-05

        def _ste(x, q):
            return x + jax.lax.stop_gradient(q - x)

        def bitlinear(x, W, b):
            w_scale = jnp.clip(jnp.mean(jnp.abs(W)), EPS, None)
            Wq = _ste(W, jnp.clip(jnp.round(W / w_scale), -1.0, 1.0) * w_scale)
            x_scale = jnp.clip(jnp.max(jnp.abs(x), axis=-1, keepdims=True), EPS, None)
            xq = _ste(x, jnp.clip(jnp.round(x * (QB / x_scale)), -QB - 1.0, QB) * (x_scale / QB))
            return jnp.einsum('bnd,hd->bnh', xq, Wq) + b
        h = bitlinear(x, W1, b1)
        h = jax.nn.gelu(h, approximate=False)
        return bitlinear(h, W2, b2)

    def _L1_attn_ref(x, Wqkv_w, Wqkv_b, conv_w, conv_b, out_w, out_b):
        import jax, jax.numpy as jnp
        import numpy as np
        import math
        D_MODEL = 128
        NUM_HEADS = 16
        HEAD_DIM = D_MODEL // NUM_HEADS
        B, S = (2, 256)

        def _causal_attn(q, k, v):
            scale = 1.0 / math.sqrt(q.shape[-1])
            scores = jnp.einsum('bthd,bshd->bhts', q, k) * scale
            t = q.shape[1]
            mask = jnp.tril(jnp.ones((t, t), dtype=bool))
            scores = jnp.where(mask, scores, -jnp.inf)
            attn = jax.nn.softmax(scores, axis=-1)
            return jnp.einsum('bhts,bshd->bthd', attn, v)
        b, s, d = x.shape
        qkv = x @ Wqkv_w.T + Wqkv_b
        qkv = qkv.reshape(b, s, 3, NUM_HEADS, HEAD_DIM)
        q, k, v = (qkv[:, :, 0], qkv[:, :, 1], qkv[:, :, 2])
        ctx = _causal_attn(q, k, v)
        ctx_c = ctx.reshape(b, s, d).transpose(0, 2, 1)
        conv_out = jax.lax.conv_general_dilated(ctx_c, conv_w, window_strides=(1,), padding=[(1, 1)], dimension_numbers=('NCH', 'OIH', 'NCH')) + conv_b[None, :, None]
        q2 = conv_out.transpose(0, 2, 1).reshape(b, s, NUM_HEADS, HEAD_DIM)
        ctx2 = _causal_attn(q2, k, v)
        out = ctx2.reshape(b, s, d) @ out_w.T + out_b
        return out

    def _L1_xattn_ref(query_input, source_input, bias, wq, wk, wv, wo):
        import jax, jax.numpy as jnp
        import numpy as np
        HIDDEN = 128
        NUM_HEADS = 16
        DEPTH = HIDDEN // NUM_HEADS
        B, F, T = (2, 256, 256)
        q = jnp.einsum('bfh,hnd->bfnd', query_input, wq)
        k = jnp.einsum('bth,hnd->btnd', source_input, wk)
        v = jnp.einsum('bth,hnd->btnd', source_input, wv)
        q = q * DEPTH ** (-0.5)
        logits = jnp.einsum('btnd,bfnd->bnft', k, q) + bias
        weights = jax.nn.softmax(logits, axis=-1)
        attn = jnp.einsum('bnft,btnd->bfnd', weights, v)
        return jnp.einsum('bfnd,ndh->bfh', attn, wo)

    def _L1_ffn_ref(x, gate_W, W1, b1, W2, b2):
        import jax, jax.numpy as jnp
        import numpy as np
        TOP_K = 2
        N_EXPERTS = 8
        E = W1.shape[0]
        d_in = x.shape[-1]
        d_out = W2.shape[-1]
        x_flat = x.reshape(-1, d_in)
        logits = x_flat @ gate_W
        gates = jax.nn.softmax(logits, axis=-1)
        tk_g, tk_i = jax.lax.top_k(gates, TOP_K)
        tk_g = tk_g / (jnp.sum(tk_g, axis=-1, keepdims=True) + 1e-08)
        cw = jnp.sum(jax.nn.one_hot(tk_i, E, dtype=x.dtype) * tk_g[..., None], axis=1)
        out = x_flat
        for e in range(E):
            h = jax.nn.relu(x_flat @ W1[e] + b1[e])
            out = out + cw[:, e:e + 1] * (h @ W2[e] + b2[e])
        return out.reshape(x.shape[:-1] + (d_out,))
    x = x + _L0_attn_ref(_layernorm(x, axis=-1), L0_attn_norm1_w, L0_attn_W_in, L0_attn_conv_w, L0_attn_conv_b, L0_attn_dt_bias, L0_attn_A_log, L0_attn_D, L0_attn_norm_gate_w, L0_attn_W_out, L0_attn_norm2_w, L0_attn_mlp_w1, L0_attn_mlp_b1, L0_attn_mlp_w2, L0_attn_mlp_b2)
    x = x + _L0_xattn_ref(_layernorm(x, axis=-1), ctx_1024, itok_BxS_0_7, itok_BxS_0_4092, L0_xattn_Wqj, L0_xattn_Wkj, L0_xattn_Wvj, L0_xattn_Wqi, L0_xattn_Wki, L0_xattn_Wvi, L0_xattn_Wout, L0_xattn_gain, L0_xattn_council_weights)
    x = x + _L0_ffn_ref(_layernorm(x, axis=-1), L0_ffn_W1, L0_ffn_b1, L0_ffn_W2, L0_ffn_b2)
    x = x + _L1_attn_ref(_layernorm(x, axis=-1), L1_attn_Wqkv_w, L1_attn_Wqkv_b, L1_attn_conv_w, L1_attn_conv_b, L1_attn_out_w, L1_attn_out_b)
    x = x + _L1_xattn_ref(_layernorm(x, axis=-1), ctx_1024, mask_Bx1xSxS2_ff0, L1_xattn_wq, L1_xattn_wk, L1_xattn_wv, L1_xattn_wo)
    x = x + _L1_ffn_ref(_layernorm(x, axis=-1), L1_ffn_gate_W, L1_ffn_W1, L1_ffn_b1, L1_ffn_W2, L1_ffn_b2)
    return x

_drawn_inputs = setup_inputs


def setup_inputs(seed=0):
    import zlib

    import numpy as np

    out = dict(_drawn_inputs(seed))
    spreads = {'L0_attn_norm1_w': (1.0, 0.2),
     'L0_attn_conv_b': (0.0, 0.1),
     'L0_attn_D': (1.0, 0.2),
     'L0_attn_norm_gate_w': (1.0, 0.2),
     'L0_attn_norm2_w': (1.0, 0.2),
     'L0_attn_mlp_b1': (0.0, 0.1),
     'L0_attn_mlp_b2': (0.0, 0.1),
     'L0_xattn_council_weights': (1.0, 0.6),
     'L0_ffn_b1': (0.0, 0.701),
     'L0_ffn_b2': (0.0, 0.1),
     'L1_attn_Wqkv_b': (0.0, 0.543),
     'L1_attn_conv_b': (0.0, 0.8),
     'L1_attn_out_b': (0.0, 0.1),
     'L1_ffn_b1': (0.0, 0.439),
     'L1_ffn_b2': (0.0, 0.353)}
    factors = {'L0_attn_dt_bias': 5.681,
     'L0_attn_A_log': 8.0,
     'L0_xattn_Wqj': 8.0,
     'L0_xattn_Wkj': 8.0,
     'L0_xattn_Wqi': 8.0,
     'L0_xattn_Wki': 8.0,
     'L0_ffn_W1': 4.15,
     'L0_ffn_W2': 3.521,
     'L1_attn_Wqkv_w': 6.117,
     'L1_attn_conv_w': 8.0,
     'L1_attn_out_w': 3.564}
    for name, (base, spread) in spreads.items():
        noise = np.random.default_rng([zlib.crc32(name.encode()), seed]).standard_normal(out[name].shape)
        drawn = base * np.exp(spread * noise) if base else spread * noise
        out[name] = jnp.asarray(drawn.astype(out[name].dtype))
    for name, factor in factors.items():
        out[name] = (out[name] * factor).astype(out[name].dtype)
    return out
```

```python
import concourse.bass as bass
from concourse import mybir
from contextlib import ExitStack
import numpy as np

fp32 = mybir.dt.float32
fp16 = mybir.dt.float16
bf16 = mybir.dt.bfloat16
i32 = mybir.dt.int32
u32 = mybir.dt.uint32
ALU = mybir.AluOpType
ACT = mybir.ActivationFunctionType
AX = mybir.AxisListType

P = 128
D = 128
S = 64
BATCH = 128
T = 4
NB = 2 * T
N = T * P
GROUPS = BATCH // NB
H = 16
HD = D // H
E = 8
F = 256
DI = 256
NH = 4
NS = 16
FF = 512
MAGIC = 12582912.0
BIG = -1.0e30
VW = 2 * (HD + 1)


def shape_constants():
    p = np.arange(P)
    b, s = p // S, p % S
    t = np.arange(S)
    same = b[:, None] == b[None, :]
    return {
        "c_ident": np.eye(P, dtype=np.float32),
        "c_after": (same & (s[:, None] > s[None, :])).astype(np.float32),
        "c_upto": (s[:, None] <= t[None, :]).astype(np.float32),
        "c_seen": 0.25 * (s[:, None] <= t[None, :]).astype(np.float32),
        "c_causal": np.where(t[None, :] <= s[:, None], 0.0, BIG).astype(np.float32),
        "c_coef": np.broadcast_to((1.0 / np.arange(17, 0, -2)).astype(np.float32), (P, 9)).copy(),
        "c_iota": np.broadcast_to(t.astype(np.float32), (P, S)).copy(),
    }


def program(nc, a, out, groups=GROUPS, upto=99):
    ctx = ExitStack()
    with ctx:
        def sb(name, shape, dt=fp32):
            return ctx.enter_context(nc.sbuf_tensor(name, shape, dt))

        def sem(name):
            return ctx.enter_context(nc.semaphore(name))

        PA = ctx.enter_context(nc.psum_tensor("PA", [P, 4, 512], fp32))
        PB = ctx.enter_context(nc.psum_tensor("PB", [P, 4, 512], fp32))

        ident = sb("ident", [P, P])
        ident16 = sb("ident16", [P, P], fp16)
        identb = sb("identb", [P, P], bf16)
        after = sb("after", [P, P])
        uptot = sb("uptot", [P, S])
        seen = sb("seen", [P, S])
        causal = sb("causal", [P, S])
        causalb = sb("causalb", [P, S], bf16)
        iota = sb("iota", [P, S])
        coef = sb("coef", [P, 9])
        mhalf = sb("mhalf", [P, 2 * T])
        ones = sb("ones", [P, P])

        w_in = sb("w_in", [P, 548])
        w_bc = sb("w_bc", [P, 48])
        norm1 = sb("norm1", [P, 1])
        cw_x = sb("cw_x", [P, 2, 3])
        cb_x = sb("cb_x", [P, 2])
        cw_bc = sb("cw_bc", [48, 3])
        cb_bc = sb("cb_bc", [48, 1])
        dtb = sb("dtb", [P, NH])
        alog = sb("alog", [P, NH])
        negA = sb("negA", [P, NH])
        dskip = sb("dskip", [P, 2])
        ngate = sb("ngate", [P, 2])
        w_out = sb("w_out", [P, 2, D])
        norm2 = sb("norm2", [P, 1])
        w1m = sb("w1m", [P, FF])
        b1m = sb("b1m", [P, 4])
        w2m = sb("w2m", [P, 4, D])
        b2m = sb("b2m", [P, D])

        wqk = sb("wqk", [P, 2, P])
        wvo = sb("wvo", [P, 2, P])
        woutT = sb("woutT", [P, P])
        gain = sb("gain", [P, 1])
        council = sb("council", [P, 2])
        csum = sb("csum", [P, 4])

        f1T = sb("f1T", [P, FF], bf16)
        f2T = sb("f2T", [P, 4, D], bf16)
        fb1 = sb("fb1", [P, FF])
        fb2 = sb("fb2", [P, D])
        fabs = sb("fabs", [P, 2])
        fscale = sb("fscale", [P, 2])
        finv = sb("finv", [P, 2])
        fs127 = sb("fs127", [P, 2])

        wqkT = sb("wqkT", [P, 2 * D])
        qkb = sb("qkb", [P, 2 * D])
        vb = sb("vb", [P, D])
        wvT = sb("wvT", [P, D])
        wv_par = sb("wv_par", [P, 2, S])
        vb_par = sb("vb_par", [P, S])
        cvT = sb("cvT", [P, 3, D])
        cvb = sb("cvb", [P, D])
        owT = sb("owT", [P, D])
        ob = sb("ob", [P, D])
        ewq = sb("ewq", [P, D])
        ewk = sb("ewk", [P, D])
        ewv = sb("ewv", [P, D])
        ewv_par = sb("ewv_par", [P, 2, S])
        ewo = sb("ewo", [P, D])

        gate = sb("gate", [P, E])
        mw1 = sb("mw1", [P, E, F])
        mb1 = sb("mb1", [P, 2 * E])
        mw2 = sb("mw2", [P, 2 * E, D])
        mb2 = sb("mb2", [E, D])

        room = {k: sb("room_" + k, [P, 2048]) for k in ("seg", "mix", "gate", "chan", "prob", "turn", "hidden")}

        def part(k, at, shape, dt=fp32):
            count = int(np.prod(shape))
            words = count // (1 if dt == fp32 else 2)
            assert at + words <= 2048
            ap = room[k][:, at:at + words]
            if dt != fp32:
                ap = ap.bitcast(dt)
            if len(shape) == 1:
                return ap
            names = "abcd"[:len(shape)]
            return ap.rearrange(f"p ({' '.join(names)}) -> p {' '.join(names)}", **dict(zip(names[1:], shape[1:])))

        f1 = part("hidden", 0, [4, D])
        f2 = part("hidden", 512, [FF])
        f1q = part("hidden", 1024, [4, D], bf16)
        f2q = part("hidden", 1280, [FF], bf16)
        xw = part("prob", 0, [7, P])
        aw = part("prob", 896, [3, D])
        cvw = part("prob", 1280, [3 * D])
        oww = part("prob", 1664, [D])
        owp = part("prob", 1792, [D])
        cvp = part("turn", 0, [3, D])
        G = part("seg", 0, [T, NH, S])
        dec = part("seg", 1024, [T, NH, S])
        hb = part("seg", 0, [T, FF])
        xdt = part("mix", 0, [T, NH, S])
        M = part("mix", 1024, [T, NH, S])
        g32 = part("mix", 0, [T, FF])
        zs = part("gate", 0, [2, N])
        gsq = part("gate", 1024, [2, N])
        hs = part("gate", 0, [4, N])
        y2 = part("chan", 0, [2, N])
        xc = part("chan", 1024, [2, N])
        gq = part("chan", 0, [T, FF], bf16)
        gqT = part("chan", 1024, [T, 4, P], bf16)
        Pr = part("prob", 0, [4, 2 * 4, S])
        PT = part("turn", 0, [4, 2 * 2, P])
        hid = part("hidden", 0, [2, 2, N])

        xin = sb("xin", [P, T, D])
        ctx2 = sb("ctx2", [P, T, 2, D])
        idsb = sb("idsb", [P, T, S], i32)
        ptr = sb("ptr", [P, T], i32)
        mark = sb("mark", [1, 1])
        st = sb("st", [P, T, 6])
        mv = sb("mv", [P, T, 2])
        var = sb("var", [P, T, 2])
        msq = sb("msq", [P, T])
        rs = sb("rs", [P, T, 2])
        h = sb("h", [P, T, D])
        u = sb("u", [P, T, D])
        hT = sb("hT", [P, N])
        bcc = sb("bcc", [48, N])
        bT = sb("bT", [NS, N])
        cT = sb("cT", [NS, N])
        dv = sb("dv", [P, T * NH])
        dn = sb("dn", [P, T * NH])
        du = sb("du", [P, T * NH])
        dw = sb("dw", [P, T * NH])
        dr = sb("dr", [P, T * NH])
        dz = sb("dz", [P, T * NH])
        dq = sb("dq", [P, T * NH])
        dp = sb("dp", [P, T * NH])
        dtt = sb("dtt", [P, T, NH])
        aa = sb("aa", [P, T, NH])
        cbm = sb("cbm", [P, T, S])
        rg = sb("rg", [P, T])
        rgi = sb("rgi", [P, T])
        x1 = sb("x1", [P, T, D])
        xb = sb("xb", [P, T, D])
        xA = sb("xA", [P, T, D])
        ctxT = sb("ctxT", [P, T, P])
        pf = sb("pf", [P, T, 3])
        O = sb("O", [P, T, 3, S])
        qx = sb("qx", [P, 2, N])
        prod = sb("prod", [P, 2, T, 3, S])
        sc = sb("sc", [P, 2, T, 3])
        rid = sb("rid", [P, T])
        rprod = sb("rprod", [P, T, S])
        R = sb("R", [P, T, 6])
        V6 = sb("V6", [P, T, 6])
        smx = sb("smx", [P, 2 * T])
        ssm = sb("ssm", [P, 2 * T])
        Pm = sb("Pm", [P, T, 2, S])
        cT2 = qx
        PmT = sb("PmT", [P, T, P])
        amx = sb("amx", [P, T])
        ainv = sb("ainv", [P, T])
        asc = sb("asc", [P, T])
        t32 = sb("t32", [P, T, D])
        xq = sb("xq", [P, T, D], bf16)
        xqT = sb("xqT", [P, N], bf16)

        xB = sb("xB", [P, T, D])
        xo = sb("xo", [P, T, D])
        ctxTB = sb("ctxTB", [P, T, P])
        maskE = sb("maskE", [P, T, S])
        bst = sb("bst", [P, T, 6])
        bmv = sb("bmv", [P, T, 2])
        bvar = sb("bvar", [P, T])
        brs = sb("brs", [P, T])
        bh = sb("bh", [P, T, D])
        bhT = sb("bhT", [P, N])
        qk32 = sb("qk32", [P, T, 2, D])
        aug = sb("aug", [P, 2, T, H, 32], fp16)
        augT = sb("augT", [P, T, 2, 4, P], fp16)
        Vx = sb("Vx", [P, NB, E, VW])
        mx = sb("mx", [P, 4, 2 * 4])
        rc = sb("rc", [P, 4, 2 * 4])
        cx = sb("cx", [P, T, D])
        cxT = sb("cxT", [P, 3, NB, S])
        lg = sb("lg", [P, T, E])
        m8 = sb("m8", [P, T, E])
        ix8 = sb("ix8", [P, T, E], u32)
        ixf = sb("ixf", [P, T, 2])
        e8 = sb("e8", [P, T, E])
        s8 = sb("s8", [P, T])
        r8 = sb("r8", [P, T])
        g2 = sb("g2", [P, T, 2])
        d2 = sb("d2", [P, T])
        cw2 = sb("cw2", [P, T, 2])
        oh = sb("oh", [P, T, 2, E])
        cwt = sb("cwt", [P, T, E])
        cwT = sb("cwT", [E, N])
        acc = sb("acc", [P, T, D])

        s = {}

        def sig(name):
            if name not in s:
                s[name] = sem(name)
            return s[name]

        def wait_apart(engine, name, value):
            engine.wait_ge(sig("preset"), 10)
            engine.wait_ge(sig(name), value)

        block = ctx.enter_context(nc.Block())

        x_v = a["x"].rearrange("(g t b) s d -> g (b s) t d", t=T, b=2)
        out_v = out.rearrange("(g t b) s d -> g (b s) t d", t=T, b=2)
        c_v = a["ctx_1024"].rearrange("(g t b) s d -> g s (t b) d", t=T, b=2)
        m_v = a["mask_Bx1xSxS2_ff0"].rearrange("(g t b) o s l -> g (b s) t (o l)", t=T, b=2)
        p_v = a["itok_BxS_0_4092"].rearrange("(g t b) s -> g (b s) t", t=T, b=2)
        i_v = a["itok_BxS_0_7"].rearrange("(g t b) s -> g b t s", t=T, b=2)

        def row(ap, n=P):
            return ap.rearrange("(o k) -> o k", o=1).broadcast_to([n, ap.shape[0]])

        LOADS = []
        PADDED = []

        def load(dst, src, to=LOADS):
            to.append((dst, src))

        W = lambda k: a[k]
        load(ident[:, :], W("c_ident"))
        load(after[:, :], W("c_after"))
        load(uptot[:, :], W("c_upto"))
        load(seen[:, :], W("c_seen"))
        load(causal[:, :], W("c_causal"))
        load(iota[:, :], W("c_iota"))
        load(coef[:, :], W("c_coef"))
        load(w_in[:, :], W("L0_attn_W_in"))
        load(norm1[:, :], W("L0_attn_norm1_w").rearrange("(k o) -> k o", o=1))
        load(cw_x[:, :, :], W("L0_attn_conv_w")[0:DI, :].rearrange("(c k) w -> k c w", c=2))
        load(cb_x[:, :], W("L0_attn_conv_b")[0:DI].rearrange("(c k) -> k c", c=2))
        load(cw_bc[0:NS, :], W("L0_attn_conv_w")[DI:DI + NS, :], PADDED)
        load(cw_bc[32:32 + NS, :], W("L0_attn_conv_w")[DI + NS:DI + 2 * NS, :], PADDED)
        load(cb_bc[0:NS, :], W("L0_attn_conv_b")[DI:DI + NS].rearrange("(k o) -> k o", o=1), PADDED)
        load(cb_bc[32:32 + NS, :], W("L0_attn_conv_b")[DI + NS:DI + 2 * NS].rearrange("(k o) -> k o", o=1), PADDED)
        load(dtb[:, :], row(W("L0_attn_dt_bias")))
        load(alog[:, :], row(W("L0_attn_A_log")))
        for hh in range(NH):
            load(dskip[S * (hh % 2):S * (hh % 2) + S, hh // 2:hh // 2 + 1], row(W("L0_attn_D")[hh:hh + 1], S))
        load(ngate[:, :], W("L0_attn_norm_gate_w").rearrange("(c k) -> k c", c=2))
        load(w_out[:, :, :], W("L0_attn_W_out").rearrange("(c k) d -> k c d", c=2))
        load(norm2[:, :], W("L0_attn_norm2_w").rearrange("(k o) -> k o", o=1))
        load(w1m[:, :], W("L0_attn_mlp_w1"))
        load(b1m[:, :], W("L0_attn_mlp_b1").rearrange("(c k) -> k c", c=4))
        load(w2m[:, :, :], W("L0_attn_mlp_w2").rearrange("(c k) d -> k c d", c=4))
        load(b2m[:, :], row(W("L0_attn_mlp_b2")))
        for n_, k in enumerate(("Wqj", "Wkj", "Wvj", "Wqi", "Wki", "Wvi", "Wout")):
            load(xw[:, n_, :], W("L0_xattn_" + k))
        load(gain[:, :], W("L0_xattn_gain").broadcast_to([P, 1]))
        load(council[:, :], row(W("L0_xattn_council_weights")))
        load(f1[:, :, :], W("L0_ffn_W1").rearrange("(c k) d -> k c d", c=4))
        load(f2[:, :], W("L0_ffn_W2"))
        load(fb1[:, :], row(W("L0_ffn_b1")))
        load(fb2[:, :], row(W("L0_ffn_b2")))
        load(aw[:, :, :], W("L1_attn_Wqkv_w").rearrange("(c k) d -> k c d", c=3))
        load(qkb[:, :], row(W("L1_attn_Wqkv_b")[0:2 * D]))
        load(vb[:, :], row(W("L1_attn_Wqkv_b")[2 * D:3 * D]))
        load(cvw[:, :], W("L1_attn_conv_w").rearrange("o i k -> o (i k)"))
        load(cvb[:, :], row(W("L1_attn_conv_b")))
        load(oww[:, :], W("L1_attn_out_w"))
        load(ob[:, :], row(W("L1_attn_out_b")))
        load(ewq[:, :], W("L1_xattn_wq").rearrange("i n d -> i (n d)"))
        load(ewk[:, :], W("L1_xattn_wk").rearrange("i n d -> i (n d)"))
        load(ewv[:, :], W("L1_xattn_wv").rearrange("i n d -> i (n d)"))
        wo_v = W("L1_xattn_wo").rearrange("(cc h2 j) d m -> j cc h2 d m", cc=2, h2=2)
        for j in range(4):
            for cc in range(2):
                for h2 in range(2):
                    at = ((j * 2 + cc) * 2 + h2) * HD
                    load(ewo[at:at + HD, :], wo_v[j, cc, h2])
        load(gate[:, :], W("L1_ffn_gate_W"))
        load(mw1[:, :, :], W("L1_ffn_W1").rearrange("e k f -> k e f"))
        load(mb1[:, :], W("L1_ffn_b1").rearrange("e (c k) -> k (e c)", c=2))
        load(mw2[:, :, :], W("L1_ffn_W2").rearrange("e (c k) d -> k (e c) d", c=2))
        load(mb2[:, :], W("L1_ffn_b2"))
        NLOADS = len(LOADS)

        @block.sync
        def _(sp):
            for dst, src in LOADS[::2]:
                sp.dma_start(dst, src, allow_slow_non_contiguous=True).then_inc(sig("weights_loaded"), 16)
            with sp.Fori(0, groups) as i:
                sp.wait_ge(sig("u_ready"), i * T)
                sp.wait_ge(sig("xb_ready"), i)
                sp.dma_start(xin[:, :, :], x_v[i]).then_inc(sig("x_loaded"), 16)
                sp.wait_ge(sig("cx_ps"), i)
                sp.dma_start(ctx2[0:S, :, :, :], c_v[i].rearrange("s (t b) d -> s t b d", b=2)).then_inc(sig("ctx_loaded"), 16)
                sp.dma_start(ctx2[S:P, :, :, :], c_v[i].rearrange("s (t b) d -> s t b d", b=2)).then_inc(sig("ctx_loaded"), 16)
                sp.wait_ge(sig("ids_free"), i)
                for b in range(2):
                    sp.dma_start(idsb[S * b:S * b + S, :, :],
                                 i_v[i, b:b + 1].broadcast_to([S, T, S])).then_inc(sig("ids_loaded"), 16)
                sp.wait_ge(sig("pf"), i * 4)
                sp.dma_start(ptr[:, :], p_v[i], allow_slow_non_contiguous=True).then_inc(sig("ptr_loaded"), 16)
                sp.wait_ge(sig("s_biased"), i * 8)
                sp.dma_start(maskE[:, :, :], m_v[i]).then_inc(sig("mask_loaded"), 16)
                sp.wait_ge(sig("out_ready"), (i + 1) * T)
                sp.dma_start(out_v[i], acc[:, :, :]).then_inc(sig("stored"), 16)
            sp.wait_ge(sig("stored"), 16 * groups)

        @block.gpsimd
        def _(pool):
            pool.memset(cw_bc[:, :], 0.0).then_inc(sig("preset"), 1)
            pool.memset(cb_bc[:, :], 0.0).then_inc(sig("preset"), 1)
            pool.wait_ge(sig("preset"), 2)
            for dst, src in PADDED:
                pool.dma_start(dst, src, allow_slow_non_contiguous=True).then_inc(sig("padded_loaded"), 16)
            pool.memset(mhalf[:, :], -0.5).then_inc(sig("preset"), 1)
            pool.memset(ones[:, :], 1.0).then_inc(sig("preset"), 1)
            pool.memset(w_bc[:, :], 0.0).then_inc(sig("preset"), 1)
            pool.memset(aug[:, :, :, :, :], 0.0).then_inc(sig("preset"), 1)
            pool.memset(cxT[:, :, :, :], 0.0).then_inc(sig("preset"), 1)
            pool.memset(Vx[:, :, :, :], 0.0).then_inc(sig("preset"), 1)
            pool.wait_ge(sig("preset"), 8)
            pool.memset(Vx[0:S, :, :, HD:HD + 1], 1.0).then_inc(sig("preset"), 1)
            pool.memset(Vx[S:P, :, :, VW - 1:VW], 1.0).then_inc(sig("preset"), 1)
            pool.wait_ge(sig("setup_done"), 3)

            def rsqrt(dst, src, wait, value, done):
                pool.wait_ge(sig(wait), value)
                k = dst.shape[1]
                pool.tensor_tensor(dst, src, mhalf[:, 0:k], ALU.pow).then_inc(sig(done), 1)

            with pool.Fori(0, groups) as i:
                rsqrt(rs[:, :, :].rearrange("p t k -> p (t k)"), var[:, :, :].rearrange("p t k -> p (t k)"),
                      "ln_var", i * 5 + 2, "ln_rstd")
                pool.wait_ge(sig("x_loaded"), i * 16 + 16)
                pool.wait_ge(sig("xA_ready"), i)
                pool.tensor_tensor(xb[:, :, :], xin[:, :, :], b2m[:, :].unsqueeze(1).broadcast_to([P, T, D]),
                                   ALU.add).then_inc(sig("xb_ready"), 1)
                pool.wait_ge(sig("dt_z"), i * 2 + 1)
                pool.tensor_tensor(dq[:, :], dz[:, :], dz[:, :], ALU.mult).then_inc(sig("dt_poly"), 1)
                for k in range(9):
                    if k:
                        pool.wait_ge(sig("dt_poly"), i * 18 + 2 * k)
                        pool.tensor_tensor(dp[:, :], dp[:, :], coef[:, k:k + 1].broadcast_to([P, T * NH]),
                                           ALU.add).then_inc(sig("dt_poly"), 1)
                    pool.wait_ge(sig("dt_poly"), i * 18 + 2 * k + 1)
                    if k:
                        pool.tensor_tensor(dp[:, :], dp[:, :], (dz if k == 8 else dq)[:, :], ALU.mult).then_inc(sig("dt_poly"), 1)
                    else:
                        pool.tensor_tensor(dp[:, :], dq[:, :], coef[:, 0:1].broadcast_to([P, T * NH]),
                                           ALU.mult).then_inc(sig("dt_poly"), 1)
                pool.wait_ge(sig("a_ready"), i + 1)
                for t in range(T):
                    pool.tensor_tensor(G[:, t, :, :], aa[:, t, :].unsqueeze(2).broadcast_to([P, NH, S]),
                                       uptot[:, :].unsqueeze(1).broadcast_to([P, NH, S]),
                                       ALU.mult).then_inc(sig("G_ready"), 1)
                rsqrt(rg[:, :], rgi[:, :], "gate_var", i + 1, "gate_rstd")
                rsqrt(rs[:, :, 0], var[:, :, 0], "ln_var", i * 5 + 3, "ln_rstd")
                rsqrt(rs[:, :, 0], var[:, :, 0], "ln_var", i * 5 + 4, "ln_rstd")
                for x_ in range(2):
                    pool.wait_ge(sig("sm"), i * 6 + 6)
                    for t in range(T):
                        pool.tensor_tensor(prod[:, x_, t, :, :], O[:, t, :, :],
                                           sc[:, x_, t, :].unsqueeze(2).broadcast_to([P, 3, S]),
                                           ALU.mult).then_inc(sig("OW_ready"), 1)
                rsqrt(rs[:, :, 0], var[:, :, 0], "ln_var", i * 5 + 5, "ln_rstd")
                pool.wait_ge(sig("x2_ready"), i + 1)
                pool.tensor_tensor(xb[:, :, :], xA[:, :, :], fb2[:, :].unsqueeze(1).broadcast_to([P, T, D]),
                                   ALU.add).then_inc(sig("xb2_ready"), 1)
                for k in range(3):
                    rsqrt(brs[:, :], bvar[:, :], "bln_var", i * 3 + k + 1, "bln_rstd")
                    if k == 0:
                        pool.tensor_tensor(xo[:, :, :], xB[:, :, :], ob[:, :].unsqueeze(1).broadcast_to([P, T, D]),
                                           ALU.add).then_inc(sig("xo_ready"), 1)
                    if k == 2:
                        pool.wait_ge(sig("bh_ready"), (i * 3 + 3) * T)
                        pool.tensor_tensor(xo[:, :, :], xB[:, :, :], bh[:, :, :], ALU.add).then_inc(sig("xh_ready"), 1)

        @block.vector
        def _(v):
            v.wait_ge(sig("weights_loaded"), 16 * NLOADS)
            v.wait_ge(sig("padded_loaded"), 16 * len(PADDED))
            v.wait_ge(sig("preset"), 10)
            c = [0]

            def link(ins):
                c[0] += 1
                ins.then_inc(sig("v_setup"), 1)
                v.wait_ge(sig("v_setup"), c[0])

            def par(o, i_):
                for h2 in range(2):
                    for j in range(4):
                        v.tensor_copy(o(h2).rearrange("p (j cc d) -> p j cc d", j=4, cc=2)[:, j],
                                      i_(h2).rearrange("p (cc h j d) -> p h j cc d", cc=2, h=2, j=4)[:, h2, j])

            v.tensor_copy(ident16[:, :], ident[:, :])
            v.tensor_copy(identb[:, :], ident[:, :])
            v.tensor_copy(causalb[:, :], causal[:, :])
            link(v.tensor_scalar(w_in[:, :], w_in[:, :], norm1[:, :], None, ALU.mult))
            v.tensor_copy(w_bc[:, 0:NS], w_in[:, 2 * DI:2 * DI + NS])
            v.tensor_copy(w_bc[:, 32:32 + NS], w_in[:, 2 * DI + NS:2 * DI + 2 * NS])
            for k in range(2):
                v.tensor_scalar(w_out[:, k, :], w_out[:, k, :], ngate[:, k:k + 1], None, ALU.mult)
            link(v.tensor_scalar(w1m[:, :], w1m[:, :], norm2[:, :], None, ALU.mult))
            link(v.tensor_reduce(fabs[:, 0:1], f1[:, :, :], AX.XY, ALU.add, apply_absolute_value=True))
            v.tensor_reduce(fabs[:, 1:2], f2[:, :], AX.X, ALU.add, apply_absolute_value=True).then_inc(sig("dve_setup"), 1)
            v.tensor_scalar(ewq[:, :], ewq[:, :], HD ** -0.5, None, ALU.mult)
            v.tensor_scalar(qkb[:, 0:D], qkb[:, 0:D], HD ** -0.5, None, ALU.mult)
            v.tensor_scalar(cvb[:, :], cvb[:, :], HD ** -0.5, None, ALU.mult)
            v.tensor_reduce(csum[:, 0:1], council[:, :], AX.X, ALU.max)
            for k in range(3):
                for j in range(4):
                    v.tensor_copy(cvp[:, k, 32 * j:32 * j + 32].rearrange("p (a d) -> p a d", d=HD),
                                  cvw[:, :].rearrange("p (a j d k) -> p k j a d", a=4, j=4, k=3)[:, k, j])
            for j in range(4):
                v.tensor_copy(owp[:, 32 * j:32 * j + 32].rearrange("p (a d) -> p a d", d=HD),
                              oww[:, :].rearrange("p (a j d) -> p j a d", a=4, j=4)[:, j])
            par(lambda h2: ewv_par[:, h2, :], lambda h2: ewv[:, :])
            link(v.tensor_copy(csum[:, 1:2], gain[:, :]))
            link(v.tensor_scalar(council[:, :], council[:, :], csum[:, 0:1], None, ALU.subtract))
            for h2 in range(2):
                for j in range(4):
                    v.tensor_copy(vb_par[S * h2:S * h2 + S, :].rearrange("p (j cc d) -> p j cc d", j=4, cc=2)[:, j],
                                  vb[S * h2:S * h2 + S, :].rearrange("p (cc h j d) -> p h j cc d", cc=2, h=2, j=4)[:, h2, j])
            v.memset(R[:, :, :], 0.0).then_inc(sig("dve_setup"), 1)
            v.wait_ge(sig("pe_setup"), 1)
            link(v.tensor_scalar(fscale[:, :], PA[:, 0, 0:2], 1.0 / (FF * D), 1e-5, ALU.mult, ALU.max))
            link(v.reciprocal(finv[:, :], fscale[:, :]))
            v.tensor_scalar(fs127[:, :], fscale[:, :], 1.0 / 127.0, None, ALU.mult)
            f1f = f1[:, :, :].rearrange("p c d -> p (c d)")
            f1qf = f1q[:, :, :].rearrange("p c d -> p (c d)")
            for wgt, qd, k in ((f1f, f1qf, 0), (f2[:, :], f2q[:, :], 1)):
                link(v.tensor_scalar(wgt, wgt, finv[:, k:k + 1], MAGIC, ALU.mult, ALU.add))
                link(v.tensor_scalar(wgt, wgt, MAGIC, 1.0, ALU.subtract, ALU.min))
                link(v.tensor_scalar(qd, wgt, -1.0, None, ALU.max))
            v.wait_ge(sig("act_setup"), 2)
            link(v.tensor_reduce(csum[:, 2:3], council[:, :], AX.X, ALU.add))
            link(v.reciprocal(csum[:, 3:4], csum[:, 2:3]))
            link(v.tensor_scalar(council[:, :], council[:, :], csum[:, 3:4], csum[:, 1:2], ALU.mult, ALU.mult))
            v.wait_ge(sig("act_setup"), 1)
            link(v.tensor_scalar(negA[:, :], negA[:, :], -1.0, None, ALU.mult))
            v.memset(dz[:, :], 0.0).then_inc(sig("dve_setup"), 1)
            v.wait_ge(sig("pe_setup"), 2)
            v.tensor_copy(woutT[:, :], PA[:, 1, 0:P])
            v.tensor_scalar(wqk[:, :, :], PA[:, 1, 128:384].rearrange("p (a b) -> p a b", a=2), float(D) ** -0.5, None, ALU.mult)
            v.tensor_scalar(wqkT[:, 0:D], PA[:, 2, 0:D], HD ** -0.5, None, ALU.mult)
            v.tensor_copy(wqkT[:, D:2 * D], PA[:, 2, D:2 * D])
            v.tensor_copy(owT[:, :], PA[:, 2, 384:512])
            v.tensor_scalar(cvT[:, :, :], PA[:, 3, 0:384].rearrange("p (a b) -> p a b", a=3), HD ** -0.5, None, ALU.mult)
            link(v.tensor_copy(wvT[:, :], PA[:, 2, 256:384]))
            par(lambda h2: wv_par[:, h2, :], lambda h2: wvT[:, :])
            v.tensor_copy(f1T[:, :], PB[:, 0, 0:256].bitcast(bf16))
            v.tensor_copy(f2T[:, :, :].rearrange("p a b -> p (a b)"), PB[:, 1, 0:256].bitcast(bf16))
            v.tensor_copy(dw[:, :], dz[:, :]).then_inc(sig("dve_setup"), 1)
            v.wait_ge(sig("pe_setup"), 3)
            for x_ in range(2):
                v.tensor_scalar(wvo[:, x_, :], PA[:, 0, x_ * P:x_ * P + P], council[:, x_:x_ + 1], None, ALU.mult)
            v.tensor_copy(dw[:, :], dz[:, :]).then_inc(sig("setup_done"), 3)
            v.wait_ge(sig("setup_done"), 3)

            def stats(src, i_st, i_mv, stat, mean, s_st, s_mv):
                for t in range(T):
                    v.bn_stats(stat[:, t, :], src[:, t, :]).then_inc(sig(s_st), 1)
                v.wait_ge(sig(s_st), i_st + T)
                v.memset(mark[:, :], 0.0)
                for t in range(T):
                    v.bn_aggr(mean[:, t, :], stat[:, t, :]).then_inc(sig(s_mv), 1)
                v.wait_ge(sig(s_mv), i_mv + T)

            with v.Fori(0, groups) as i:
                v.wait_ge(sig("x_loaded"), i * 16 + 16)
                stats(xin, i * 16, i * 16, st, mv, "ln_stat", "ln_mean")
                v.tensor_scalar(var[:, :, 0], mv[:, :, 1], 1e-5, None, ALU.add).then_inc(sig("ln_var"), 1)
                v.tensor_scalar(var[:, :, 1], mv[:, :, 1], 1.0 + 1e-6, 1e-11, ALU.mult, ALU.add).then_inc(sig("ln_var"), 1)
                v.wait_ge(sig("ln_rstd"), i * 4 + 1)
                for t in range(T):
                    v.tensor_scalar(h[:, t, :], xin[:, t, :], mv[:, t, 0:1], rs[:, t, 1:2], ALU.subtract,
                                    ALU.mult).then_inc(sig("h_ready"), 1)
                for t in range(T):
                    v.tensor_scalar(u[:, t, :], xin[:, t, :], mv[:, t, 0:1], rs[:, t, 0:1], ALU.subtract,
                                    ALU.mult).then_inc(sig("u_ready"), 1)
                for c_ in range(3):
                    src = (PA[:, 2, :], PA[:, 0, :], PA[0:48, 1, :])[c_].rearrange("p (b s) -> p b s", b=NB)
                    dst = (xc[:, 0, :], xc[:, 1, :], bcc[:, :])[c_].rearrange("p (b s) -> p b s", b=NB)
                    for k in (1, 0):
                        tap = (cw_x[:, 0, k:k + 1], cw_x[:, 1, k:k + 1], cw_bc[:, k:k + 1])[c_]
                        lag = 2 - k
                        if k == 1:
                            v.wait_ge(sig("conv_tap"), i * 3 + c_ + 1)
                        else:
                            v.wait_ge(sig("conv_done"), i * 6 + 2 * c_ + 1)
                        v.scalar_tensor_tensor(dst[:, :, lag:S], src[:, :, 0:S - lag], tap, dst[:, :, lag:S],
                                               ALU.mult, ALU.add).then_inc(sig("conv_done"), 1)
                v.wait_ge(sig("dt_ps"), i + 1)
                v.tensor_tensor(dv[:, :].rearrange("p (t k) -> p t k", k=NH), PA[:, 3, 0:T * NH].rearrange("p (t k) -> p t k", k=NH),
                                dtb[:, :].unsqueeze(1).broadcast_to([P, T, NH]), ALU.add).then_inc(sig("dt_v"), 1)
                v.wait_ge(sig("dt_v"), i + 1)
                v.scalar_tensor_tensor(dn[:, :], dv[:, :], -1.0, dv[:, :], ALU.mult, ALU.min).then_inc(sig("dt_n"), 1)
                v.wait_ge(sig("dt_u"), i + 1)
                v.tensor_scalar(dw[:, :], du[:, :], 2.0, None, ALU.add).then_inc(sig("dt_w"), 1)
                v.wait_ge(sig("dt_w"), i * 2 + 1)
                v.reciprocal(dr[:, :], dw[:, :]).then_inc(sig("dt_w"), 1)
                v.wait_ge(sig("dt_w"), i * 2 + 2)
                v.tensor_tensor(dz[:, :], du[:, :], dr[:, :], ALU.mult).then_inc(sig("dt_z"), 1)
                v.tensor_scalar(dv[:, :], dv[:, :], 0.0, None, ALU.max).then_inc(sig("dt_z"), 1)
                v.wait_ge(sig("cb_ps"), i + 1)
                v.tensor_tensor(cbm[:, :, :], PA[:, 1, 0:T * S].rearrange("p (t s) -> p t s", t=T),
                                seen[:, :].unsqueeze(1).broadcast_to([P, T, S]), ALU.mult).then_inc(sig("cbm_ready"), 1)
                v.wait_ge(sig("dt_poly"), i * 18 + 18)
                v.wait_ge(sig("dt_z"), i * 2 + 2)
                dtf = dtt[:, :, :].rearrange("p t k -> p (t k)")
                v.scalar_tensor_tensor(dtf, dp[:, :], 2.0, dv[:, :], ALU.mult, ALU.add).then_inc(sig("dt_ready"), 1)
                v.wait_ge(sig("dt_ready"), i + 1)
                v.tensor_tensor(aa[:, :, :], dtt[:, :, :], negA[:, :].unsqueeze(1).broadcast_to([P, T, NH]),
                                ALU.mult).then_inc(sig("a_ready"), 1)
                for k in range(2):
                    v.wait_ge(sig("xT_ps"), i * 2 + k + 1)
                    v.tensor_tensor(xdt[:, 2 * k:2 * k + 2, :, :], PA[:, 2 + k, :].rearrange("p (t k s) -> p t k s", t=2, k=NH),
                                    dtt[:, 2 * k:2 * k + 2, :].unsqueeze(3).broadcast_to([P, 2, NH, S]),
                                    ALU.mult).then_inc(sig("xdt_ready"), 1)
                for t in range(T):
                    if t == 0:
                        v.wait_ge(sig("cbm_ready"), i + 1)
                    if t % 2 == 0:
                        v.wait_ge(sig("decay"), i * 2 + t // 2 + 1)
                    v.tensor_tensor(M[:, t, :, :], dec[:, t, :, :], cbm[:, t, :].unsqueeze(1).broadcast_to([P, NH, S]),
                                    ALU.mult).then_inc(sig("M_ready"), 1)
                for k in range(2):
                    v.wait_ge(sig("y_ps"), i + 1)
                    for b in range(2):
                        of = lambda ap: ap.rearrange("p (t b s) -> p b t s", t=T, b=2)[:, b]
                        ins = v.scalar_tensor_tensor(of(y2[:, k, :]), of(xc[:, k, :]), dskip[:, k:k + 1],
                                                     PA[:, 2 * b + k, 0:T * S].rearrange("p (t s) -> p t s", t=T), ALU.mult,
                                                     ALU.add)
                    ins.then_inc(sig("y_skip"), 1)
                for k in range(2):
                    v.wait_ge(sig("y_skip"), i * 2 + k + 1)
                    v.tensor_tensor(y2[:, k, :], y2[:, k, :], zs[:, k, :], ALU.mult).then_inc(sig("g_ready"), 1)
                v.wait_ge(sig("gate_ps"), i + 1)
                v.tensor_scalar(rgi[:, :], PA[:, 3, 0:T], 1.0 / DI, 1e-5, ALU.mult, ALU.add).then_inc(sig("gate_var"), 1)
                v.wait_ge(sig("gate_rstd"), i + 1)
                v.wait_ge(sig("mix_ps"), i + 1)
                for t in range(T):
                    v.scalar_tensor_tensor(x1[:, t, :], PA[:, 2, t * P:t * P + P], rg[:, t:t + 1], u[:, t, :], ALU.mult,
                                           ALU.add).then_inc(sig("x1_ready"), 1)
                v.wait_ge(sig("x1_ready"), i * 4 + 4)
                stats(x1, i * 16 + 4, i * 16 + 4, st, mv, "ln_stat", "ln_mean")
                v.tensor_tensor(msq[:, :], mv[:, :, 0], mv[:, :, 0], ALU.mult).then_inc(sig("msq_ready"), 1)
                v.wait_ge(sig("msq_ready"), i + 1)
                v.scalar_tensor_tensor(var[:, :, 0], msq[:, :], 1e-6, mv[:, :, 1], ALU.add, ALU.add).then_inc(sig("ln_var"), 1)
                v.wait_ge(sig("xb_ready"), i + 1)
                v.tensor_tensor(xb[:, :, :], xb[:, :, :], x1[:, :, :], ALU.add).then_inc(sig("xb_sum"), 1)
                v.wait_ge(sig("ln_rstd"), i * 4 + 2)
                for t in range(T):
                    v.tensor_scalar(h[:, t, :], x1[:, t, :], rs[:, t, 0:1], None, ALU.mult).then_inc(sig("h_ready"), 1)
                v.wait_ge(sig("xb_sum"), i + 1)
                v.wait_ge(sig("mlp_ps"), i + 1)
                v.tensor_tensor(xA[:, :, :], PA[:, 3, :].rearrange("p (t d) -> p t d", t=T), xb[:, :, :],
                                ALU.add).then_inc(sig("xA_ready"), 1)

                v.wait_ge(sig("xA_ready"), i + 1)
                stats(xA, i * 16 + 8, i * 16 + 8, st, mv, "ln_stat", "ln_mean")
                v.tensor_scalar(var[:, :, 0], mv[:, :, 1], 1e-5, None, ALU.add).then_inc(sig("ln_var"), 1)
                v.wait_ge(sig("ptr_loaded"), i * 16 + 16)
                for k in range(3):
                    v.tensor_scalar(pf[:, :, k], ptr[:, :], float(k), 0.0, ALU.add, ALU.max).then_inc(sig("pf"), 1)
                v.wait_ge(sig("pf"), i * 4 + 3)
                v.tensor_scalar(pf[:, :, :], pf[:, :, :], float(S - 1), None, ALU.min).then_inc(sig("pf"), 1)
                v.wait_ge(sig("pf"), i * 4 + 4)
                for t in range(T):
                    v.tensor_tensor(O[:, t, :, :], pf[:, t, :].unsqueeze(2).broadcast_to([P, 3, S]),
                                    iota[:, :].unsqueeze(1).broadcast_to([P, 3, S]), ALU.is_equal).then_inc(sig("O_ready"), 1)
                v.wait_ge(sig("O_ready"), i * 4 + 4)
                v.wait_ge(sig("ids_loaded"), i * 32 + 32)
                v.tensor_tensor(rprod[:, :, :], O[:, :, 0, :], idsb[:, :, :], ALU.mult).then_inc(sig("ids_free"), 1)
                v.wait_ge(sig("ids_free"), i + 1)
                v.tensor_reduce(rid[:, :], rprod[:, :, :], AX.X, ALU.add).then_inc(sig("rid_ready"), 1)
                v.wait_ge(sig("rid_ready"), i + 1)
                v.tensor_tensor(R[:, :, 0:5], rid[:, :].unsqueeze(2).broadcast_to([P, T, 5]),
                                iota[:, 0:5].unsqueeze(1).broadcast_to([P, T, 5]), ALU.is_equal).then_inc(sig("R_ready"), 1)
                v.wait_ge(sig("R_ready"), i * 3 + 1)
                v.tensor_reduce(R[:, :, 5], R[:, :, 0:5], AX.X, ALU.add).then_inc(sig("R_ready"), 1)
                v.wait_ge(sig("R_ready"), i * 3 + 2)
                v.tensor_scalar(R[:, :, 5], R[:, :, 5], -1.0, 1.0, ALU.mult, ALU.add).then_inc(sig("R_ready"), 1)
                v.wait_ge(sig("ln_rstd"), i * 4 + 3)
                for t in range(T):
                    v.tensor_scalar(h[:, t, :], xA[:, t, :], mv[:, t, 0:1], rs[:, t, 0:1], ALU.subtract,
                                    ALU.mult).then_inc(sig("h_ready"), 1)
                v.wait_ge(sig("sx_ps"), i + 1)
                sx = PA[:, 3, :].rearrange("p (t x s) -> p x t s", t=T, x=2)
                for x_ in range(2):
                    for k in range(3):
                        v.tensor_tensor(prod[:, x_, :, k, :], sx[:, x_], O[:, :, k, :], ALU.mult).then_inc(sig("sx_prod"), 1)
                for x_ in range(2):
                    v.wait_ge(sig("sx_prod"), i * 6 + 3 * x_ + 3)
                    v.tensor_reduce(sc[:, x_, :, :], prod[:, x_, :, :, :], AX.X, ALU.add).then_inc(sig("sx_ready"), 1)
                v.wait_ge(sig("sx_ready"), i * 2 + 2)
                l0, l1, l2 = (sc[:, 0, :, k] for k in range(3))
                v.tensor_tensor(V6[:, :, 0], l1, l2, ALU.add)
                v.tensor_tensor(V6[:, :, 1], l1, l2, ALU.max)
                v.tensor_scalar(V6[:, :, 2], l1, -1.0, None, ALU.mult)
                v.scalar_tensor_tensor(V6[:, :, 3], l1, -1.0, l2, ALU.mult, ALU.max)
                v.tensor_tensor(V6[:, :, 4], l1, l2, ALU.subtract)
                v.tensor_copy(V6[:, :, 5], l0).then_inc(sig("V6"), 1)
                v.wait_ge(sig("V6"), i * 3 + 1)
                v.scalar_tensor_tensor(V6[:, :, 4], V6[:, :, 4], -1.0, V6[:, :, 4], ALU.mult, ALU.max).then_inc(sig("V6"), 1)
                v.wait_ge(sig("V6"), i * 3 + 2)
                v.tensor_tensor(V6[:, :, :], V6[:, :, :], R[:, :, :], ALU.mult).then_inc(sig("V6"), 1)
                v.wait_ge(sig("V6"), i * 3 + 3)
                v.tensor_reduce(l0, V6[:, :, :], AX.X, ALU.add).then_inc(sig("sm"), 1)
                sc8 = sc[:, :, :, :].rearrange("p x t k -> p (x t) k")
                v.wait_ge(sig("sm"), i * 6 + 1)
                v.tensor_reduce(smx[:, :], sc8, AX.X, ALU.max).then_inc(sig("sm"), 1)
                v.wait_ge(sig("sm"), i * 6 + 2)
                v.tensor_tensor(sc8, sc8, smx[:, :].unsqueeze(2).broadcast_to([P, 2 * T, 3]), ALU.subtract).then_inc(sig("sm"), 1)
                v.wait_ge(sig("sm_exp"), i + 1)
                v.tensor_reduce(ssm[:, :], sc8, AX.X, ALU.add).then_inc(sig("sm"), 1)
                v.wait_ge(sig("sm"), i * 6 + 4)
                v.reciprocal(ssm[:, :], ssm[:, :]).then_inc(sig("sm"), 1)
                v.wait_ge(sig("sm"), i * 6 + 5)
                v.tensor_tensor(sc8, sc8, ssm[:, :].unsqueeze(2).broadcast_to([P, 2 * T, 3]), ALU.mult).then_inc(sig("sm"), 1)
                for x_ in range(2):
                    v.wait_ge(sig("OW_ready"), i * 8 + 4 * x_ + 4)
                    v.tensor_tensor(Pm[:, :, x_, :], prod[:, x_, :, 0, :], prod[:, x_, :, 1, :], ALU.add).then_inc(sig("Pm_part"), 1)
                for x_ in range(2):
                    v.wait_ge(sig("Pm_part"), i * 2 + x_ + 1)
                    v.tensor_tensor(Pm[:, :, x_, :], Pm[:, :, x_, :], prod[:, x_, :, 2, :], ALU.add).then_inc(sig("Pm_ready"), 1)
                v.wait_ge(sig("cx_ps"), i + 1)
                v.tensor_copy(cT2[:, 1, :], PA[:, 2, :]).then_inc(sig("cT2_dve"), 1)
                v.wait_ge(sig("xo_ps"), i + 1)
                v.tensor_tensor(xA[:, :, :], xA[:, :, :], PA[:, 3, :].rearrange("p (t d) -> p t d", t=T),
                                ALU.add).then_inc(sig("x2_ready"), 1)

                v.wait_ge(sig("x2_ready"), i + 1)
                stats(xA, i * 16 + 12, i * 16 + 12, st, mv, "ln_stat", "ln_mean")
                v.tensor_scalar(var[:, :, 0], mv[:, :, 1], 1e-5, None, ALU.add).then_inc(sig("ln_var"), 1)
                v.wait_ge(sig("ln_rstd"), i * 4 + 4)
                for t in range(T):
                    v.tensor_scalar(h[:, t, :], xA[:, t, :], mv[:, t, 0:1], rs[:, t, 0:1], ALU.subtract,
                                    ALU.mult).then_inc(sig("h_ready"), 1)

                def row_scale(k):
                    v.wait_ge(sig("q_small"), i * 10 + 5 * k + 1)
                    v.tensor_scalar(amx[:, :], amx[:, :], 1e-5, None, ALU.max).then_inc(sig("q_small"), 1)
                    v.wait_ge(sig("q_small"), i * 10 + 5 * k + 2)
                    v.reciprocal(ainv[:, :], amx[:, :]).then_inc(sig("q_small"), 1)
                    v.tensor_scalar(asc[:, :], amx[:, :], fs127[:, k:k + 1], None, ALU.mult).then_inc(sig("q_small"), 1)
                    v.wait_ge(sig("q_small"), i * 10 + 5 * k + 4)
                    v.tensor_scalar(ainv[:, :], ainv[:, :], 127.0, None, ALU.mult).then_inc(sig("q_small"), 1)
                    v.wait_ge(sig("q_small"), i * 10 + 5 * k + 5)

                v.wait_ge(sig("h_ready"), i * 16 + 16)
                v.tensor_reduce(amx[:, :], h[:, :, :], AX.X, ALU.max, apply_absolute_value=True).then_inc(sig("q_small"), 1)
                row_scale(0)
                for t in range(T):
                    v.tensor_scalar(t32[:, t, :], h[:, t, :], ainv[:, t:t + 1], MAGIC, ALU.mult, ALU.add).then_inc(sig("t32"), 1)
                v.wait_ge(sig("t32"), i * 4 + 4)
                v.tensor_scalar(xq[:, :, :], t32[:, :, :], MAGIC, 127.0, ALU.subtract, ALU.min).then_inc(sig("xq_ready"), 1)
                for t in range(T):
                    v.wait_ge(sig("f1_ps"), i * 4 + t + 1)
                    v.scalar_tensor_tensor(hb[:, t, :], PA[:, t, :], asc[:, t:t + 1], fb1[:, :], ALU.mult,
                                           ALU.add).then_inc(sig("hb_ready"), 1)
                for t in range(T):
                    v.wait_ge(sig("gelu"), i * 4 + t + 1)
                    ins = v.tensor_reduce(amx[:, t:t + 1], hb[:, t, :], AX.X, ALU.max, apply_absolute_value=True)
                ins.then_inc(sig("q_small"), 1)
                row_scale(1)
                for t in range(T):
                    v.wait_ge(sig("g32"), i * 4 + t + 1)
                    v.tensor_scalar(gq[:, t, :], g32[:, t, :], MAGIC, 127.0, ALU.subtract, ALU.min).then_inc(sig("gq_ready"), 1)
                v.wait_ge(sig("xb2_ready"), i + 1)
                v.wait_ge(sig("f2_ps"), i + 1)
                v.wait_ge(sig("out_ready"), i * T)
                for t in range(T):
                    v.scalar_tensor_tensor(xB[:, t, :], PA[:, 3, t * P:t * P + P], asc[:, t:t + 1], xb[:, t, :], ALU.mult,
                                           ALU.add).then_inc(sig("xB_part"), 1)

                def norm(k):
                    stats(xB, (i * 3 + k) * T, (i * 3 + k) * T, bst, bmv, "bln_stat", "bln_mean")
                    v.tensor_scalar(bvar[:, :], bmv[:, :, 1], 1e-5, None, ALU.add).then_inc(sig("bln_var"), 1)
                    v.wait_ge(sig("bln_rstd"), i * 3 + k + 1)
                    for t in range(T):
                        v.tensor_scalar(bh[:, t, :], xB[:, t, :], bmv[:, t, 0:1], brs[:, t:t + 1], ALU.subtract,
                                        ALU.mult).then_inc(sig("bh_ready"), 1)

                def queries_keys(k, what, bias):
                    for r in range(2):
                        v.wait_ge(sig("qk_ps"), i * 6 + 2 * k + r + 1)
                        if what == 2:
                            src = PB[:, r, :].rearrange("p (t q d) -> p t q d", t=2, q=2)
                            dst = qk32[:, 2 * r:2 * r + 2, :, :]
                            if bias is None:
                                v.tensor_copy(dst, src).then_inc(sig("qk32"), 1)
                            else:
                                v.tensor_tensor(dst.rearrange("p t q d -> p t (q d)"), src.rearrange("p t q d -> p t (q d)"),
                                                bias.unsqueeze(1).broadcast_to([P, 2, 2 * D]), ALU.add).then_inc(sig("qk32"), 1)
                        else:
                            v.tensor_tensor(qk32[:, 2 * r:2 * r + 2, 0, :], PB[:, r, 0:256].rearrange("p (t d) -> p t d", t=2),
                                            bias.unsqueeze(1).broadcast_to([P, 2, D]), ALU.add).then_inc(sig("qk32"), 1)
                    for r in range(2):
                        for q in range(2):
                            if what == 1 and q == 1:
                                continue
                            v.wait_ge(sig("aug_hi"), (i * 10 + (0, 4, 6)[k]) + (2 * r + q + 1 if what == 2 else r + 1))
                            slot = 16 if q == 0 else 8
                            lo = aug[:, q, 2 * r:2 * r + 2, :, slot:slot + HD]
                            hi = aug[:, q, 2 * r:2 * r + 2, :, 0:HD]
                            v.tensor_tensor(lo, qk32[:, 2 * r:2 * r + 2, q, :].rearrange("p t (h d) -> p t h d", h=H), hi,
                                            ALU.subtract).then_inc(sig("aug_lo"), 1)

                def values(k, bias):
                    v.wait_ge(sig("v_ps"), i * 2 + k + 1)
                    for h2 in range(2):
                        rows_ = slice(S * h2, S * h2 + S)
                        dst = Vx[rows_, :, :, 9 * h2:9 * h2 + HD]
                        src = PB[rows_, 3, :].rearrange("p (b u d) -> p b u d", b=NB, u=8)
                        if bias is None:
                            v.tensor_copy(dst, src).then_inc(sig("v_ready"), 1)
                        else:
                            bb = bias[rows_, :].rearrange("p (u d) -> p u d", u=8).unsqueeze(1).broadcast_to([S, NB, 8, HD])
                            v.tensor_tensor(dst, src, bb, ALU.add).then_inc(sig("v_ready"), 1)

                def top(k, r, j):
                    n_ = (i * 3 + k) * 8 + 4 * r + j
                    src = PB[:, j, :].rearrange("p (a s) -> p a s", s=S)
                    v.wait_ge(sig("s_ps"), n_ + 1)
                    if k == 2:
                        if r == 0 and j == 0:
                            v.wait_ge(sig("mask_loaded"), i * 16 + 16)
                        v.tensor_tensor(Pr[:, j, :, :].rearrange("p (t c) s -> p t c s", t=2), src.rearrange("p (t c) s -> p t c s", t=2),
                                        maskE[:, 2 * r:2 * r + 2, :].unsqueeze(2).broadcast_to([P, 2, 4, S]),
                                        ALU.add).then_inc(sig("s_biased"), 1)
                        v.wait_ge(sig("s_biased"), i * 8 + 4 * r + j + 1)
                        src = Pr[:, j, :, :]
                    v.tensor_reduce(mx[:, j, :], src, AX.X, ALU.max).then_inc(sig("mx"), 1)

                def shift(k, r, j):
                    n_ = (i * 3 + k) * 8 + 4 * r + j
                    src = Pr[:, j, :, :] if k == 2 else PB[:, j, :].rearrange("p (a s) -> p a s", s=S)
                    v.wait_ge(sig("mx"), n_ + 1)
                    v.tensor_tensor(Pr[:, j, :, :], src, mx[:, j, :].unsqueeze(2).broadcast_to([P, 8, S]),
                                    ALU.subtract).then_inc(sig("s_shifted"), 1)

                def attend(k):
                    for r in range(2):
                        top(k, r, 0)
                        for j in range(1, 4):
                            top(k, r, j)
                            shift(k, r, j - 1)
                        shift(k, r, 3)
                        for j in (1, 3):
                            v.wait_ge(sig("pT_ps"), (i * 3 + k) * 8 + 4 * r + j + 1)
                            v.tensor_copy(PT[:, j, :, :].rearrange("p a s -> p (a s)"), PB[:, j, :]).then_inc(sig("PT_dve"), 1)
                        v.wait_ge(sig("pv_ps"), (i * 3 + k) * 2 + r + 1)
                        pv = PB[:, :, 0:8 * (HD + 1)].rearrange("p j (a d) -> p j a d", d=HD + 1)
                        v.reciprocal(rc[:, :, :], pv[:, :, :, HD]).then_inc(sig("rc"), 1)
                        v.wait_ge(sig("rc"), (i * 3 + k) * 2 + r + 1)
                        for t2 in range(2):
                            a4 = slice(4 * t2, 4 * t2 + 4)
                            v.tensor_tensor(cx[:, 2 * r + t2, :].rearrange("p (j a d) -> p j a d", j=4, a=4), pv[:, :, a4, 0:HD],
                                            rc[:, :, a4].unsqueeze(3).broadcast_to([P, 4, 4, HD]), ALU.mult).then_inc(sig("cx_ready"), 1)

                v.wait_ge(sig("xB_part"), i * 4 + 4)
                norm(0)
                queries_keys(0, 2, qkb[:, :])
                values(0, vb_par)
                attend(0)
                v.wait_ge(sig("cxT_ready"), i * 3 + 1)
                v.tensor_copy(cxT[:, 0, :, 1:S], cxT[:, 1, :, 0:S - 1]).then_inc(sig("cxT_shifted"), 1)
                v.tensor_copy(cxT[:, 2, :, 0:S - 1], cxT[:, 1, :, 1:S]).then_inc(sig("cxT_shifted"), 1)
                queries_keys(1, 1, cvb[:, :])
                attend(1)
                v.wait_ge(sig("xo_ready"), i + 1)
                v.wait_ge(sig("o_ps"), i * 2 + 1)
                v.tensor_tensor(xB[:, :, :], xo[:, :, :], PB[:, 1, :].rearrange("p (t d) -> p t d", t=T),
                                ALU.add).then_inc(sig("xB_sum"), 1)
                v.wait_ge(sig("xB_sum"), i * 2 + 1)
                norm(1)
                queries_keys(2, 2, None)
                values(1, None)
                attend(2)
                v.wait_ge(sig("o_ps"), i * 2 + 2)
                v.tensor_tensor(xB[:, :, :], xB[:, :, :], PB[:, 1, :].rearrange("p (t d) -> p t d", t=T),
                                ALU.add).then_inc(sig("xB_sum"), 1)
                v.wait_ge(sig("xB_sum"), i * 2 + 2)
                norm(2)
                v.wait_ge(sig("lg_ps"), i + 1)
                v.tensor_copy(lg[:, :, :], PB[:, 3, 0:T * E].rearrange("p (t e) -> p t e", t=T)).then_inc(sig("lg"), 1)
                v.wait_ge(sig("lg"), i + 1)
                v.memset(mark[:, :], 0.0)
                for t in range(T):
                    v.max(m8[:, t, :], lg[:, t, :]).then_inc(sig("m8"), 1)
                v.wait_ge(sig("m8"), i * 4 + 4)
                v.memset(mark[:, :], 0.0)
                for t in range(T):
                    v.max_index(ix8[:, t, :], m8[:, t, :], lg[:, t, :]).then_inc(sig("ix8"), 1)
                k0 = i * 11
                v.tensor_tensor(e8[:, :, :], m8[:, :, :], m8[:, :, 0:1].broadcast_to([P, T, E]), ALU.subtract).then_inc(sig("gates"), 1)
                v.wait_ge(sig("ix8"), i * 4 + 4)
                v.tensor_copy(ixf[:, :, :], ix8[:, :, 0:2]).then_inc(sig("gates"), 1)
                v.wait_ge(sig("gates"), k0 + 2)
                for t in range(T):
                    ins = v.tensor_tensor(oh[:, t, :, :], iota[:, 0:E].unsqueeze(1).broadcast_to([P, 2, E]),
                                          ixf[:, t, :].unsqueeze(2).broadcast_to([P, 2, E]), ALU.is_equal)
                ins.then_inc(sig("gates"), 1)
                v.wait_ge(sig("e8_exp"), i + 1)
                v.tensor_reduce(s8[:, :], e8[:, :, :], AX.X, ALU.add).then_inc(sig("gates"), 1)
                v.wait_ge(sig("gates"), k0 + 4)
                v.reciprocal(r8[:, :], s8[:, :]).then_inc(sig("gates"), 1)
                v.wait_ge(sig("gates"), k0 + 5)
                v.tensor_tensor(g2[:, :, :], e8[:, :, 0:2], r8[:, :].unsqueeze(2).broadcast_to([P, T, 2]), ALU.mult).then_inc(sig("gates"), 1)
                v.wait_ge(sig("gates"), k0 + 6)
                v.scalar_tensor_tensor(d2[:, :], g2[:, :, 0], 1e-8, g2[:, :, 1], ALU.add, ALU.add).then_inc(sig("gates"), 1)
                v.wait_ge(sig("gates"), k0 + 7)
                v.reciprocal(r8[:, :], d2[:, :]).then_inc(sig("gates"), 1)
                v.wait_ge(sig("gates"), k0 + 8)
                v.tensor_tensor(cw2[:, :, :], g2[:, :, :], r8[:, :].unsqueeze(2).broadcast_to([P, T, 2]), ALU.mult).then_inc(sig("gates"), 1)
                v.wait_ge(sig("gates"), k0 + 9)
                for t in range(T):
                    ins = v.tensor_tensor(oh[:, t, :, :], oh[:, t, :, :], cw2[:, t, :].unsqueeze(2).broadcast_to([P, 2, E]), ALU.mult)
                ins.then_inc(sig("gates"), 1)
                v.wait_ge(sig("gates"), k0 + 10)
                v.tensor_tensor(cwt[:, :, :], oh[:, :, 0, :], oh[:, :, 1, :], ALU.add).then_inc(sig("gates"), 1)
                v.wait_ge(sig("stored"), i * 16)
                v.wait_ge(sig("xh_ready"), i + 1)
                for e in range(E + 1):
                    if e < E:
                        v.wait_ge(sig("w1_ps"), i * 16 + 2 * e + 2)
                        if e >= 2:
                            v.wait_ge(sig("w2_ps"), i * 8 + e - 1)
                        v.tensor_scalar(hid[:, e % 2, 1, :], PB[:, 1, :], mb1[:, 2 * e + 1:2 * e + 2], 0.0, ALU.add,
                                        ALU.max).then_inc(sig("hid_dve"), 1)
                    if e == 0:
                        v.wait_ge(sig("b2_ps"), i + 1)
                        v.tensor_tensor(acc[:, :, :], xo[:, :, :], PB[:, 3, :].rearrange("p (t d) -> p t d", t=T),
                                        ALU.add).then_inc(sig("acc"), 1)
                    else:
                        v.wait_ge(sig("w2_ps"), i * 8 + e)
                        for t in range(T):
                            if t == 0:
                                v.wait_ge(sig("acc"), i * 8 + e)
                            ins = v.scalar_tensor_tensor(acc[:, t, :], PB[:, 2 + (e - 1) % 2, t * P:t * P + P], cwt[:, t, e - 1:e],
                                                         acc[:, t, :], ALU.mult, ALU.add)
                            if e == E:
                                ins.then_inc(sig("out_ready"), 1)
                        if e < E:
                            ins.then_inc(sig("acc"), 1)

        @block.scalar
        def _(act):
            for dst, src in LOADS[1::2]:
                act.dma_start(dst, src, allow_slow_non_contiguous=True).then_inc(sig("weights_loaded"), 16)
            act.wait_ge(sig("weights_loaded"), 16 * NLOADS)
            act.activation(negA[:, :], alog[:, :], ACT.Exp).then_inc(sig("act_setup"), 1)
            act.wait_ge(sig("dve_setup"), 2)
            act.activation(council[:, :], council[:, :], ACT.Exp).then_inc(sig("act_setup"), 1)
            act.wait_ge(sig("setup_done"), 3)

            def copy(dst, src, wait, value, done):
                act.wait_ge(sig(wait), value)
                act.activation(dst, src, ACT.Copy).then_inc(sig(done), 1)

            with act.Fori(0, groups) as i:
                copy(hT[:, :], PA[:, 0, :], "hT_ps", i * 3 + 1, "hT_ready")
                for k in range(2):
                    act.wait_ge(sig("z_ps"), i * 2 + k + 1)
                    act.activation(zs[:, k, :], PA[:, (1, 3)[k], :], ACT.Silu).then_inc(sig("z_ready"), 1)
                for c_ in range(3):
                    act.wait_ge(sig("xbc_ps"), i * 3 + c_ + 1)
                    if c_ < 2:
                        act.activation(xc[:, c_, :], PA[:, (2, 0)[c_], :], ACT.Identity, bias=cb_x[:, c_:c_ + 1],
                                       scale=cw_x[:, c_, 2:3]).then_inc(sig("conv_tap"), 1)
                    else:
                        act.activation(bcc[:, :], PA[0:48, 1, :], ACT.Identity, bias=cb_bc[:, :],
                                       scale=cw_bc[:, 2:3]).then_inc(sig("conv_tap"), 1)
                for c_ in range(2):
                    act.wait_ge(sig("conv_done"), i * 6 + 2 * c_ + 2)
                    act.activation(xc[:, c_, :], xc[:, c_, :], ACT.Silu).then_inc(sig("xs_ready"), 1)
                act.wait_ge(sig("conv_done"), i * 6 + 6)
                act.activation(bT[:, :], bcc[0:NS, :], ACT.Silu).then_inc(sig("bc_ready"), 1)
                act.activation(cT[:, :], bcc[32:32 + NS, :], ACT.Silu).then_inc(sig("bc_ready"), 1)
                act.wait_ge(sig("dt_n"), i + 1)
                act.activation(du[:, :], dn[:, :], ACT.Exp).then_inc(sig("dt_u"), 1)
                for k in range(2):
                    act.wait_ge(sig("seg_ps"), i * 2 + k + 1)
                    act.activation(dec[:, 2 * k:2 * k + 2, :, :].rearrange("p t k s -> p (t k s)"), PA[:, (0, 1)[k], :],
                                   ACT.Exp).then_inc(sig("decay"), 1)
                for k in range(2):
                    act.wait_ge(sig("g_ready"), i * 2 + k + 1)
                    act.activation(gsq[:, k, :], y2[:, k, :], ACT.Square).then_inc(sig("gsq"), 1)
                copy(hT[:, :], PA[:, 0, :], "hT_ps", i * 3 + 2, "hT_ready")
                for k in range(4):
                    act.wait_ge(sig("mh_ps"), i * 4 + k + 1)
                    act.activation(hs[:, k, :], PA[:, (1, 2)[k % 2], :], ACT.Silu, bias=b1m[:, k:k + 1]).then_inc(sig("hs"), 1)
                copy(ctxT[:, :, :].rearrange("p t s -> p (t s)"), PA[:, 0, :], "cxT_ps", i + 1, "ctxT_ready")
                copy(hT[:, :], PA[:, 1, :], "hT_ps", i * 3 + 3, "hT_ready")
                for k in range(2):
                    copy(qx[:, k, :], PA[:, (0, 2)[k], :], "qx_ps", i * 2 + k + 1, "qx_ready")
                act.wait_ge(sig("sm"), i * 6 + 3)
                sc24 = sc[:, :, :, :].rearrange("p x t k -> p (x t k)")
                act.activation(sc24, sc24, ACT.Exp).then_inc(sig("sm_exp"), 1)
                copy(PmT[:, :, :].rearrange("p t s -> p (t s)"), PA[:, 0, :], "PmT_ps", i + 1, "PmT_ready")
                copy(cT2[:, 0, :], PA[:, 1, :], "cx_ps", i + 1, "cT2_act")
                copy(xqT[:, :].bitcast(fp32), PA[:, 0, 0:256], "xqT_ps", i + 1, "xqT_ready")
                for t in range(T):
                    act.wait_ge(sig("hb_ready"), i * 4 + t + 1)
                    act.activation(hb[:, t, :], hb[:, t, :], ACT.Gelu).then_inc(sig("gelu"), 1)
                act.wait_ge(sig("q_small"), i * 10 + 10)
                for t in range(T):
                    act.activation(g32[:, t, :], hb[:, t, :], ACT.Copy, bias=MAGIC, scale=ainv[:, t:t + 1]).then_inc(sig("g32"), 1)
                for t in range(T):
                    copy(gqT[:, t, :, :].rearrange("p c k -> p (c k)").bitcast(fp32), PA[:, (0, 1)[t % 2], 0:256],
                         "gqT_ps", i * 4 + t + 1, "gqT_ready")
                def split_hi(k, what):
                    for r in range(2):
                        act.wait_ge(sig("qk32"), i * 6 + 2 * k + r + 1)
                        for q in range(what):
                            src = qk32[:, 2 * r:2 * r + 2, q, :].rearrange("p t (h d) -> p t h d", h=H)
                            for n_, slot in enumerate((0, 8) if q == 0 else (0, 16)):
                                ins = act.activation(aug[:, q, 2 * r:2 * r + 2, :, slot:slot + HD], src, ACT.Copy)
                            ins.then_inc(sig("aug_hi"), 1)

                def transposed(k, what):
                    for t in range(T):
                        act.wait_ge(sig("augT_ps"), (i * 3 + k) * T + t + 1)
                        w_ = 256 * what
                        act.activation(augT[:, t, 0:what, :, :].rearrange("p q c k -> p (q c k)").bitcast(fp32),
                                       PB[:, t, 0:w_], ACT.Copy).then_inc(sig("augT_ready"), 1)

                def attend(k):
                    for r in range(2):
                        for j in range(4):
                            act.wait_ge(sig("s_shifted"), (i * 3 + k) * 8 + 4 * r + j + 1)
                            pr = Pr[:, j, :, :].rearrange("p a s -> p (a s)")
                            act.activation(pr, pr, ACT.Exp).then_inc(sig("exp_ready"), 1)
                        for j in (0, 2):
                            copy(PT[:, j, :, :].rearrange("p a s -> p (a s)"), PB[:, j, :],
                                 "pT_ps", (i * 3 + k) * 8 + 4 * r + j + 1, "PT_act")

                copy(bhT[:, :], PB[:, 0, :], "bhT_ps", i * 3 + 1, "bhT_ready")
                split_hi(0, 2)
                transposed(0, 2)
                attend(0)
                act.wait_ge(sig("cxo_ps"), i * 3 + 1)
                cxp = PB[:, 1, :].rearrange("p (b s) -> p b s", b=NB)
                act.activation(cxT[:, 1, :, :], cxp, ACT.Copy).then_inc(sig("cxT_ready"), 1)
                split_hi(1, 1)
                transposed(1, 1)
                attend(1)
                copy(bhT[:, :], PB[:, 0, :], "cxo_ps", i * 3 + 2, "cxT_ready")
                copy(bhT[:, :], PB[:, 0, :], "bhT_ps", i * 3 + 2, "bhT_ready")
                split_hi(2, 2)
                transposed(2, 2)
                attend(2)
                copy(bhT[:, :], PB[:, 0, :], "cxo_ps", i * 3 + 3, "cxT_ready")
                copy(bhT[:, :], PB[:, 0, :], "bhT_ps", i * 3 + 3, "bhT_ready")
                act.wait_ge(sig("gates"), i * 11 + 1)
                act.activation(e8[:, :, :], e8[:, :, :], ACT.Exp).then_inc(sig("e8_exp"), 1)
                copy(cwT[:, :], PB[0:E, 2, :], "cwT_ps", i + 1, "cwT_ready")
                for e in range(E):
                    act.wait_ge(sig("w1_ps"), i * 16 + 2 * e + 1)
                    if e >= 2:
                        act.wait_ge(sig("w2_ps"), i * 8 + e - 1)
                    act.activation(hid[:, e % 2, 0, :], PB[:, 0, :], ACT.Relu, bias=mb1[:, 2 * e:2 * e + 1]).then_inc(sig("hid_act"), 1)

        @block.tensor
        def _(pe):
            mm, tr = pe.matmul, pe.transpose
            pe.wait_ge(sig("preset"), 10)
            pe.wait_ge(sig("dve_setup"), 1)
            mm(PA[:, 0, 0:2], ones[:, :], fabs[:, :], start=True, stop=True).then_inc(sig("pe_setup"), 1)
            pe.wait_ge(sig("dve_setup"), 3)
            tr(PA[:, 1, 0:P], xw[:, 6, :], ident[:, :])
            for x_ in range(2):
                mm(PA[:, 1, 128 + 128 * x_:256 + 128 * x_], xw[:, 3 * x_, :], xw[:, 3 * x_ + 1, :], start=True, stop=True)
            for k in range(3):
                tr(PA[:, 2, P * k:P * k + P], aw[:, k, :], ident[:, :])
            tr(PA[:, 2, 384:512], owp[:, :], ident[:, :])
            for k in range(3):
                tr(PA[:, 3, P * k:P * k + P], cvp[:, k, :], ident[:, :])
            for k in range(4):
                tr(PB[:, 0, 64 * k:64 * k + 64].bitcast(bf16), f1q[:, k, :], identb[:, :])
                ins = tr(PB[:, 1, 64 * k:64 * k + 64].bitcast(bf16), f2q[:, P * k:P * k + P], identb[:, :])
            ins.then_inc(sig("pe_setup"), 1)
            pe.wait_ge(sig("dve_setup"), 4)
            for x_ in range(2):
                ins = mm(PA[:, 0, x_ * P:x_ * P + P], xw[:, 3 * x_ + 2, :], woutT[:, :], start=True, stop=True)
            ins.then_inc(sig("pe_setup"), 1)
            pe.wait_ge(sig("setup_done"), 3)

            def tile(t):
                return slice(t * P, t * P + P)

            def seq(t, b):
                return slice(t * P + b * S, t * P + b * S + S)

            with pe.Fori(0, groups) as i:
                def norm_T(bank, k):
                    for t in range(T):
                        pe.wait_ge(sig("h_ready"), i * 16 + 4 * k + t + 1)
                        ins = tr(PA[:, bank, tile(t)], h[:, t, :], ident[:, :])
                    ins.then_inc(sig("hT_ps"), 1)

                norm_T(0, 0)
                pe.wait_ge(sig("hT_ready"), i * 3 + 1)
                mm(PA[:, 1, :], w_in[:, 0:P], hT[:, :], start=True, stop=True).then_inc(sig("z_ps"), 1)
                mm(PA[:, 2, :], w_in[:, DI:DI + P], hT[:, :], start=True, stop=True).then_inc(sig("xbc_ps"), 1)
                mm(PA[:, 3, :], w_in[:, P:2 * P], hT[:, :], start=True, stop=True).then_inc(sig("z_ps"), 1)
                mm(PA[:, 0, :], w_in[:, DI + P:DI + 2 * P], hT[:, :], start=True, stop=True).then_inc(sig("xbc_ps"), 1)
                pe.wait_ge(sig("z_ready"), i * 2 + 1)
                mm(PA[0:48, 1, :], w_bc[:, :], hT[:, :], start=True, stop=True).then_inc(sig("xbc_ps"), 1)
                pe.wait_ge(sig("z_ready"), i * 2 + 2)
                for t in range(T):
                    ins = mm(PA[:, 3, NH * t:NH * t + NH], hT[:, tile(t)], w_in[:, 2 * DI + 2 * NS:548], start=True, stop=True)
                ins.then_inc(sig("dt_ps"), 1)
                pe.wait_ge(sig("bc_ready"), i * 2 + 2)
                for t in range(T):
                    for b in range(2):
                        ins = mm(PA[S * b:S * b + S, 1, t * S:t * S + S], bT[:, seq(t, b)], cT[:, seq(t, b)], start=True, stop=True)
                ins.then_inc(sig("cb_ps"), 1)
                pe.wait_ge(sig("xs_ready"), i * 2 + 2)
                pe.wait_ge(sig("dt_v"), i + 1)
                for k in range(2):
                    for t in (2 * k, 2 * k + 1):
                        for c_ in range(2):
                            ins = tr(PA[:, 2 + k, 256 * (t % 2) + P * c_:256 * (t % 2) + P * c_ + P], xc[:, c_, tile(t)], ident[:, :])
                    ins.then_inc(sig("xT_ps"), 1)
                pe.wait_ge(sig("cbm_ready"), i + 1)
                for k in range(2):
                    pe.wait_ge(sig("G_ready"), i * 4 + 2 * k + 2)
                    mm(PA[:, k, :], after[:, :], G[:, 2 * k:2 * k + 2, :, :].rearrange("p t k s -> p (t k s)"),
                       start=True, stop=True).then_inc(sig("seg_ps"), 1)
                wait_apart(pe, "M_ready", i * 4 + 4)
                for t in range(T):
                    for b in range(2):
                        for hh in range(NH):
                            r = S * (hh % 2)
                            ins = mm(PA[r:r + S, 2 * b + hh // 2, t * S:t * S + S], xdt[S * b:S * b + S, t, hh, :], M[S * b:S * b + S, t, hh, :],
                                     start=True, stop=True)
                ins.then_inc(sig("y_ps"), 1)
                for t in range(T):
                    for k in range(2):
                        if t == 0:
                            pe.wait_ge(sig("gsq"), i * 2 + k + 1)
                        ins = mm(PA[:, 3, t:t + 1], gsq[:, k, tile(t)], ones[:, 0:1], start=(k == 0), stop=(k == 1))
                ins.then_inc(sig("gate_ps"), 1)
                for t in range(T):
                    for k in range(2):
                        ins = mm(PA[:, 2, tile(t)], y2[:, k, tile(t)], w_out[:, k, :], start=(k == 0), stop=(k == 1))
                ins.then_inc(sig("mix_ps"), 1)
                norm_T(0, 1)
                pe.wait_ge(sig("hT_ready"), i * 3 + 2)
                for k in range(4):
                    if k >= 2:
                        pe.wait_ge(sig("hs"), i * 4 + k - 1)
                    mm(PA[:, (1, 2)[k % 2], :], w1m[:, P * k:P * k + P], hT[:, :], start=True, stop=True).then_inc(sig("mh_ps"), 1)
                pe.wait_ge(sig("ctx_loaded"), i * 32 + 32)
                pe.wait_ge(sig("hs"), i * 4 + 4)
                for t in range(T):
                    for k in range(4):
                        ins = mm(PA[:, 3, tile(t)], hs[:, k, tile(t)], w2m[:, k, :], start=(k == 0), stop=(k == 3))
                ins.then_inc(sig("mlp_ps"), 1)

                for t in range(T):
                    for b in range(2):
                        ins = tr(PA[:, 0, seq(t, b)], ctx2[0:S, t, b, :], ident[0:S, 0:S])
                ins.then_inc(sig("cxT_ps"), 1)
                norm_T(1, 2)
                pe.wait_ge(sig("ctxT_ready"), i + 1)
                pe.wait_ge(sig("hT_ready"), i * 3 + 3)
                for x_ in range(2):
                    mm(PA[:, (0, 2)[x_], :], wqk[:, x_, :], hT[:, :], start=True, stop=True).then_inc(sig("qx_ps"), 1)
                pe.wait_ge(sig("xA_ready"), i + 1)
                pe.wait_ge(sig("qx_ready"), i * 2 + 2)
                for t in range(T):
                    for x_ in range(2):
                        for b in range(2):
                            ins = mm(PA[S * b:S * b + S, 3, t * P + x_ * S:t * P + x_ * S + S], qx[:, x_, seq(t, b)],
                                     ctxT[:, t, b * S:b * S + S], start=True, stop=True)
                ins.then_inc(sig("sx_ps"), 1)
                pe.wait_ge(sig("Pm_ready"), i * 2 + 2)
                for t in range(T):
                    ins = tr(PA[:, 0, tile(t)], Pm[:, t, :, :].rearrange("p x s -> p (x s)"), ident[:, :])
                ins.then_inc(sig("PmT_ps"), 1)
                pe.wait_ge(sig("PmT_ready"), i + 1)
                for t in range(T):
                    for b in range(2):
                        for x_ in range(2):
                            ins = mm(PA[:, 1 + x_, seq(t, b)], ctx2[S * x_:S * x_ + S, t, b, :], PmT[S * x_:S * x_ + S, t, b * S:b * S + S],
                                     start=True, stop=True)
                ins.then_inc(sig("cx_ps"), 1)
                pe.wait_ge(sig("cT2_act"), i + 1)
                pe.wait_ge(sig("cT2_dve"), i + 1)
                for t in range(T):
                    for x_ in range(2):
                        ins = mm(PA[:, 3, tile(t)], cT2[:, x_, tile(t)], wvo[:, x_, :], start=(x_ == 0), stop=(x_ == 1))
                ins.then_inc(sig("xo_ps"), 1)

                pe.wait_ge(sig("xq_ready"), i + 1)
                for t in range(T):
                    ins = tr(PA[:, 0, S * t:S * t + S].bitcast(bf16), xq[:, t, :], identb[:, :])
                ins.then_inc(sig("xqT_ps"), 1)
                pe.wait_ge(sig("xqT_ready"), i + 1)
                for t in range(T):
                    mm(PA[:, t, :], xqT[:, tile(t)], f1T[:, :], start=True, stop=True).then_inc(sig("f1_ps"), 1)
                for t in range(T):
                    pe.wait_ge(sig("gq_ready"), i * 4 + t + 1)
                    if t >= 2:
                        pe.wait_ge(sig("gqT_ready"), i * 4 + t - 1)
                    for k in range(4):
                        ins = tr(PA[:, (0, 1)[t % 2], S * k:S * k + S].bitcast(bf16), gq[:, t, k * P:k * P + P], identb[:, :])
                    ins.then_inc(sig("gqT_ps"), 1)
                for t in range(T):
                    pe.wait_ge(sig("gqT_ready"), i * 4 + t + 1)
                    for k in range(4):
                        ins = mm(PA[:, 3, tile(t)], gqT[:, t, k, :], f2T[:, k, :], start=(k == 0), stop=(k == 3))
                ins.then_inc(sig("f2_ps"), 1)

                def b_norm_T(k):
                    for t in range(T):
                        pe.wait_ge(sig("bh_ready"), (i * 3 + k) * T + t + 1)
                        ins = tr(PB[:, 0, tile(t)], bh[:, t, :], ident[:, :])
                    ins.then_inc(sig("bhT_ps"), 1)
                    pe.wait_ge(sig("bhT_ready"), i * 3 + k + 1)

                def values(src, wgt):
                    for t in range(T):
                        for b in range(2):
                            for h2 in range(2):
                                ins = mm(PB[S * h2:S * h2 + S, 3, seq(t, b)], src(t, b), wgt[:, h2, :], start=True, stop=True)
                    ins.then_inc(sig("v_ps"), 1)

                def transposes(k, what):
                    pe.wait_ge(sig("aug_lo"), i * 10 + (4, 6, 10)[k])
                    if k != 1:
                        pe.wait_ge(sig("v_ready"), i * 4 + (2 if k == 0 else 4))
                    for t in range(T):
                        for q in range(what):
                            for c_ in range(4):
                                at = 64 * (4 * q + c_)
                                ins = tr(PB[:, t, at:at + 64].bitcast(fp16),
                                         aug[:, q, t, 4 * c_:4 * c_ + 4, :].rearrange("p h s -> p (h s)"), ident16[:, :])
                        ins.then_inc(sig("augT_ps"), 1)

                def attend(k):
                    pe.wait_ge(sig("augT_ready"), (i * 3 + k) * T + T)
                    for r in range(2):
                        n_ = (i * 3 + k) * 8 + 4 * r
                        if r:
                            pe.wait_ge(sig("cx_ready"), (i * 3 + k) * T + 2)
                        for j in range(4):
                            if k < 2:
                                mm(PB[:, j, :], identb[:, :], causalb[:, :].unsqueeze(1).broadcast_to([P, 8, S]),
                                   start=True, stop=False, skip_group_check=True)
                            rows_ = slice(32 * j, 32 * j + 32)
                            for t2 in range(2):
                                for c_ in range(4):
                                    for b in range(2):
                                        at = (4 * t2 + c_) * S
                                        ins = mm(PB[S * b:S * b + S, j, at:at + S], augT[rows_, 2 * r + t2, 0, c_, S * b:S * b + S],
                                                 augT[rows_, 2 * r + t2, 1, c_, S * b:S * b + S],
                                                 start=(k == 2), stop=True, skip_group_check=True)
                            ins.then_inc(sig("s_ps"), 1)
                        for j in range(4):
                            pe.wait_ge(sig("exp_ready"), n_ + j + 1)
                            for a_ in range(4):
                                ins = tr(PB[:, j, P * a_:P * a_ + P], Pr[:, j, 2 * a_:2 * a_ + 2, :].rearrange("p h s -> p (h s)"), ident[:, :])
                            ins.then_inc(sig("pT_ps"), 1)
                        for j in range(4):
                            pe.wait_ge(sig(("PT_act", "PT_dve")[j % 2]), (i * 3 + k) * 4 + 2 * r + j // 2 + 1)
                            for t2 in range(2):
                                for cc in range(2):
                                    for b in range(2):
                                        a_ = 2 * t2 + cc
                                        ins = mm(PB[S * b:S * b + S, j, VW * a_:VW * a_ + VW], PT[:, j, a_, S * b:S * b + S],
                                                 Vx[:, 2 * (2 * r + t2) + b, 2 * j + cc, :], start=True, stop=True)
                        ins.then_inc(sig("pv_ps"), 1)

                def context_T(bank, k):
                    for t in range(T):
                        pe.wait_ge(sig("cx_ready"), (i * 3 + k) * T + t + 1)
                        if t == 0:
                            pe.wait_ge(sig("cx_ready"), (i * 3 + k) * T + T)
                        ins = tr(PB[:, bank, tile(t)], cx[:, t, :], ident[:, :])
                    ins.then_inc(sig("cxo_ps"), 1)
                    pe.wait_ge(sig("cxT_ready"), i * 3 + k + 1)

                b_norm_T(0)
                for t in range(T):
                    ins = mm(PB[:, t // 2, 256 * (t % 2):256 * (t % 2) + 256], bhT[:, tile(t)], wqkT[:, :], start=True, stop=True)
                    if t % 2:
                        ins.then_inc(sig("qk_ps"), 1)
                values(lambda t, b: bhT[:, seq(t, b)], wv_par)
                transposes(0, 2)
                attend(0)
                context_T(1, 0)
                pe.wait_ge(sig("cxT_shifted"), i * 2 + 2)
                for t in range(T):
                    for k in range(3):
                        ins = mm(PB[:, t // 2, P * (t % 2):P * (t % 2) + P], cxT[:, k, 2 * t:2 * t + 2, :].rearrange("p b s -> p (b s)"), cvT[:, k, :], start=(k == 0), stop=(k == 2))
                    if t % 2:
                        ins.then_inc(sig("qk_ps"), 1)
                transposes(1, 1)
                attend(1)
                context_T(0, 1)
                for t in range(T):
                    ins = mm(PB[:, 1, tile(t)], bhT[:, tile(t)], owT[:, :], start=True, stop=True)
                ins.then_inc(sig("o_ps"), 1)
                b_norm_T(1)
                pe.wait_ge(sig("xB_sum"), i * 2 + 1)
                for t in range(T):
                    at = 256 * (t % 2)
                    mm(PB[:, t // 2, at:at + P], bhT[:, tile(t)], ewq[:, :], start=True, stop=True)
                    ins = mm(PB[:, t // 2, at + P:at + 2 * P], ctxT[:, t, :], ewk[:, :], start=True, stop=True)
                    if t % 2:
                        ins.then_inc(sig("qk_ps"), 1)
                values(lambda t, b: ctxT[:, t, S * b:S * b + S], ewv_par)
                transposes(2, 2)
                attend(2)
                context_T(0, 2)
                for t in range(T):
                    ins = mm(PB[:, 1, tile(t)], bhT[:, tile(t)], ewo[:, :], start=True, stop=True)
                ins.then_inc(sig("o_ps"), 1)
                b_norm_T(2)
                for t in range(T):
                    ins = mm(PB[:, 3, E * t:E * t + E], bhT[:, tile(t)], gate[:, :], start=True, stop=True)
                ins.then_inc(sig("lg_ps"), 1)

                def up(e):
                    for c_ in range(2):
                        if e >= 1:
                            pe.wait_ge(sig(("hid_act", "hid_dve")[c_]), i * 8 + e)
                        mm(PB[:, c_, :], mw1[:, e, P * c_:P * c_ + P], bhT[:, :], start=True, stop=True).then_inc(sig("w1_ps"), 1)

                up(0)
                pe.wait_ge(sig("gates"), i * 11 + 11)
                for t in range(T):
                    ins = tr(PB[0:E, 2, tile(t)], cwt[:, t, :], ident[:, :])
                ins.then_inc(sig("cwT_ps"), 1)
                pe.wait_ge(sig("cwT_ready"), i + 1)
                for t in range(T):
                    ins = mm(PB[:, 3, tile(t)], cwT[:, tile(t)], mb2[:, :], start=True, stop=True)
                ins.then_inc(sig("b2_ps"), 1)
                for e in range(E):
                    if e + 1 < E:
                        up(e + 1)
                    pe.wait_ge(sig("hid_act"), i * 8 + e + 1)
                    pe.wait_ge(sig("hid_dve"), i * 8 + e + 1)
                    if e >= 1:
                        pe.wait_ge(sig("acc"), i * 8 + e)
                    for t in range(T):
                        for c_ in range(2):
                            ins = mm(PB[:, 2 + e % 2, tile(t)], hid[:, e % 2, c_, tile(t)], mw2[:, 2 * e + c_, :], start=(c_ == 0), stop=(c_ == 1))
                    ins.then_inc(sig("w2_ps"), 1)


_INS = ['x', 'ctx_1024', 'itok_BxS_0_7', 'itok_BxS_0_4092', 'mask_Bx1xSxS2_ff0', 'L0_attn_norm1_w', 'L0_attn_W_in',
        'L0_attn_conv_w', 'L0_attn_conv_b', 'L0_attn_dt_bias', 'L0_attn_A_log', 'L0_attn_D', 'L0_attn_norm_gate_w',
        'L0_attn_W_out', 'L0_attn_norm2_w', 'L0_attn_mlp_w1', 'L0_attn_mlp_b1', 'L0_attn_mlp_w2', 'L0_attn_mlp_b2',
        'L0_xattn_Wqj', 'L0_xattn_Wkj', 'L0_xattn_Wvj', 'L0_xattn_Wqi', 'L0_xattn_Wki', 'L0_xattn_Wvi', 'L0_xattn_Wout',
        'L0_xattn_gain', 'L0_xattn_council_weights', 'L0_ffn_W1', 'L0_ffn_b1', 'L0_ffn_W2', 'L0_ffn_b2',
        'L1_attn_Wqkv_w', 'L1_attn_Wqkv_b', 'L1_attn_conv_w', 'L1_attn_conv_b', 'L1_attn_out_w', 'L1_attn_out_b',
        'L1_xattn_wq', 'L1_xattn_wk', 'L1_xattn_wv', 'L1_xattn_wo', 'L1_ffn_gate_W', 'L1_ffn_W1', 'L1_ffn_b1',
        'L1_ffn_W2', 'L1_ffn_b2']


def kernel(**inputs):
    import numpy as _np
    import concourse.bacc as _bacc
    from concourse import mybir as _mybir
    from concourse.bass_utils import run_bass_kernel_spmd as _run

    nc = _bacc.Bacc("TRN2", target_bir_lowering=False, num_devices=1)
    given = {name: _np.ascontiguousarray(inputs[name]) for name in _INS}
    given["L0_xattn_gain"] = given["L0_xattn_gain"].reshape(1, 1)
    given.update(shape_constants())
    arrays, args = {}, {}
    for name, arr in given.items():
        arrays[f"in_{name}_dram"] = arr
        args[name] = nc.dram_tensor(f"in_{name}_dram", arr.shape, _mybir.dt.from_np(arr.dtype), kind="ExternalInput").ap()
    out = nc.dram_tensor("out_0_dram", (BATCH, S, D), _mybir.dt.float32, kind="ExternalOutput").ap()
    program(nc, args, out)
    r = _run(nc, [arrays], core_ids=[0])
    return r.results[0]["out_0_dram"]
```

```python
import concourse.bass as bass
from concourse import mybir
from contextlib import ExitStack
import numpy as np

fp32 = mybir.dt.float32
fp16 = mybir.dt.float16
bf16 = mybir.dt.bfloat16
i32 = mybir.dt.int32
u32 = mybir.dt.uint32
ALU = mybir.AluOpType
ACT = mybir.ActivationFunctionType
AX = mybir.AxisListType

P = 128
D = 128
S = 64
BATCH = 128
T = 4
NB = 2 * T
N = T * P
GROUPS = BATCH // NB
H = 16
HD = D // H
E = 8
F = 256
DI = 256
NH = 4
NS = 16
FF = 512
MAGIC = 12582912.0
W1_SCALE = 64.0
BIG = -1.0e30
VW = 2 * (HD + 1)


ORDER = {
    "pool": "ABAAAAABAAABABAA",
    "vector": ("AABBBBBABAAABAABBBAABBAABABBABBBBAABABBBBBBBBBBAABBAABBBBABABABABBBABABABBABAABBAAABBAAAAA"
              "BABBBABBBABABBBAABBBB"),
    "scalar": ("ABBBBBBBAAAAAAAAABBBBBBBABABBBBBBABBBBBBBABBBBBBBAAABABBBABBBBAAABBBBBBBAAABABBBBBBBAABBAB"
              "ABABAAAABABBBABAABAAAA"),
    "tensor": ("BBBBAABBBBBBABBBBAABBBBBBABABABBBBBABBBBBBABBBBABBBBBBAABABABBBBBAABAABBBBBBBBBBABABBBBBBA"
              "ABBBBBBBAABABAAABAABBBBBABABBBBBA"),
}


def shape_constants():
    p = np.arange(P)
    b, s = p // S, p % S
    t = np.arange(S)
    same = b[:, None] == b[None, :]
    return {
        "c_ident": np.eye(P, dtype=np.float32),
        "c_after": (same & (s[:, None] > s[None, :])).astype(np.float32),
        "c_upto": (s[:, None] <= t[None, :]).astype(np.float32),
        "c_seen": 0.25 * (s[:, None] <= t[None, :]).astype(np.float32),
        "c_causal": np.where(t[None, :] <= s[:, None], 0.0, BIG).astype(np.float32),
        "c_coef": np.broadcast_to((1.0 / np.arange(17, 0, -2)).astype(np.float32), (P, 9)).copy(),
        "c_iota": np.broadcast_to(t.astype(np.float32), (P, S)).copy(),
    }


def program(nc, a, out, groups=GROUPS):
    ctx = ExitStack()
    with ctx:
        def sb(name, shape, dt=fp32):
            return ctx.enter_context(nc.sbuf_tensor(name, shape, dt))

        def sem(name):
            return ctx.enter_context(nc.semaphore(name))

        PA = ctx.enter_context(nc.psum_tensor("PA", [P, 4, 512], fp32))
        PB = ctx.enter_context(nc.psum_tensor("PB", [P, 4, 512], fp32))

        ident = sb("ident", [P, P])
        ident16 = sb("ident16", [P, P], fp16)
        identb = sb("identb", [P, P], bf16)
        after = sb("after", [P, P])
        uptot = sb("uptot", [P, S])
        seen = sb("seen", [P, S])
        causal = sb("causal", [P, S])
        causalb = sb("causalb", [P, S], bf16)
        iota = sb("iota", [P, S])
        coef = sb("coef", [P, 9])
        mhalf = sb("mhalf", [P, 2 * T])
        ones = sb("ones", [P, P])

        w_in = sb("w_in", [P, 548])
        w_bc = sb("w_bc", [P, 48])
        norm1 = sb("norm1", [P, 1])
        cw_x = sb("cw_x", [P, 2, 3])
        cb_x = sb("cb_x", [P, 2])
        cw_bc = sb("cw_bc", [48, 3])
        cb_bc = sb("cb_bc", [48, 1])
        dtb = sb("dtb", [P, NH])
        alog = sb("alog", [P, NH])
        negA = sb("negA", [P, NH])
        dskip = sb("dskip", [P, 2])
        ngate = sb("ngate", [P, 2])
        w_out = sb("w_out", [P, 2, D])
        norm2 = sb("norm2", [P, 1])
        w1m = sb("w1m", [P, FF])
        b1m = sb("b1m", [P, 4])
        w2m = sb("w2m", [P, 4, D])
        b2m = sb("b2m", [P, D])

        wqk = sb("wqk", [P, 2, P])
        wvo = sb("wvo", [P, 2, P])
        woutT = sb("woutT", [P, P])
        gain = sb("gain", [P, 1])
        council = sb("council", [P, 2])
        csum = sb("csum", [P, 4])

        f1T = sb("f1T", [P, FF], bf16)
        f2T = sb("f2T", [P, 4, D], bf16)
        fb1 = sb("fb1", [P, FF])
        fb2 = sb("fb2", [P, D])
        fabs = sb("fabs", [P, 2])
        fscale = sb("fscale", [P, 2])
        finv = sb("finv", [P, 2])
        fs127 = sb("fs127", [P, 2])

        wqkT = sb("wqkT", [P, 2 * D])
        qkb = sb("qkb", [P, 2 * D])
        vb = sb("vb", [P, D])
        wvT = sb("wvT", [P, D])
        wv_par = sb("wv_par", [P, 2, S])
        vb_par = sb("vb_par", [P, S])
        cvT = sb("cvT", [P, 3, D])
        cvb = sb("cvb", [P, D])
        owT = sb("owT", [P, D])
        ob = sb("ob", [P, D])
        ewq = sb("ewq", [P, D])
        ewk = sb("ewk", [P, D])
        ewv = sb("ewv", [P, D])
        ewv_par = sb("ewv_par", [P, 2, S])
        ewo = sb("ewo", [P, D])

        gate = sb("gate", [P, E])
        mw1h = sb("mw1h", [P, E, F], fp16)
        mw1l = sb("mw1l", [P, E, F], fp16)
        mb1 = sb("mb1", [P, 2 * E])
        mw2 = sb("mw2", [P, 2 * E, D])
        mb2 = sb("mb2", [E, D])

        room = {k: sb("room_" + k, [P, 2048]) for k in ("seg", "mix", "gate", "chan", "prob", "turn", "hidden")}

        def part(k, at, shape, dt=fp32):
            count = int(np.prod(shape))
            words = count // (1 if dt == fp32 else 2)
            assert at + words <= 2048
            ap = room[k][:, at:at + words]
            if dt != fp32:
                ap = ap.bitcast(dt)
            if len(shape) == 1:
                return ap
            names = "abcd"[:len(shape)]
            return ap.rearrange(f"p ({' '.join(names)}) -> p {' '.join(names)}", **dict(zip(names[1:], shape[1:])))

        f1 = part("hidden", 0, [4, D])
        f2 = part("hidden", 512, [FF])
        f1q = part("hidden", 1024, [4, D], bf16)
        f2q = part("hidden", 1280, [FF], bf16)
        xw = part("prob", 0, [7, P])
        aw = part("prob", 896, [3, D])
        cvw = part("prob", 1280, [3 * D])
        oww = part("prob", 1664, [D])
        owp = part("prob", 1792, [D])
        cvp = part("turn", 0, [3, D])
        mw1 = part("seg", 0, [E, F])
        G = part("seg", 0, [T, NH, S])
        dec = part("seg", 1024, [T, NH, S])
        hb = part("seg", 0, [T, FF])
        xdt = part("mix", 0, [T, NH, S])
        M = part("mix", 1024, [T, NH, S])
        Vc = part("mix", 0, [NB, D])
        g32 = part("mix", 0, [T, FF])
        zs = part("gate", 0, [2, N])
        gsq = part("gate", 1024, [2, N])
        hs = part("gate", 0, [4, N])
        y2 = part("chan", 0, [2, N])
        xc = part("chan", 1024, [2, N])
        gq = part("chan", 0, [T, FF], bf16)
        gqT = part("chan", 1024, [T, 4, P], bf16)
        Pr = part("prob", 0, [4, 2 * 4, S])
        PT = part("turn", 0, [4, 2 * 2, P])
        hid = part("hidden", 0, [2, 2, N])

        xin = sb("xin", [P, T, D])
        ctxn = sb("ctxn", [P, T, D])
        idsb = sb("idsb", [P, T, S], i32)
        ptr = sb("ptr", [P, T], i32)
        mark = sb("mark", [1, 1])
        st = sb("st", [P, T, 6])
        mv = sb("mv", [P, T, 2])
        var = sb("var", [P, T, 2])
        msq = sb("msq", [P, T])
        rs = sb("rs", [P, T, 2])
        h = sb("h", [P, T, D])
        u = sb("u", [P, T, D])
        hT = sb("hT", [P, N])
        bcc = sb("bcc", [48, N])
        bT = sb("bT", [NS, N])
        cT = sb("cT", [NS, N])
        dv = sb("dv", [P, T * NH])
        dn = sb("dn", [P, T * NH])
        du = sb("du", [P, T * NH])
        dw = sb("dw", [P, T * NH])
        dr = sb("dr", [P, T * NH])
        dz = sb("dz", [P, T * NH])
        dq = sb("dq", [P, T * NH])
        dp = sb("dp", [P, T * NH])
        dtt = sb("dtt", [P, T, NH])
        aa = sb("aa", [P, T, NH])
        cbm = sb("cbm", [P, T, S])
        rg = sb("rg", [P, T])
        rgi = sb("rgi", [P, T])
        x1 = sb("x1", [P, T, D])
        xb = sb("xb", [P, T, D])
        xA = sb("xA", [P, T, D])
        ctxT = sb("ctxT", [P, T, P])
        pf = sb("pf", [P, T, 3])
        O = sb("O", [P, T, 3, S])
        qx = sb("qx", [P, 2, N])
        prod = sb("prod", [P, 2, T, 3, S])
        sc = sb("sc", [P, 2, T, 3])
        rid = sb("rid", [P, T])
        rprod = sb("rprod", [P, T, S])
        R = sb("R", [P, T, 6])
        V6 = sb("V6", [P, T, 6])
        smx = sb("smx", [P, 2 * T])
        ssm = sb("ssm", [P, 2 * T])
        Pm = sb("Pm", [P, T, 2, S])
        PmT = sb("PmT", [P, T, P])
        amx = sb("amx", [P, T])
        ainv = sb("ainv", [P, T])
        asc = sb("asc", [P, T])
        t32 = sb("t32", [P, T, D])
        xq = sb("xq", [P, T, D], bf16)
        xqT = sb("xqT", [P, N], bf16)

        xB = sb("xB", [P, T, D])
        xo = sb("xo", [P, T, D])
        ctxTB = sb("ctxTB", [P, T, P])
        maskE = sb("maskE", [P, T, S])
        bst = sb("bst", [P, T, 6])
        bmv = sb("bmv", [P, T, 2])
        bvar = sb("bvar", [P, T])
        brs = sb("brs", [P, T])
        bh = sb("bh", [P, T, D])
        bhT = sb("bhT", [P, N])
        bhh = sb("bhh", [P, N], fp16)
        bhl = sb("bhl", [P, N], fp16)
        qk32 = sb("qk32", [P, T, 2, D])
        aug = sb("aug", [P, 2, T, H, 32], fp16)
        augT = sb("augT", [P, T, 2, 4, P], fp16)
        Vx = sb("Vx", [P, NB, E, VW])
        mx = sb("mx", [P, 4, 2 * 4])
        rc = sb("rc", [P, 4, 2 * 4])
        cx = sb("cx", [P, T, D])
        cxT = sb("cxT", [P, 3, NB, S])
        lg = sb("lg", [P, T, E])
        m8 = sb("m8", [P, T, E])
        ix8 = sb("ix8", [P, T, E], u32)
        ixf = sb("ixf", [P, T, 2])
        e8 = sb("e8", [P, T, E])
        s8 = sb("s8", [P, T])
        r8 = sb("r8", [P, T])
        g2 = sb("g2", [P, T, 2])
        d2 = sb("d2", [P, T])
        cw2 = sb("cw2", [P, T, 2])
        oh = sb("oh", [P, T, 2, E])
        cwt = sb("cwt", [P, T, E])
        cwT = sb("cwT", [E, N])
        acc = sb("acc", [P, T, D])

        s = {}

        def sig(name):
            if name not in s:
                s[name] = sem(name)
            return s[name]

        def first(i):
            return isinstance(i, int) and i == 0

        def interleave(order, chain_a, chain_b):
            chains = {"A": chain_a, "B": chain_b}
            for chain in chains.values():
                next(chain)
            for which in order:
                next(chains[which], None)

        def alone(chain):
            for _ in chain:
                pass

        block = ctx.enter_context(nc.Block())

        x_v = a["x"].rearrange("(g t b) s d -> g (b s) t d", t=T, b=2)
        out_v = out.rearrange("(g t b) s d -> g (b s) t d", t=T, b=2)
        c_v = a["ctx_1024"].rearrange("(g t b) s d -> g (b s) t d", t=T, b=2)
        m_v = a["mask_Bx1xSxS2_ff0"].rearrange("(g t b) o s l -> g (b s) t (o l)", t=T, b=2)
        p_v = a["itok_BxS_0_4092"].rearrange("(g t b) s -> g (b s) t", t=T, b=2)
        i_v = a["itok_BxS_0_7"].rearrange("(g t b) s -> g b t s", t=T, b=2)

        def row(ap, n=P):
            return ap.rearrange("(o k) -> o k", o=1).broadcast_to([n, ap.shape[0]])

        FIRST = []
        LOADS = []
        PADDED = []

        def load(dst, src, to=LOADS):
            to.append((dst, src))

        W = lambda k: a[k]
        load(ident[:, :], W("c_ident"), FIRST)
        load(after[:, :], W("c_after"))
        load(uptot[:, :], W("c_upto"))
        load(seen[:, :], W("c_seen"))
        load(causal[:, :], W("c_causal"), FIRST)
        load(iota[:, :], W("c_iota"))
        load(coef[:, :], W("c_coef"))
        load(w_in[:, :], W("L0_attn_W_in"), FIRST)
        load(norm1[:, :], W("L0_attn_norm1_w").rearrange("(k o) -> k o", o=1), FIRST)
        load(cw_x[:, :, :], W("L0_attn_conv_w")[0:DI, :].rearrange("(c k) w -> k c w", c=2))
        load(cb_x[:, :], W("L0_attn_conv_b")[0:DI].rearrange("(c k) -> k c", c=2))
        load(cw_bc[0:NS, :], W("L0_attn_conv_w")[DI:DI + NS, :], PADDED)
        load(cw_bc[32:32 + NS, :], W("L0_attn_conv_w")[DI + NS:DI + 2 * NS, :], PADDED)
        load(cb_bc[0:NS, :], W("L0_attn_conv_b")[DI:DI + NS].rearrange("(k o) -> k o", o=1), PADDED)
        load(cb_bc[32:32 + NS, :], W("L0_attn_conv_b")[DI + NS:DI + 2 * NS].rearrange("(k o) -> k o", o=1), PADDED)
        load(dtb[:, :], row(W("L0_attn_dt_bias")))
        load(alog[:, :], row(W("L0_attn_A_log")))
        for hh in range(NH):
            load(dskip[S * (hh % 2):S * (hh % 2) + S, hh // 2:hh // 2 + 1], row(W("L0_attn_D")[hh:hh + 1], S), PADDED)
        load(ngate[:, :], W("L0_attn_norm_gate_w").rearrange("(c k) -> k c", c=2), FIRST)
        load(w_out[:, :, :], W("L0_attn_W_out").rearrange("(c k) d -> k c d", c=2), FIRST)
        load(norm2[:, :], W("L0_attn_norm2_w").rearrange("(k o) -> k o", o=1), FIRST)
        load(w1m[:, :], W("L0_attn_mlp_w1"), FIRST)
        load(b1m[:, :], W("L0_attn_mlp_b1").rearrange("(c k) -> k c", c=4))
        load(w2m[:, :, :], W("L0_attn_mlp_w2").rearrange("(c k) d -> k c d", c=4))
        load(b2m[:, :], row(W("L0_attn_mlp_b2")))
        for n_, k in enumerate(("Wqj", "Wkj", "Wvj", "Wqi", "Wki", "Wvi", "Wout")):
            load(xw[:, n_, :], W("L0_xattn_" + k))
        load(gain[:, :], W("L0_xattn_gain").broadcast_to([P, 1]))
        load(council[:, :], row(W("L0_xattn_council_weights")))
        load(f1[:, :, :], W("L0_ffn_W1").rearrange("(c k) d -> k c d", c=4))
        load(f2[:, :], W("L0_ffn_W2"))
        load(fb1[:, :], row(W("L0_ffn_b1")))
        load(fb2[:, :], row(W("L0_ffn_b2")))
        load(aw[:, :, :], W("L1_attn_Wqkv_w").rearrange("(c k) d -> k c d", c=3))
        load(qkb[:, :], row(W("L1_attn_Wqkv_b")[0:2 * D]))
        load(vb[:, :], row(W("L1_attn_Wqkv_b")[2 * D:3 * D]))
        load(cvw[:, :], W("L1_attn_conv_w").rearrange("o i k -> o (i k)"))
        load(cvb[:, :], row(W("L1_attn_conv_b")))
        load(oww[:, :], W("L1_attn_out_w"))
        load(ob[:, :], row(W("L1_attn_out_b")))
        load(ewq[:, :], W("L1_xattn_wq").rearrange("i n d -> i (n d)"))
        load(ewk[:, :], W("L1_xattn_wk").rearrange("i n d -> i (n d)"))
        load(ewv[:, :], W("L1_xattn_wv").rearrange("i n d -> i (n d)"))
        wo_v = W("L1_xattn_wo").rearrange("(cc h2 j) d m -> j cc h2 d m", cc=2, h2=2)
        for j in range(4):
            for cc in range(2):
                for h2 in range(2):
                    at = ((j * 2 + cc) * 2 + h2) * HD
                    load(ewo[at:at + HD, :], wo_v[j, cc, h2], PADDED)
        load(gate[:, :], W("L1_ffn_gate_W"))
        load(mw1[:, :, :], W("L1_ffn_W1").rearrange("e k f -> k e f"), FIRST)
        load(mb1[:, :], W("L1_ffn_b1").rearrange("e (c k) -> k (e c)", c=2), FIRST)
        load(mw2[:, :, :], W("L1_ffn_W2").rearrange("e (c k) d -> k (e c) d", c=2), FIRST)
        load(mb2[:, :], W("L1_ffn_b2"))
        NLOADS = len(LOADS)

        @block.sync
        def _(sp):
            for dst, src in FIRST[::2]:
                sp.dma_start(dst, src, allow_slow_non_contiguous=True).then_inc(sig("first_loaded"), 16)
            for dst, src in LOADS[::2]:
                sp.dma_start(dst, src, allow_slow_non_contiguous=True).then_inc(sig("weights_loaded"), 16)

            def loads(i):
                if not first(i):
                    sp.wait_ge(sig("u_ready"), i * T)
                    sp.wait_ge(sig("xb_ready"), i)
                sp.dma_start(xin[:, :, :], x_v[i]).then_inc(sig("x_loaded"), 16)
                if not first(i):
                    sp.wait_ge(sig("ids_free"), i)
                for b in range(2):
                    sp.dma_start(idsb[S * b:S * b + S, :, :],
                                 i_v[i, b:b + 1].broadcast_to([S, T, S])).then_inc(sig("ids_loaded"), 16)
                if not first(i):
                    sp.wait_ge(sig("pf"), i * 4)
                sp.dma_start(ptr[:, :], p_v[i], allow_slow_non_contiguous=True).then_inc(sig("ptr_loaded"), 16)
                if not first(i):
                    sp.wait_ge(sig("cxT_ps"), i)
                sp.dma_start(ctxn[:, :, :], c_v[i]).then_inc(sig("ctx_loaded"), 16)

            def mask(i):
                if not first(i):
                    sp.wait_ge(sig("s_biased"), i * 8)
                sp.dma_start(maskE[:, :, :], m_v[i]).then_inc(sig("mask_loaded"), 16)

            def store(i):
                sp.wait_ge(sig("out_ready"), (i + 1) * T)
                sp.dma_start(out_v[i], acc[:, :, :]).then_inc(sig("stored"), 16)

            loads(0)
            mask(0)
            loads(1)
            with sp.Fori(2, groups) as i:
                mask(i - 1)
                loads(i)
                store(i - 2)
            mask(groups - 1)
            store(groups - 2)
            store(groups - 1)
            sp.wait_ge(sig("stored"), 16 * groups)

        @block.gpsimd
        def _(pool):
            pool.memset(cw_bc[:, :], 0.0).then_inc(sig("preset"), 1)
            pool.memset(cb_bc[:, :], 0.0).then_inc(sig("preset"), 1)
            pool.memset(mhalf[:, :], -0.5).then_inc(sig("preset"), 1)
            pool.memset(ones[:, :], 1.0).then_inc(sig("preset"), 1)
            pool.memset(w_bc[:, :], 0.0).then_inc(sig("preset"), 1)
            pool.memset(aug[:, :, :, :, :], 0.0).then_inc(sig("preset"), 1)
            pool.memset(cxT[:, :, :, :], 0.0).then_inc(sig("preset"), 1)
            pool.memset(Vx[:, :, :, :], 0.0).then_inc(sig("preset"), 1)
            pool.wait_ge(sig("preset"), 8)
            pool.memset(Vx[0:S, :, :, HD:HD + 1], 1.0).then_inc(sig("preset"), 1)
            pool.memset(Vx[S:P, :, :, VW - 1:VW], 1.0).then_inc(sig("preset"), 1)
            for dst, src in PADDED:
                pool.dma_start(dst, src, allow_slow_non_contiguous=True).then_inc(sig("padded_loaded"), 16)
            pool.wait_ge(sig("setup_done"), 3)

            def rsqrt(dst, src, wait, value, done):
                pool.wait_ge(sig(wait), value)
                k = dst.shape[1]
                pool.tensor_tensor(dst, src, mhalf[:, 0:k], ALU.pow).then_inc(sig(done), 1)

            def chain_a(i):
                yield "A00"
                rsqrt(rs[:, :, :].rearrange("p t k -> p (t k)"), var[:, :, :].rearrange("p t k -> p (t k)"),
                      "ln_var", i * 5 + 2, "ln_rstd")
                yield "A03"
                pool.wait_ge(sig("x_loaded"), i * 16 + 16)
                if not first(i):
                    pool.wait_ge(sig("xA_ready"), i)
                pool.tensor_tensor(xb[:, :, :], xin[:, :, :], b2m[:, :].unsqueeze(1).broadcast_to([P, T, D]),
                                   ALU.add).then_inc(sig("xb_ready"), 1)
                yield "A07"
                pool.wait_ge(sig("dt_z"), i * 2 + 1)
                pool.tensor_tensor(dq[:, :], dz[:, :], dz[:, :], ALU.mult).then_inc(sig("dt_poly"), 1)
                for k in range(9):
                    if k:
                        pool.wait_ge(sig("dt_poly"), i * 18 + 2 * k)
                        pool.tensor_tensor(dp[:, :], dp[:, :], coef[:, k:k + 1].broadcast_to([P, T * NH]),
                                           ALU.add).then_inc(sig("dt_poly"), 1)
                    pool.wait_ge(sig("dt_poly"), i * 18 + 2 * k + 1)
                    if k:
                        pool.tensor_tensor(dp[:, :], dp[:, :], (dz if k == 8 else dq)[:, :], ALU.mult).then_inc(sig("dt_poly"), 1)
                    else:
                        pool.tensor_tensor(dp[:, :], dq[:, :], coef[:, 0:1].broadcast_to([P, T * NH]),
                                           ALU.mult).then_inc(sig("dt_poly"), 1)
                yield "A08"
                pool.wait_ge(sig("a_ready"), i + 1)
                for t in range(T):
                    pool.tensor_tensor(G[:, t, :, :], aa[:, t, :].unsqueeze(2).broadcast_to([P, NH, S]),
                                       uptot[:, :].unsqueeze(1).broadcast_to([P, NH, S]),
                                       ALU.mult).then_inc(sig("G_ready"), 1)
                yield "A12"
                rsqrt(rg[:, :], rgi[:, :], "gate_var", i + 1, "gate_rstd")
                yield "A13"
                rsqrt(rs[:, :, 0], var[:, :, 0], "ln_var", i * 5 + 3, "ln_rstd")
                yield "A17"
                rsqrt(rs[:, :, 0], var[:, :, 0], "ln_var", i * 5 + 4, "ln_rstd")
                yield "A23"
                for x_ in range(2):
                    pool.wait_ge(sig("sm"), i * 6 + 6)
                    for t in range(T):
                        pool.tensor_tensor(prod[:, x_, t, :, :], O[:, t, :, :],
                                           sc[:, x_, t, :].unsqueeze(2).broadcast_to([P, 3, S]),
                                           ALU.mult).then_inc(sig("OW_ready"), 1)
                yield "A27"
                rsqrt(rs[:, :, 0], var[:, :, 0], "ln_var", i * 5 + 5, "ln_rstd")
                yield "A28"
                pool.wait_ge(sig("x2_ready"), i + 1)
                pool.tensor_tensor(xb[:, :, :], xA[:, :, :], fb2[:, :].unsqueeze(1).broadcast_to([P, T, D]),
                                   ALU.add).then_inc(sig("xb2_ready"), 1)
                yield "A32"
                if not first(i):
                    pool.wait_ge(sig("v_ps"), i * 2)
                pool.wait_ge(sig("ctxT_ready"), i + 1)
                pool.tensor_tensor(ctxTB[:, :, :], ctxT[:, :, :], ones[:, :].unsqueeze(1).broadcast_to([P, T, P]),
                                   ALU.mult).then_inc(sig("ctxTB_ready"), 1)

                yield "B00"
                rsqrt(brs[:, :], bvar[:, :], "bln_var", i * 3 + 1, "bln_rstd")

            def chain_b(i):
                yield "B04"
                if not first(i):
                    pool.wait_ge(sig("acc"), i * E)
                pool.wait_ge(sig("xB_part"), i * 4 + 4)
                pool.tensor_tensor(xo[:, :, :], xB[:, :, :], ob[:, :].unsqueeze(1).broadcast_to([P, T, D]),
                                   ALU.add).then_inc(sig("xo_ready"), 1)
                yield "B20"
                rsqrt(brs[:, :], bvar[:, :], "bln_var", i * 3 + 2, "bln_rstd")
                yield "E00"
                rsqrt(brs[:, :], bvar[:, :], "bln_var", i * 3 + 3, "bln_rstd")
                yield "E01"
                pool.wait_ge(sig("bh_ready"), (i * 3 + 3) * T)
                pool.tensor_tensor(xo[:, :, :], xB[:, :, :], bh[:, :, :], ALU.add).then_inc(sig("xh_ready"), 1)

            alone(chain_a(0))
            with pool.Fori(1, groups) as i:
                interleave(ORDER["pool"], chain_a(i), chain_b(i - 1))
            alone(chain_b(groups - 1))

        @block.vector
        def _(v):
            v.wait_ge(sig("first_loaded"), 16 * len(FIRST))
            v.wait_ge(sig("preset"), 10)
            c = [0]

            def link(ins):
                c[0] += 1
                ins.then_inc(sig("v_setup"), 1)
                v.wait_ge(sig("v_setup"), c[0])

            def par(o, i_):
                for h2 in range(2):
                    for j in range(4):
                        v.tensor_copy(o(h2).rearrange("p (j cc d) -> p j cc d", j=4, cc=2)[:, j],
                                      i_(h2).rearrange("p (cc h j d) -> p h j cc d", cc=2, h=2, j=4)[:, h2, j])

            v.tensor_copy(ident16[:, :], ident[:, :])
            v.tensor_scalar(mb1[:, :], mb1[:, :], W1_SCALE, None, ALU.mult)
            v.tensor_scalar(mw2[:, :, :], mw2[:, :, :], 1.0 / W1_SCALE, None, ALU.mult)
            link(v.tensor_scalar(mw1[:, :, :], mw1[:, :, :], W1_SCALE, None, ALU.mult))
            link(v.tensor_copy(mw1h[:, :, :], mw1[:, :, :]))
            v.tensor_tensor(mw1l[:, :, :], mw1[:, :, :], mw1h[:, :, :], ALU.subtract)
            v.tensor_copy(identb[:, :], ident[:, :])
            v.tensor_copy(causalb[:, :], causal[:, :])
            link(v.tensor_scalar(w_in[:, :], w_in[:, :], norm1[:, :], None, ALU.mult))
            v.tensor_copy(w_bc[:, 0:NS], w_in[:, 2 * DI:2 * DI + NS])
            v.tensor_copy(w_bc[:, 32:32 + NS], w_in[:, 2 * DI + NS:2 * DI + 2 * NS])
            for k in range(2):
                v.tensor_scalar(w_out[:, k, :], w_out[:, k, :], ngate[:, k:k + 1], None, ALU.mult)
            link(v.tensor_scalar(w1m[:, :], w1m[:, :], norm2[:, :], None, ALU.mult))
            v.wait_ge(sig("weights_loaded"), 16 * NLOADS)
            v.wait_ge(sig("padded_loaded"), 16 * len(PADDED))
            link(v.tensor_reduce(fabs[:, 0:1], f1[:, :, :], AX.XY, ALU.add, apply_absolute_value=True))
            v.tensor_reduce(fabs[:, 1:2], f2[:, :], AX.X, ALU.add, apply_absolute_value=True).then_inc(sig("dve_setup"), 1)
            v.tensor_scalar(ewq[:, :], ewq[:, :], HD ** -0.5, None, ALU.mult)
            v.tensor_scalar(qkb[:, 0:D], qkb[:, 0:D], HD ** -0.5, None, ALU.mult)
            v.tensor_scalar(cvb[:, :], cvb[:, :], HD ** -0.5, None, ALU.mult)
            v.tensor_reduce(csum[:, 0:1], council[:, :], AX.X, ALU.max)
            for k in range(3):
                for j in range(4):
                    v.tensor_copy(cvp[:, k, 32 * j:32 * j + 32].rearrange("p (a d) -> p a d", d=HD),
                                  cvw[:, :].rearrange("p (a j d k) -> p k j a d", a=4, j=4, k=3)[:, k, j])
            for j in range(4):
                v.tensor_copy(owp[:, 32 * j:32 * j + 32].rearrange("p (a d) -> p a d", d=HD),
                              oww[:, :].rearrange("p (a j d) -> p j a d", a=4, j=4)[:, j])
            par(lambda h2: ewv_par[:, h2, :], lambda h2: ewv[:, :])
            link(v.tensor_copy(csum[:, 1:2], gain[:, :]))
            link(v.tensor_scalar(council[:, :], council[:, :], csum[:, 0:1], None, ALU.subtract))
            for h2 in range(2):
                for j in range(4):
                    v.tensor_copy(vb_par[S * h2:S * h2 + S, :].rearrange("p (j cc d) -> p j cc d", j=4, cc=2)[:, j],
                                  vb[S * h2:S * h2 + S, :].rearrange("p (cc h j d) -> p h j cc d", cc=2, h=2, j=4)[:, h2, j])
            v.memset(R[:, :, :], 0.0).then_inc(sig("dve_setup"), 1)
            v.wait_ge(sig("pe_setup"), 1)
            link(v.tensor_scalar(fscale[:, :], PA[:, 0, 0:2], 1.0 / (FF * D), 1e-5, ALU.mult, ALU.max))
            link(v.reciprocal(finv[:, :], fscale[:, :]))
            v.tensor_scalar(fs127[:, :], fscale[:, :], 1.0 / 127.0, None, ALU.mult)
            f1f = f1[:, :, :].rearrange("p c d -> p (c d)")
            f1qf = f1q[:, :, :].rearrange("p c d -> p (c d)")
            for wgt, qd, k in ((f1f, f1qf, 0), (f2[:, :], f2q[:, :], 1)):
                link(v.tensor_scalar(wgt, wgt, finv[:, k:k + 1], MAGIC, ALU.mult, ALU.add))
                link(v.tensor_scalar(wgt, wgt, MAGIC, 1.0, ALU.subtract, ALU.min))
                link(v.tensor_scalar(qd, wgt, -1.0, None, ALU.max))
            v.wait_ge(sig("act_setup"), 2)
            link(v.tensor_reduce(csum[:, 2:3], council[:, :], AX.X, ALU.add))
            link(v.reciprocal(csum[:, 3:4], csum[:, 2:3]))
            link(v.tensor_scalar(council[:, :], council[:, :], csum[:, 3:4], csum[:, 1:2], ALU.mult, ALU.mult))
            v.wait_ge(sig("act_setup"), 1)
            link(v.tensor_scalar(negA[:, :], negA[:, :], -1.0, None, ALU.mult))
            v.memset(dz[:, :], 0.0).then_inc(sig("dve_setup"), 1)
            v.wait_ge(sig("pe_setup"), 2)
            v.tensor_copy(woutT[:, :], PA[:, 1, 0:P])
            v.tensor_scalar(wqk[:, :, :], PA[:, 1, 128:384].rearrange("p (a b) -> p a b", a=2), float(D) ** -0.5, None, ALU.mult)
            v.tensor_scalar(wqkT[:, 0:D], PA[:, 2, 0:D], HD ** -0.5, None, ALU.mult)
            v.tensor_copy(wqkT[:, D:2 * D], PA[:, 2, D:2 * D])
            v.tensor_copy(owT[:, :], PA[:, 2, 384:512])
            v.tensor_scalar(cvT[:, :, :], PA[:, 3, 0:384].rearrange("p (a b) -> p a b", a=3), HD ** -0.5, None, ALU.mult)
            link(v.tensor_copy(wvT[:, :], PA[:, 2, 256:384]))
            par(lambda h2: wv_par[:, h2, :], lambda h2: wvT[:, :])
            v.tensor_copy(f1T[:, :], PB[:, 0, 0:256].bitcast(bf16))
            v.tensor_copy(f2T[:, :, :].rearrange("p a b -> p (a b)"), PB[:, 1, 0:256].bitcast(bf16))
            v.tensor_copy(dw[:, :], dz[:, :]).then_inc(sig("dve_setup"), 1)
            v.wait_ge(sig("pe_setup"), 3)
            for x_ in range(2):
                v.tensor_scalar(wvo[:, x_, :], PA[:, 0, x_ * P:x_ * P + P], council[:, x_:x_ + 1], None, ALU.mult)
            v.tensor_copy(dw[:, :], dz[:, :]).then_inc(sig("setup_done"), 3)
            v.wait_ge(sig("setup_done"), 3)

            def stats(src, i_st, i_mv, stat, mean, s_st, s_mv):
                for t in range(T):
                    v.bn_stats(stat[:, t, :], src[:, t, :]).then_inc(sig(s_st), 1)
                v.wait_ge(sig(s_st), i_st + T)
                v.memset(mark[:, :], 0.0)
                for t in range(T):
                    v.bn_aggr(mean[:, t, :], stat[:, t, :]).then_inc(sig(s_mv), 1)
                v.wait_ge(sig(s_mv), i_mv + T)

            def norm(i, k):
                yield ("B00", "B20", "E00")[k]
                if k == 0:
                    v.wait_ge(sig("xB_part"), i * 4 + 4)
                stats(xB, (i * 3 + k) * T, (i * 3 + k) * T, bst, bmv, "bln_stat", "bln_mean")
                v.tensor_scalar(bvar[:, :], bmv[:, :, 1], 1e-5, None, ALU.add).then_inc(sig("bln_var"), 1)
                yield ("B01", "B21", "E01")[k]
                v.wait_ge(sig("bln_rstd"), i * 3 + k + 1)
                for t in range(T):
                    v.tensor_scalar(bh[:, t, :], xB[:, t, :], bmv[:, t, 0:1], brs[:, t:t + 1], ALU.subtract,
                                    ALU.mult).then_inc(sig("bh_ready"), 1)

            def queries_keys(i, k, what, bias, ps):
                yield f"B{k}2"
                for r in range(2):
                    v.wait_ge(sig("qk_ps"), i * 6 + 2 * k + r + 1)
                    if what == 2:
                        src = ps[:, r, :].rearrange("p (t q d) -> p t q d", t=2, q=2)
                        dst = qk32[:, 2 * r:2 * r + 2, :, :]
                        if bias is None:
                            v.tensor_copy(dst, src).then_inc(sig("qk32"), 1)
                        else:
                            v.tensor_tensor(dst.rearrange("p t q d -> p t (q d)"), src.rearrange("p t q d -> p t (q d)"),
                                            bias.unsqueeze(1).broadcast_to([P, 2, 2 * D]), ALU.add).then_inc(sig("qk32"), 1)
                    else:
                        v.tensor_tensor(qk32[:, 2 * r:2 * r + 2, 0, :], ps[:, r, 0:256].rearrange("p (t d) -> p t d", t=2),
                                        bias.unsqueeze(1).broadcast_to([P, 2, D]), ALU.add).then_inc(sig("qk32"), 1)
                yield f"B{k}3"
                for r in range(2):
                    for q in range(2):
                        if what == 1 and q == 1:
                            continue
                        v.wait_ge(sig("aug_hi"), (i * 10 + (0, 4, 6)[k]) + (2 * r + q + 1 if what == 2 else r + 1))
                        slot = 16 if q == 0 else 8
                        lo = aug[:, q, 2 * r:2 * r + 2, :, slot:slot + HD]
                        hi = aug[:, q, 2 * r:2 * r + 2, :, 0:HD]
                        v.tensor_tensor(lo, qk32[:, 2 * r:2 * r + 2, q, :].rearrange("p t (h d) -> p t h d", h=H), hi,
                                        ALU.subtract).then_inc(sig("aug_lo"), 1)

            def values(i, k, bias, ps):
                v.wait_ge(sig("v_ps"), i * 2 + k + 1)
                for h2 in range(2):
                    rows_ = slice(S * h2, S * h2 + S)
                    dst = Vx[rows_, :, :, 9 * h2:9 * h2 + HD]
                    src = ps[rows_, 3, :].rearrange("p (b u d) -> p b u d", b=NB, u=8)
                    if bias is None:
                        v.tensor_copy(dst, src).then_inc(sig("v_ready"), 1)
                    else:
                        bb = bias[rows_, :].rearrange("p (u d) -> p u d", u=8).unsqueeze(1).broadcast_to([S, NB, 8, HD])
                        v.tensor_tensor(dst, src, bb, ALU.add).then_inc(sig("v_ready"), 1)

            def chain_a(i):
                yield "A00"
                v.wait_ge(sig("x_loaded"), i * 16 + 16)
                stats(xin, i * 16, i * 16, st, mv, "ln_stat", "ln_mean")
                v.tensor_scalar(var[:, :, 0], mv[:, :, 1], 1e-5, None, ALU.add).then_inc(sig("ln_var"), 1)
                v.tensor_scalar(var[:, :, 1], mv[:, :, 1], 1.0 + 1e-6, 1e-11, ALU.mult, ALU.add).then_inc(sig("ln_var"), 1)
                yield "A02"
                v.wait_ge(sig("ln_rstd"), i * 4 + 1)
                for t in range(T):
                    v.tensor_scalar(h[:, t, :], xin[:, t, :], mv[:, t, 0:1], rs[:, t, 1:2], ALU.subtract,
                                    ALU.mult).then_inc(sig("h_ready"), 1)
                yield "A03"
                for t in range(T):
                    v.tensor_scalar(u[:, t, :], xin[:, t, :], mv[:, t, 0:1], rs[:, t, 0:1], ALU.subtract,
                                    ALU.mult).then_inc(sig("u_ready"), 1)
                yield "A04"
                for c_ in range(3):
                    if c_:
                        yield "A04"
                    src = (PA[:, 2, :], PA[:, 0, :], PA[0:48, 1, :])[c_].rearrange("p (b s) -> p b s", b=NB)
                    dst = (xc[:, 0, :], xc[:, 1, :], bcc[:, :])[c_].rearrange("p (b s) -> p b s", b=NB)
                    for k in (1, 0):
                        tap = (cw_x[:, 0, k:k + 1], cw_x[:, 1, k:k + 1], cw_bc[:, k:k + 1])[c_]
                        lag = 2 - k
                        if k == 1:
                            v.wait_ge(sig("conv_tap"), i * 3 + c_ + 1)
                        else:
                            v.wait_ge(sig("conv_done"), i * 6 + 2 * c_ + 1)
                        v.scalar_tensor_tensor(dst[:, :, lag:S], src[:, :, 0:S - lag], tap, dst[:, :, lag:S],
                                               ALU.mult, ALU.add).then_inc(sig("conv_done"), 1)
                yield "A05"
                v.wait_ge(sig("dt_ps"), i + 1)
                v.tensor_tensor(dv[:, :].rearrange("p (t k) -> p t k", k=NH), PA[:, 3, 0:T * NH].rearrange("p (t k) -> p t k", k=NH),
                                dtb[:, :].unsqueeze(1).broadcast_to([P, T, NH]), ALU.add).then_inc(sig("dt_v"), 1)
                v.wait_ge(sig("dt_v"), i + 1)
                v.scalar_tensor_tensor(dn[:, :], dv[:, :], -1.0, dv[:, :], ALU.mult, ALU.min).then_inc(sig("dt_n"), 1)
                yield "A06"
                v.wait_ge(sig("dt_u"), i + 1)
                v.tensor_scalar(dw[:, :], du[:, :], 2.0, None, ALU.add).then_inc(sig("dt_w"), 1)
                v.wait_ge(sig("dt_w"), i * 2 + 1)
                v.reciprocal(dr[:, :], dw[:, :]).then_inc(sig("dt_w"), 1)
                v.wait_ge(sig("dt_w"), i * 2 + 2)
                v.tensor_tensor(dz[:, :], du[:, :], dr[:, :], ALU.mult).then_inc(sig("dt_z"), 1)
                v.tensor_scalar(dv[:, :], dv[:, :], 0.0, None, ALU.max).then_inc(sig("dt_z"), 1)
                yield "A07"
                v.wait_ge(sig("cb_ps"), i + 1)
                v.tensor_tensor(cbm[:, :, :], PA[:, 1, 0:T * S].rearrange("p (t s) -> p t s", t=T),
                                seen[:, :].unsqueeze(1).broadcast_to([P, T, S]), ALU.mult).then_inc(sig("cbm_ready"), 1)
                yield "A08"
                v.wait_ge(sig("dt_poly"), i * 18 + 18)
                v.wait_ge(sig("dt_z"), i * 2 + 2)
                dtf = dtt[:, :, :].rearrange("p t k -> p (t k)")
                v.scalar_tensor_tensor(dtf, dp[:, :], 2.0, dv[:, :], ALU.mult, ALU.add).then_inc(sig("dt_ready"), 1)
                v.wait_ge(sig("dt_ready"), i + 1)
                v.tensor_tensor(aa[:, :, :], dtt[:, :, :], negA[:, :].unsqueeze(1).broadcast_to([P, T, NH]),
                                ALU.mult).then_inc(sig("a_ready"), 1)
                yield "A09"
                for k in range(2):
                    v.wait_ge(sig("xT_ps"), i * 2 + k + 1)
                    v.tensor_tensor(xdt[:, 2 * k:2 * k + 2, :, :], PA[:, 2 + k, :].rearrange("p (t k s) -> p t k s", t=2, k=NH),
                                    dtt[:, 2 * k:2 * k + 2, :].unsqueeze(3).broadcast_to([P, 2, NH, S]),
                                    ALU.mult).then_inc(sig("xdt_ready"), 1)
                yield "A10"
                for t in range(T):
                    if t == 0:
                        v.wait_ge(sig("cbm_ready"), i + 1)
                    if t % 2 == 0:
                        if t:
                            yield "A10"
                        v.wait_ge(sig("decay"), i * 2 + t // 2 + 1)
                    v.tensor_tensor(M[:, t, :, :], dec[:, t, :, :], cbm[:, t, :].unsqueeze(1).broadcast_to([P, NH, S]),
                                    ALU.mult).then_inc(sig("M_ready"), 1)
                yield "A11"
                for k in range(2):
                    v.wait_ge(sig("y_ps"), i + 1)
                    for b in range(2):
                        of = lambda ap: ap.rearrange("p (t b s) -> p b t s", t=T, b=2)[:, b]
                        ins = v.scalar_tensor_tensor(of(y2[:, k, :]), of(xc[:, k, :]), dskip[:, k:k + 1],
                                                     PA[:, 2 * b + k, 0:T * S].rearrange("p (t s) -> p t s", t=T), ALU.mult,
                                                     ALU.add)
                    ins.then_inc(sig("y_skip"), 1)
                for k in range(2):
                    v.wait_ge(sig("y_skip"), i * 2 + k + 1)
                    v.tensor_tensor(y2[:, k, :], y2[:, k, :], zs[:, k, :], ALU.mult).then_inc(sig("g_ready"), 1)
                yield "A12"
                v.wait_ge(sig("gate_ps"), i + 1)
                v.tensor_scalar(rgi[:, :], PA[:, 3, 0:T], 1.0 / DI, 1e-5, ALU.mult, ALU.add).then_inc(sig("gate_var"), 1)
                yield "A13"
                v.wait_ge(sig("gate_rstd"), i + 1)
                v.wait_ge(sig("mix_ps"), i + 1)
                for t in range(T):
                    v.scalar_tensor_tensor(x1[:, t, :], PA[:, 2, t * P:t * P + P], rg[:, t:t + 1], u[:, t, :], ALU.mult,
                                           ALU.add).then_inc(sig("x1_ready"), 1)
                v.wait_ge(sig("x1_ready"), i * 4 + 4)
                stats(x1, i * 16 + 4, i * 16 + 4, st, mv, "ln_stat", "ln_mean")
                v.tensor_tensor(msq[:, :], mv[:, :, 0], mv[:, :, 0], ALU.mult).then_inc(sig("msq_ready"), 1)
                v.wait_ge(sig("msq_ready"), i + 1)
                v.scalar_tensor_tensor(var[:, :, 0], msq[:, :], 1e-6, mv[:, :, 1], ALU.add, ALU.add).then_inc(sig("ln_var"), 1)
                yield "A14"
                v.wait_ge(sig("xb_ready"), i + 1)
                v.tensor_tensor(xb[:, :, :], xb[:, :, :], x1[:, :, :], ALU.add).then_inc(sig("xb_sum"), 1)
                v.wait_ge(sig("ln_rstd"), i * 4 + 2)
                for t in range(T):
                    v.tensor_scalar(h[:, t, :], x1[:, t, :], rs[:, t, 0:1], None, ALU.mult).then_inc(sig("h_ready"), 1)
                yield "A16"
                v.wait_ge(sig("xb_sum"), i + 1)
                v.wait_ge(sig("mlp_ps"), i + 1)
                v.tensor_tensor(xA[:, :, :], PA[:, 3, :].rearrange("p (t d) -> p t d", t=T), xb[:, :, :],
                                ALU.add).then_inc(sig("xA_ready"), 1)

                yield "A17"
                v.wait_ge(sig("xA_ready"), i + 1)
                stats(xA, i * 16 + 8, i * 16 + 8, st, mv, "ln_stat", "ln_mean")
                v.tensor_scalar(var[:, :, 0], mv[:, :, 1], 1e-5, None, ALU.add).then_inc(sig("ln_var"), 1)
                yield "A18"
                v.wait_ge(sig("ptr_loaded"), i * 16 + 16)
                for k in range(3):
                    v.tensor_scalar(pf[:, :, k], ptr[:, :], float(k), 0.0, ALU.add, ALU.max).then_inc(sig("pf"), 1)
                v.wait_ge(sig("pf"), i * 4 + 3)
                v.tensor_scalar(pf[:, :, :], pf[:, :, :], float(S - 1), None, ALU.min).then_inc(sig("pf"), 1)
                v.wait_ge(sig("pf"), i * 4 + 4)
                for t in range(T):
                    v.tensor_tensor(O[:, t, :, :], pf[:, t, :].unsqueeze(2).broadcast_to([P, 3, S]),
                                    iota[:, :].unsqueeze(1).broadcast_to([P, 3, S]), ALU.is_equal).then_inc(sig("O_ready"), 1)
                v.wait_ge(sig("O_ready"), i * 4 + 4)
                v.wait_ge(sig("ids_loaded"), i * 32 + 32)
                v.tensor_tensor(rprod[:, :, :], O[:, :, 0, :], idsb[:, :, :], ALU.mult).then_inc(sig("ids_free"), 1)
                v.wait_ge(sig("ids_free"), i + 1)
                v.tensor_reduce(rid[:, :], rprod[:, :, :], AX.X, ALU.add).then_inc(sig("rid_ready"), 1)
                v.wait_ge(sig("rid_ready"), i + 1)
                v.tensor_tensor(R[:, :, 0:5], rid[:, :].unsqueeze(2).broadcast_to([P, T, 5]),
                                iota[:, 0:5].unsqueeze(1).broadcast_to([P, T, 5]), ALU.is_equal).then_inc(sig("R_ready"), 1)
                v.wait_ge(sig("R_ready"), i * 3 + 1)
                v.tensor_reduce(R[:, :, 5], R[:, :, 0:5], AX.X, ALU.add).then_inc(sig("R_ready"), 1)
                v.wait_ge(sig("R_ready"), i * 3 + 2)
                v.tensor_scalar(R[:, :, 5], R[:, :, 5], -1.0, 1.0, ALU.mult, ALU.add).then_inc(sig("R_ready"), 1)
                yield "A19"
                v.wait_ge(sig("ln_rstd"), i * 4 + 3)
                for t in range(T):
                    v.tensor_scalar(h[:, t, :], xA[:, t, :], mv[:, t, 0:1], rs[:, t, 0:1], ALU.subtract,
                                    ALU.mult).then_inc(sig("h_ready"), 1)
                yield "A21"
                v.wait_ge(sig("sx_ps"), i + 1)
                sx = PA[:, 3, :].rearrange("p (t x s) -> p x t s", t=T, x=2)
                for x_ in range(2):
                    for k in range(3):
                        v.tensor_tensor(prod[:, x_, :, k, :], sx[:, x_], O[:, :, k, :], ALU.mult).then_inc(sig("sx_prod"), 1)
                for x_ in range(2):
                    v.wait_ge(sig("sx_prod"), i * 6 + 3 * x_ + 3)
                    v.tensor_reduce(sc[:, x_, :, :], prod[:, x_, :, :, :], AX.X, ALU.add).then_inc(sig("sx_ready"), 1)
                yield "A22"
                v.wait_ge(sig("sx_ready"), i * 2 + 2)
                l0, l1, l2 = (sc[:, 0, :, k] for k in range(3))
                v.tensor_tensor(V6[:, :, 0], l1, l2, ALU.add)
                v.tensor_tensor(V6[:, :, 1], l1, l2, ALU.max)
                v.tensor_scalar(V6[:, :, 2], l1, -1.0, None, ALU.mult)
                v.scalar_tensor_tensor(V6[:, :, 3], l1, -1.0, l2, ALU.mult, ALU.max)
                v.tensor_tensor(V6[:, :, 4], l1, l2, ALU.subtract)
                v.tensor_copy(V6[:, :, 5], l0).then_inc(sig("V6"), 1)
                v.wait_ge(sig("V6"), i * 3 + 1)
                v.scalar_tensor_tensor(V6[:, :, 4], V6[:, :, 4], -1.0, V6[:, :, 4], ALU.mult, ALU.max).then_inc(sig("V6"), 1)
                v.wait_ge(sig("V6"), i * 3 + 2)
                v.tensor_tensor(V6[:, :, :], V6[:, :, :], R[:, :, :], ALU.mult).then_inc(sig("V6"), 1)
                v.wait_ge(sig("V6"), i * 3 + 3)
                v.tensor_reduce(l0, V6[:, :, :], AX.X, ALU.add).then_inc(sig("sm"), 1)
                sc8 = sc[:, :, :, :].rearrange("p x t k -> p (x t) k")
                v.wait_ge(sig("sm"), i * 6 + 1)
                v.tensor_reduce(smx[:, :], sc8, AX.X, ALU.max).then_inc(sig("sm"), 1)
                v.wait_ge(sig("sm"), i * 6 + 2)
                v.tensor_tensor(sc8, sc8, smx[:, :].unsqueeze(2).broadcast_to([P, 2 * T, 3]), ALU.subtract).then_inc(sig("sm"), 1)
                yield "A23"
                v.wait_ge(sig("sm_exp"), i + 1)
                v.tensor_reduce(ssm[:, :], sc8, AX.X, ALU.add).then_inc(sig("sm"), 1)
                v.wait_ge(sig("sm"), i * 6 + 4)
                v.reciprocal(ssm[:, :], ssm[:, :]).then_inc(sig("sm"), 1)
                v.wait_ge(sig("sm"), i * 6 + 5)
                v.tensor_tensor(sc8, sc8, ssm[:, :].unsqueeze(2).broadcast_to([P, 2 * T, 3]), ALU.mult).then_inc(sig("sm"), 1)
                yield "A24"
                for x_ in range(2):
                    v.wait_ge(sig("OW_ready"), i * 8 + 4 * x_ + 4)
                    v.tensor_tensor(Pm[:, :, x_, :], prod[:, x_, :, 0, :], prod[:, x_, :, 1, :], ALU.add).then_inc(sig("Pm_part"), 1)
                for x_ in range(2):
                    v.wait_ge(sig("Pm_part"), i * 2 + x_ + 1)
                    v.tensor_tensor(Pm[:, :, x_, :], Pm[:, :, x_, :], prod[:, x_, :, 2, :], ALU.add).then_inc(sig("Pm_ready"), 1)
                yield "A26"
                v.wait_ge(sig("xo_ps"), i + 1)
                v.tensor_tensor(xA[:, :, :], xA[:, :, :], PA[:, 3, :].rearrange("p (t d) -> p t d", t=T),
                                ALU.add).then_inc(sig("x2_ready"), 1)

                yield "A27"
                v.wait_ge(sig("x2_ready"), i + 1)
                stats(xA, i * 16 + 12, i * 16 + 12, st, mv, "ln_stat", "ln_mean")
                v.tensor_scalar(var[:, :, 0], mv[:, :, 1], 1e-5, None, ALU.add).then_inc(sig("ln_var"), 1)
                yield "A28"
                v.wait_ge(sig("ln_rstd"), i * 4 + 4)
                for t in range(T):
                    v.tensor_scalar(h[:, t, :], xA[:, t, :], mv[:, t, 0:1], rs[:, t, 0:1], ALU.subtract,
                                    ALU.mult).then_inc(sig("h_ready"), 1)

                def row_scale(k):
                    v.wait_ge(sig("q_small"), i * 10 + 5 * k + 1)
                    v.tensor_scalar(amx[:, :], amx[:, :], 1e-5, None, ALU.max).then_inc(sig("q_small"), 1)
                    v.wait_ge(sig("q_small"), i * 10 + 5 * k + 2)
                    v.reciprocal(ainv[:, :], amx[:, :]).then_inc(sig("q_small"), 1)
                    v.tensor_scalar(asc[:, :], amx[:, :], fs127[:, k:k + 1], None, ALU.mult).then_inc(sig("q_small"), 1)
                    v.wait_ge(sig("q_small"), i * 10 + 5 * k + 4)
                    v.tensor_scalar(ainv[:, :], ainv[:, :], 127.0, None, ALU.mult).then_inc(sig("q_small"), 1)

                v.wait_ge(sig("h_ready"), i * 16 + 16)
                v.tensor_reduce(amx[:, :], h[:, :, :], AX.X, ALU.max, apply_absolute_value=True).then_inc(sig("q_small"), 1)
                row_scale(0)
                v.wait_ge(sig("q_small"), i * 10 + 5)
                for t in range(T):
                    v.tensor_scalar(t32[:, t, :], h[:, t, :], ainv[:, t:t + 1], MAGIC, ALU.mult, ALU.add).then_inc(sig("t32"), 1)
                v.wait_ge(sig("t32"), i * 4 + 4)
                v.tensor_scalar(xq[:, :, :], t32[:, :, :], MAGIC, 127.0, ALU.subtract, ALU.min).then_inc(sig("xq_ready"), 1)
                yield "A29"
                for t in range(T):
                    if t:
                        yield "A29"
                    v.wait_ge(sig("f1_ps"), i * 4 + t + 1)
                    v.scalar_tensor_tensor(hb[:, t, :], PA[:, t, :], asc[:, t:t + 1], fb1[:, :], ALU.mult,
                                           ALU.add).then_inc(sig("hb_ready"), 1)
                yield "A30"
                for t in range(T):
                    if t:
                        yield "A30"
                    v.wait_ge(sig("gelu"), i * 4 + t + 1)
                    ins = v.tensor_reduce(amx[:, t:t + 1], hb[:, t, :], AX.X, ALU.max, apply_absolute_value=True)
                ins.then_inc(sig("q_small"), 1)
                row_scale(1)
                yield "A31"
                for t in range(T):
                    if t:
                        yield "A31"
                    v.wait_ge(sig("g32"), i * 4 + t + 1)
                    v.tensor_scalar(gq[:, t, :], g32[:, t, :], MAGIC, 127.0, ALU.subtract, ALU.min).then_inc(sig("gq_ready"), 1)
                yield "A32"
                v.wait_ge(sig("q_small"), i * 10 + 10)
                v.wait_ge(sig("xb2_ready"), i + 1)
                v.wait_ge(sig("f2_ps"), i + 1)
                if not first(i):
                    v.wait_ge(sig("xh_ready"), i)
                    v.wait_ge(sig("bhT_ready"), i * 3)
                for t in range(T):
                    v.scalar_tensor_tensor(xB[:, t, :], PA[:, 3, t * P:t * P + P], asc[:, t:t + 1], xb[:, t, :], ALU.mult,
                                           ALU.add).then_inc(sig("xB_part"), 1)
                yield from norm(i, 0)
                yield from queries_keys(i, 0, 2, qkb[:, :], PA)
                values(i, 0, vb_par, PA)

            def chain_b(i):
                def top(k, r, j):
                    n_ = (i * 3 + k) * 8 + 4 * r + j
                    src = PB[:, j, :].rearrange("p (a s) -> p a s", s=S)
                    v.wait_ge(sig("s_ps"), n_ + 1)
                    if k == 2:
                        if r == 0 and j == 0:
                            v.wait_ge(sig("mask_loaded"), i * 16 + 16)
                        v.tensor_tensor(Pr[:, j, :, :].rearrange("p (t c) s -> p t c s", t=2), src.rearrange("p (t c) s -> p t c s", t=2),
                                        maskE[:, 2 * r:2 * r + 2, :].unsqueeze(2).broadcast_to([P, 2, 4, S]),
                                        ALU.add).then_inc(sig("s_biased"), 1)
                        v.wait_ge(sig("s_biased"), i * 8 + 4 * r + j + 1)
                        src = Pr[:, j, :, :]
                    v.tensor_reduce(mx[:, j, :], src, AX.X, ALU.max).then_inc(sig("mx"), 1)

                def shift(k, r, j):
                    n_ = (i * 3 + k) * 8 + 4 * r + j
                    src = Pr[:, j, :, :] if k == 2 else PB[:, j, :].rearrange("p (a s) -> p a s", s=S)
                    v.wait_ge(sig("mx"), n_ + 1)
                    v.tensor_tensor(Pr[:, j, :, :], src, mx[:, j, :].unsqueeze(2).broadcast_to([P, 8, S]),
                                    ALU.subtract).then_inc(sig("s_shifted"), 1)

                def attend(k):
                    for r in range(2):
                        yield f"B{k}{4 + 3 * r}"
                        top(k, r, 0)
                        for j in range(1, 4):
                            top(k, r, j)
                            shift(k, r, j - 1)
                            yield f"B{k}{4 + 3 * r}"
                        shift(k, r, 3)
                        yield f"B{k}{5 + 3 * r}"
                        v.wait_ge(sig("pT_ps"), (i * 3 + k) * 8 + 4 * r + 4)
                        v.tensor_copy(PT[:, 3, :, :].rearrange("p a s -> p (a s)"), PB[:, 3, :]).then_inc(sig("PT_dve"), 1)
                        yield f"B{k}{6 + 3 * r}"
                        v.wait_ge(sig("pv_ps"), (i * 3 + k) * 2 + r + 1)
                        pv = PB[:, :, 0:8 * (HD + 1)].rearrange("p j (a d) -> p j a d", d=HD + 1)
                        v.reciprocal(rc[:, :, :], pv[:, :, :, HD]).then_inc(sig("rc"), 1)
                        v.wait_ge(sig("rc"), (i * 3 + k) * 2 + r + 1)
                        for t2 in range(2):
                            a4 = slice(4 * t2, 4 * t2 + 4)
                            v.tensor_tensor(cx[:, 2 * r + t2, :].rearrange("p (j a d) -> p j a d", j=4, a=4), pv[:, :, a4, 0:HD],
                                            rc[:, :, a4].unsqueeze(3).broadcast_to([P, 4, 4, HD]), ALU.mult).then_inc(sig("cx_ready"), 1)

                yield from attend(0)
                yield "C0"
                v.wait_ge(sig("cxT_ready"), i * 3 + 1)
                v.tensor_copy(cxT[:, 0, :, 1:S], cxT[:, 1, :, 0:S - 1]).then_inc(sig("cxT_shifted"), 1)
                v.tensor_copy(cxT[:, 2, :, 0:S - 1], cxT[:, 1, :, 1:S]).then_inc(sig("cxT_shifted"), 1)
                yield from queries_keys(i, 1, 1, cvb[:, :], PB)
                yield from attend(1)
                yield "C1"
                v.wait_ge(sig("xo_ready"), i + 1)
                v.wait_ge(sig("o_ps"), i * 2 + 1)
                v.tensor_tensor(xB[:, :, :], xo[:, :, :], PB[:, 1, :].rearrange("p (t d) -> p t d", t=T),
                                ALU.add).then_inc(sig("xB_sum"), 1)
                v.wait_ge(sig("xB_sum"), i * 2 + 1)
                yield from norm(i, 1)
                yield from queries_keys(i, 2, 2, None, PB)
                values(i, 1, None, PB)
                yield from attend(2)
                yield "C2"
                v.wait_ge(sig("o_ps"), i * 2 + 2)
                v.tensor_tensor(xB[:, :, :], xB[:, :, :], PB[:, 1, :].rearrange("p (t d) -> p t d", t=T),
                                ALU.add).then_inc(sig("xB_sum"), 1)
                v.wait_ge(sig("xB_sum"), i * 2 + 2)
                yield from norm(i, 2)
                yield "E02"
                v.wait_ge(sig("bhh_ready"), i + 1)
                v.tensor_tensor(bhl[:, :], bhT[:, :], bhh[:, :], ALU.subtract).then_inc(sig("bhl_ready"), 1)
                v.wait_ge(sig("lg_ps"), i + 1)
                v.tensor_copy(lg[:, :, :], PB[:, 3, 0:T * E].rearrange("p (t e) -> p t e", t=T)).then_inc(sig("lg"), 1)
                v.wait_ge(sig("lg"), i + 1)
                v.memset(mark[:, :], 0.0)
                for t in range(T):
                    v.max(m8[:, t, :], lg[:, t, :]).then_inc(sig("m8"), 1)
                v.wait_ge(sig("m8"), i * 4 + 4)
                v.memset(mark[:, :], 0.0)
                for t in range(T):
                    v.max_index(ix8[:, t, :], m8[:, t, :], lg[:, t, :]).then_inc(sig("ix8"), 1)
                k0 = i * 11
                v.tensor_tensor(e8[:, :, :], m8[:, :, :], m8[:, :, 0:1].broadcast_to([P, T, E]), ALU.subtract).then_inc(sig("gates"), 1)
                v.wait_ge(sig("ix8"), i * 4 + 4)
                v.tensor_copy(ixf[:, :, :], ix8[:, :, 0:2]).then_inc(sig("gates"), 1)
                v.wait_ge(sig("gates"), k0 + 2)
                for t in range(T):
                    ins = v.tensor_tensor(oh[:, t, :, :], iota[:, 0:E].unsqueeze(1).broadcast_to([P, 2, E]),
                                          ixf[:, t, :].unsqueeze(2).broadcast_to([P, 2, E]), ALU.is_equal)
                ins.then_inc(sig("gates"), 1)
                yield "E03"
                v.wait_ge(sig("e8_exp"), i + 1)
                v.tensor_reduce(s8[:, :], e8[:, :, :], AX.X, ALU.add).then_inc(sig("gates"), 1)
                v.wait_ge(sig("gates"), k0 + 4)
                v.reciprocal(r8[:, :], s8[:, :]).then_inc(sig("gates"), 1)
                v.wait_ge(sig("gates"), k0 + 5)
                v.tensor_tensor(g2[:, :, :], e8[:, :, 0:2], r8[:, :].unsqueeze(2).broadcast_to([P, T, 2]), ALU.mult).then_inc(sig("gates"), 1)
                v.wait_ge(sig("gates"), k0 + 6)
                v.scalar_tensor_tensor(d2[:, :], g2[:, :, 0], 1e-8, g2[:, :, 1], ALU.add, ALU.add).then_inc(sig("gates"), 1)
                v.wait_ge(sig("gates"), k0 + 7)
                v.reciprocal(r8[:, :], d2[:, :]).then_inc(sig("gates"), 1)
                v.wait_ge(sig("gates"), k0 + 8)
                v.tensor_tensor(cw2[:, :, :], g2[:, :, :], r8[:, :].unsqueeze(2).broadcast_to([P, T, 2]), ALU.mult).then_inc(sig("gates"), 1)
                v.wait_ge(sig("gates"), k0 + 9)
                for t in range(T):
                    ins = v.tensor_tensor(oh[:, t, :, :], oh[:, t, :, :], cw2[:, t, :].unsqueeze(2).broadcast_to([P, 2, E]), ALU.mult)
                ins.then_inc(sig("gates"), 1)
                v.wait_ge(sig("gates"), k0 + 10)
                v.tensor_tensor(cwt[:, :, :], oh[:, :, 0, :], oh[:, :, 1, :], ALU.add).then_inc(sig("gates"), 1)
                for e in range(E + 1):
                    yield f"X{e}"
                    if e == 0:
                        if not first(i):
                            v.wait_ge(sig("stored"), i * 16)
                        v.wait_ge(sig("xh_ready"), i + 1)
                    if e < E:
                        v.wait_ge(sig("w1_ps"), i * 16 + 2 * e + 2)
                        if e >= 2:
                            v.wait_ge(sig("w2_ps"), i * 8 + e - 1)
                        v.tensor_scalar(hid[:, e % 2, 1, :], PB[:, 1, :], mb1[:, 2 * e + 1:2 * e + 2], 0.0, ALU.add,
                                        ALU.max).then_inc(sig("hid_dve"), 1)
                    if e < E:
                        yield f"X{e}"
                    if e == 0:
                        v.wait_ge(sig("b2_ps"), i + 1)
                        v.tensor_tensor(acc[:, :, :], xo[:, :, :], PB[:, 3, :].rearrange("p (t d) -> p t d", t=T),
                                        ALU.add).then_inc(sig("acc"), 1)
                    else:
                        v.wait_ge(sig("w2_ps"), i * 8 + e)
                        for t in range(T):
                            if t == 0:
                                v.wait_ge(sig("acc"), i * 8 + e)
                            ins = v.scalar_tensor_tensor(acc[:, t, :], PB[:, 2 + (e - 1) % 2, t * P:t * P + P], cwt[:, t, e - 1:e],
                                                         acc[:, t, :], ALU.mult, ALU.add)
                            if e == E:
                                ins.then_inc(sig("out_ready"), 1)
                        if e < E:
                            ins.then_inc(sig("acc"), 1)

            alone(chain_a(0))
            with v.Fori(1, groups) as i:
                interleave(ORDER["vector"], chain_a(i), chain_b(i - 1))
            alone(chain_b(groups - 1))

        @block.scalar
        def _(act):
            for dst, src in FIRST[1::2]:
                act.dma_start(dst, src, allow_slow_non_contiguous=True).then_inc(sig("first_loaded"), 16)
            for dst, src in LOADS[1::2]:
                act.dma_start(dst, src, allow_slow_non_contiguous=True).then_inc(sig("weights_loaded"), 16)
            act.wait_ge(sig("weights_loaded"), 16 * NLOADS)
            act.activation(negA[:, :], alog[:, :], ACT.Exp).then_inc(sig("act_setup"), 1)
            act.wait_ge(sig("dve_setup"), 2)
            act.activation(council[:, :], council[:, :], ACT.Exp).then_inc(sig("act_setup"), 1)
            act.wait_ge(sig("setup_done"), 3)

            def copy(dst, src, wait, value, done):
                act.wait_ge(sig(wait), value)
                act.activation(dst, src, ACT.Copy).then_inc(sig(done), 1)

            def split_hi(i, k, what):
                for r in range(2):
                    if r:
                        yield f"B{k}2"
                    act.wait_ge(sig("qk32"), i * 6 + 2 * k + r + 1)
                    for q in range(what):
                        src = qk32[:, 2 * r:2 * r + 2, q, :].rearrange("p t (h d) -> p t h d", h=H)
                        for n_, slot in enumerate((0, 8) if q == 0 else (0, 16)):
                            ins = act.activation(aug[:, q, 2 * r:2 * r + 2, :, slot:slot + HD], src, ACT.Copy)
                        ins.then_inc(sig("aug_hi"), 1)

            def transposed(i, k, what, ps):
                for t in range(T):
                    if t:
                        yield f"B{k}3"
                    act.wait_ge(sig("augT_ps"), (i * 3 + k) * T + t + 1)
                    w_ = 256 * what
                    act.activation(augT[:, t, 0:what, :, :].rearrange("p q c k -> p (q c k)").bitcast(fp32),
                                   ps[:, t, 0:w_], ACT.Copy).then_inc(sig("augT_ready"), 1)

            def chain_a(i):
                yield "A02"
                copy(hT[:, :], PA[:, 0, :], "hT_ps", i * 3 + 1, "hT_ready")
                yield "A03"
                for k in range(2):
                    if k:
                        yield "A03"
                    act.wait_ge(sig("z_ps"), i * 2 + k + 1)
                    act.activation(zs[:, k, :], PA[:, (1, 3)[k], :], ACT.Silu).then_inc(sig("z_ready"), 1)
                for c_ in range(3):
                    yield "A03"
                    act.wait_ge(sig("xbc_ps"), i * 3 + c_ + 1)
                    if c_ < 2:
                        act.activation(xc[:, c_, :], PA[:, (2, 0)[c_], :], ACT.Identity, bias=cb_x[:, c_:c_ + 1],
                                       scale=cw_x[:, c_, 2:3]).then_inc(sig("conv_tap"), 1)
                    else:
                        act.activation(bcc[:, :], PA[0:48, 1, :], ACT.Identity, bias=cb_bc[:, :],
                                       scale=cw_bc[:, 2:3]).then_inc(sig("conv_tap"), 1)
                yield "A04"
                for c_ in range(2):
                    if c_:
                        yield "A04"
                    act.wait_ge(sig("conv_done"), i * 6 + 2 * c_ + 2)
                    act.activation(xc[:, c_, :], xc[:, c_, :], ACT.Silu).then_inc(sig("xs_ready"), 1)
                yield "A04"
                act.wait_ge(sig("conv_done"), i * 6 + 6)
                act.activation(bT[:, :], bcc[0:NS, :], ACT.Silu).then_inc(sig("bc_ready"), 1)
                act.activation(cT[:, :], bcc[32:32 + NS, :], ACT.Silu).then_inc(sig("bc_ready"), 1)
                yield "A05"
                act.wait_ge(sig("dt_n"), i + 1)
                act.activation(du[:, :], dn[:, :], ACT.Exp).then_inc(sig("dt_u"), 1)
                yield "A09"
                for k in range(2):
                    if k:
                        yield "A09"
                    act.wait_ge(sig("seg_ps"), i * 2 + k + 1)
                    act.activation(dec[:, 2 * k:2 * k + 2, :, :].rearrange("p t k s -> p (t k s)"), PA[:, (0, 1)[k], :],
                                   ACT.Exp).then_inc(sig("decay"), 1)
                yield "A11"
                for k in range(2):
                    act.wait_ge(sig("g_ready"), i * 2 + k + 1)
                    act.activation(gsq[:, k, :], y2[:, k, :], ACT.Square).then_inc(sig("gsq"), 1)
                yield "A14"
                copy(hT[:, :], PA[:, 0, :], "hT_ps", i * 3 + 2, "hT_ready")
                yield "A15"
                for k in range(4):
                    if k:
                        yield "A15"
                    act.wait_ge(sig("mh_ps"), i * 4 + k + 1)
                    act.activation(hs[:, k, :], PA[:, (1, 2)[k % 2], :], ACT.Silu, bias=b1m[:, k:k + 1]).then_inc(sig("hs"), 1)
                yield "A18"
                copy(ctxT[:, :, :].rearrange("p t s -> p (t s)"), PA[:, 0, :], "cxT_ps", i + 1, "ctxT_ready")
                yield "A19"
                copy(hT[:, :], PA[:, 1, :], "hT_ps", i * 3 + 3, "hT_ready")
                yield "A20"
                for k in range(2):
                    if k:
                        yield "A20"
                    copy(qx[:, k, :], PA[:, (0, 2)[k], :], "qx_ps", i * 2 + k + 1, "qx_ready")
                yield "A21"
                for k in range(2):
                    if k:
                        yield "A21"
                    copy(Vc[:, 4 * k:4 * k + 4, :].rearrange("p b d -> p (b d)"), PA[:, 1 + k, :],
                         "vc_ps", i * 2 + k + 1, "Vc_ready")
                yield "A22"
                act.wait_ge(sig("sm"), i * 6 + 3)
                sc24 = sc[:, :, :, :].rearrange("p x t k -> p (x t k)")
                act.activation(sc24, sc24, ACT.Exp).then_inc(sig("sm_exp"), 1)
                yield "A24"
                copy(PmT[:, :, :].rearrange("p t s -> p (t s)"), PA[:, 0, :], "PmT_ps", i + 1, "PmT_ready")
                yield "A28"
                copy(xqT[:, :].bitcast(fp32), PA[:, 0, 0:256], "xqT_ps", i + 1, "xqT_ready")
                yield "A29"
                for t in range(T):
                    if t:
                        yield "A29"
                    act.wait_ge(sig("hb_ready"), i * 4 + t + 1)
                    act.activation(hb[:, t, :], hb[:, t, :], ACT.Gelu).then_inc(sig("gelu"), 1)
                yield "A30"
                act.wait_ge(sig("q_small"), i * 10 + 10)
                for t in range(T):
                    act.activation(g32[:, t, :], hb[:, t, :], ACT.Copy, bias=MAGIC, scale=ainv[:, t:t + 1]).then_inc(sig("g32"), 1)
                yield "A31"
                for t in range(T):
                    if t:
                        yield "A31"
                    copy(gqT[:, t, :, :].rearrange("p c k -> p (c k)").bitcast(fp32), PA[:, (0, 1)[t % 2], 0:256],
                         "gqT_ps", i * 4 + t + 1, "gqT_ready")
                yield "B01"
                copy(hT[:, :], PA[:, 0, :], "bhT_ps", i * 3 + 1, "bhT_ready")
                yield "B02"
                yield from split_hi(i, 0, 2)
                yield "B03"
                yield from transposed(i, 0, 2, PA)

            def chain_b(i):
                def attend(k):
                    for r in range(2):
                        yield f"B{k}{4 + 3 * r}"
                        for j in range(4):
                            if j:
                                yield f"B{k}{4 + 3 * r}"
                            act.wait_ge(sig("s_shifted"), (i * 3 + k) * 8 + 4 * r + j + 1)
                            pr = Pr[:, j, :, :].rearrange("p a s -> p (a s)")
                            act.activation(pr, pr, ACT.Exp).then_inc(sig("exp_ready"), 1)
                        yield f"B{k}{5 + 3 * r}"
                        for j in range(3):
                            if j:
                                yield f"B{k}{5 + 3 * r}"
                            copy(PT[:, j, :, :].rearrange("p a s -> p (a s)"), PB[:, j, :],
                                 "pT_ps", (i * 3 + k) * 8 + 4 * r + j + 1, "PT_act")

                yield from attend(0)
                yield "C0"
                act.wait_ge(sig("cxo_ps"), i * 3 + 1)
                cxp = PB[:, 1, :].rearrange("p (b s) -> p b s", b=NB)
                act.activation(cxT[:, 1, :, :], cxp, ACT.Copy).then_inc(sig("cxT_ready"), 1)
                yield "B12"
                yield from split_hi(i, 1, 1)
                yield "B13"
                yield from transposed(i, 1, 1, PB)
                yield from attend(1)
                yield "C1"
                copy(bhT[:, :], PB[:, 0, :], "cxo_ps", i * 3 + 2, "cxT_ready")
                yield "B21"
                copy(bhT[:, :], PB[:, 0, :], "bhT_ps", i * 3 + 2, "bhT_ready")
                yield "B22"
                yield from split_hi(i, 2, 2)
                yield "B23"
                yield from transposed(i, 2, 2, PB)
                yield from attend(2)
                yield "C2"
                copy(bhT[:, :], PB[:, 0, :], "cxo_ps", i * 3 + 3, "cxT_ready")
                yield "E01"
                copy(bhT[:, :], PB[:, 0, :], "bhT_ps", i * 3 + 3, "bhT_ready")
                act.activation(bhh[:, :], PB[:, 0, :], ACT.Copy).then_inc(sig("bhh_ready"), 1)
                yield "E02"
                act.wait_ge(sig("gates"), i * 11 + 1)
                act.activation(e8[:, :, :], e8[:, :, :], ACT.Exp).then_inc(sig("e8_exp"), 1)
                yield "E04"
                copy(cwT[:, :], PB[0:E, 2, :], "cwT_ps", i + 1, "cwT_ready")
                for e in range(E):
                    yield f"X{e}"
                    act.wait_ge(sig("w1_ps"), i * 16 + 2 * e + 1)
                    if e >= 2:
                        act.wait_ge(sig("w2_ps"), i * 8 + e - 1)
                    act.activation(hid[:, e % 2, 0, :], PB[:, 0, :], ACT.Relu, bias=mb1[:, 2 * e:2 * e + 1]).then_inc(sig("hid_act"), 1)

            alone(chain_a(0))
            with act.Fori(1, groups) as i:
                interleave(ORDER["scalar"], chain_a(i), chain_b(i - 1))
            alone(chain_b(groups - 1))

        @block.tensor
        def _(pe):
            mm, tr = pe.matmul, pe.transpose
            pe.wait_ge(sig("preset"), 10)
            pe.wait_ge(sig("dve_setup"), 1)
            mm(PA[:, 0, 0:2], ones[:, :], fabs[:, :], start=True, stop=True).then_inc(sig("pe_setup"), 1)
            pe.wait_ge(sig("dve_setup"), 3)
            tr(PA[:, 1, 0:P], xw[:, 6, :], ident[:, :])
            for x_ in range(2):
                mm(PA[:, 1, 128 + 128 * x_:256 + 128 * x_], xw[:, 3 * x_, :], xw[:, 3 * x_ + 1, :], start=True, stop=True)
            for k in range(3):
                tr(PA[:, 2, P * k:P * k + P], aw[:, k, :], ident[:, :])
            tr(PA[:, 2, 384:512], owp[:, :], ident[:, :])
            for k in range(3):
                tr(PA[:, 3, P * k:P * k + P], cvp[:, k, :], ident[:, :])
            for k in range(4):
                tr(PB[:, 0, 64 * k:64 * k + 64].bitcast(bf16), f1q[:, k, :], identb[:, :])
                ins = tr(PB[:, 1, 64 * k:64 * k + 64].bitcast(bf16), f2q[:, P * k:P * k + P], identb[:, :])
            ins.then_inc(sig("pe_setup"), 1)
            pe.wait_ge(sig("dve_setup"), 4)
            for x_ in range(2):
                ins = mm(PA[:, 0, x_ * P:x_ * P + P], xw[:, 3 * x_ + 2, :], woutT[:, :], start=True, stop=True)
            ins.then_inc(sig("pe_setup"), 1)
            pe.wait_ge(sig("setup_done"), 3)

            def tile(t):
                return slice(t * P, t * P + P)

            def seq(t, b):
                return slice(t * P + b * S, t * P + b * S + S)

            def b_norm_T(i, k, ps):
                for t in range(T):
                    pe.wait_ge(sig("bh_ready"), (i * 3 + k) * T + t + 1)
                    ins = tr(ps[:, 0, tile(t)], bh[:, t, :], ident[:, :])
                ins.then_inc(sig("bhT_ps"), 1)

            def values(src, wgt, ps):
                for t in range(T):
                    for b in range(2):
                        for h2 in range(2):
                            ins = mm(ps[S * h2:S * h2 + S, 3, seq(t, b)], src(t, b), wgt[:, h2, :], start=True, stop=True)
                ins.then_inc(sig("v_ps"), 1)

            def transposes(i, k, what, ps):
                pe.wait_ge(sig("aug_lo"), i * 10 + (4, 6, 10)[k])
                if k != 1:
                    pe.wait_ge(sig("v_ready"), i * 4 + (2 if k == 0 else 4))
                for t in range(T):
                    for q in range(what):
                        for c_ in range(4):
                            at = 64 * (4 * q + c_)
                            ins = tr(ps[:, t, at:at + 64].bitcast(fp16),
                                     aug[:, q, t, 4 * c_:4 * c_ + 4, :].rearrange("p h s -> p (h s)"), ident16[:, :])
                    ins.then_inc(sig("augT_ps"), 1)

            def chain_a(i):
                def norm_T(bank, k):
                    for t in range(T):
                        pe.wait_ge(sig("h_ready"), i * 16 + 4 * k + t + 1)
                        ins = tr(PA[:, bank, tile(t)], h[:, t, :], ident[:, :])
                    ins.then_inc(sig("hT_ps"), 1)

                yield "A02"
                if not first(i):
                    pe.wait_ge(sig("augT_ready"), i * 12 - 8)
                norm_T(0, 0)
                yield "A03"
                pe.wait_ge(sig("hT_ready"), i * 3 + 1)
                mm(PA[:, 1, :], w_in[:, 0:P], hT[:, :], start=True, stop=True).then_inc(sig("z_ps"), 1)
                mm(PA[:, 2, :], w_in[:, DI:DI + P], hT[:, :], start=True, stop=True).then_inc(sig("xbc_ps"), 1)
                mm(PA[:, 3, :], w_in[:, P:2 * P], hT[:, :], start=True, stop=True).then_inc(sig("z_ps"), 1)
                mm(PA[:, 0, :], w_in[:, DI + P:DI + 2 * P], hT[:, :], start=True, stop=True).then_inc(sig("xbc_ps"), 1)
                yield "A03"
                pe.wait_ge(sig("z_ready"), i * 2 + 1)
                mm(PA[0:48, 1, :], w_bc[:, :], hT[:, :], start=True, stop=True).then_inc(sig("xbc_ps"), 1)
                pe.wait_ge(sig("z_ready"), i * 2 + 2)
                for t in range(T):
                    ins = mm(PA[:, 3, NH * t:NH * t + NH], hT[:, tile(t)], w_in[:, 2 * DI + 2 * NS:548], start=True, stop=True)
                ins.then_inc(sig("dt_ps"), 1)
                yield "A06"
                pe.wait_ge(sig("bc_ready"), i * 2 + 2)
                for t in range(T):
                    for b in range(2):
                        ins = mm(PA[S * b:S * b + S, 1, t * S:t * S + S], bT[:, seq(t, b)], cT[:, seq(t, b)], start=True, stop=True)
                ins.then_inc(sig("cb_ps"), 1)
                yield "A07"
                pe.wait_ge(sig("xs_ready"), i * 2 + 2)
                pe.wait_ge(sig("dt_v"), i + 1)
                for k in range(2):
                    for t in (2 * k, 2 * k + 1):
                        for c_ in range(2):
                            ins = tr(PA[:, 2 + k, 256 * (t % 2) + P * c_:256 * (t % 2) + P * c_ + P], xc[:, c_, tile(t)], ident[:, :])
                    ins.then_inc(sig("xT_ps"), 1)
                yield "A08"
                pe.wait_ge(sig("cbm_ready"), i + 1)
                for k in range(2):
                    if k:
                        yield "A08"
                    pe.wait_ge(sig("G_ready"), i * 4 + 2 * k + 2)
                    mm(PA[:, k, :], after[:, :], G[:, 2 * k:2 * k + 2, :, :].rearrange("p t k s -> p (t k s)"),
                       start=True, stop=True).then_inc(sig("seg_ps"), 1)
                yield "A10"
                pe.wait_ge(sig("M_ready"), i * 4 + 4)
                mm(PA[:, 0, 511:512], identb[:, :], identb[:, 0:1], start=True, stop=True)
                for t in range(T):
                    for b in range(2):
                        for hh in range(NH):
                            r = S * (hh % 2)
                            ins = mm(PA[r:r + S, 2 * b + hh // 2, t * S:t * S + S], xdt[S * b:S * b + S, t, hh, :], M[S * b:S * b + S, t, hh, :],
                                     start=True, stop=True)
                ins.then_inc(sig("y_ps"), 1)
                yield "A12"
                for t in range(T):
                    for k in range(2):
                        if t == 0:
                            pe.wait_ge(sig("gsq"), i * 2 + k + 1)
                        ins = mm(PA[:, 3, t:t + 1], gsq[:, k, tile(t)], ones[:, 0:1], start=(k == 0), stop=(k == 1))
                ins.then_inc(sig("gate_ps"), 1)
                for t in range(T):
                    for k in range(2):
                        ins = mm(PA[:, 2, tile(t)], y2[:, k, tile(t)], w_out[:, k, :], start=(k == 0), stop=(k == 1))
                ins.then_inc(sig("mix_ps"), 1)
                yield "A14"
                norm_T(0, 1)
                yield "A15"
                pe.wait_ge(sig("hT_ready"), i * 3 + 2)
                for k in range(4):
                    if k >= 2:
                        yield "A15"
                        pe.wait_ge(sig("hs"), i * 4 + k - 1)
                    mm(PA[:, (1, 2)[k % 2], :], w1m[:, P * k:P * k + P], hT[:, :], start=True, stop=True).then_inc(sig("mh_ps"), 1)
                yield "A15"
                pe.wait_ge(sig("hs"), i * 4 + 4)
                for t in range(T):
                    for k in range(4):
                        ins = mm(PA[:, 3, tile(t)], hs[:, k, tile(t)], w2m[:, k, :], start=(k == 0), stop=(k == 3))
                ins.then_inc(sig("mlp_ps"), 1)

                yield "A18"
                pe.wait_ge(sig("ctx_loaded"), i * 16 + 16)
                for t in range(T):
                    ins = tr(PA[:, 0, tile(t)], ctxn[:, t, :], ident[:, :])
                ins.then_inc(sig("cxT_ps"), 1)
                yield "A19"
                norm_T(1, 2)
                yield "A20"
                pe.wait_ge(sig("ctxT_ready"), i + 1)
                pe.wait_ge(sig("hT_ready"), i * 3 + 3)
                for x_ in range(2):
                    mm(PA[:, (0, 2)[x_], :], wqk[:, x_, :], hT[:, :], start=True, stop=True).then_inc(sig("qx_ps"), 1)
                yield "A21"
                pe.wait_ge(sig("xA_ready"), i + 1)
                pe.wait_ge(sig("qx_ready"), i * 2 + 2)
                for t in range(T):
                    for x_ in range(2):
                        for b in range(2):
                            ins = mm(PA[S * b:S * b + S, 3, t * P + x_ * S:t * P + x_ * S + S], qx[:, x_, seq(t, b)],
                                     ctxT[:, t, b * S:b * S + S], start=True, stop=True)
                ins.then_inc(sig("sx_ps"), 1)
                yield "A21"
                for t in range(T):
                    for b in range(2):
                        for x_ in range(2):
                            ins = mm(PA[S * x_:S * x_ + S, 1 + t // 2, (t % 2) * 2 * P + b * P:(t % 2) * 2 * P + b * P + P],
                                     ctxT[:, t, b * S:b * S + S], wvo[:, x_, :], start=True, stop=True)
                    if t % 2:
                        ins.then_inc(sig("vc_ps"), 1)
                yield "A24"
                pe.wait_ge(sig("Pm_ready"), i * 2 + 2)
                for t in range(T):
                    ins = tr(PA[:, 0, tile(t)], Pm[:, t, :, :].rearrange("p x s -> p (x s)"), ident[:, :])
                ins.then_inc(sig("PmT_ps"), 1)
                yield "A25"
                pe.wait_ge(sig("PmT_ready"), i + 1)
                pe.wait_ge(sig("Vc_ready"), i * 2 + 2)
                for t in range(T):
                    for b in range(2):
                        ins = mm(PA[S * b:S * b + S, 3, tile(t)], PmT[:, t, b * S:b * S + S], Vc[:, 2 * t + b, :], start=True, stop=True)
                ins.then_inc(sig("xo_ps"), 1)

                yield "A28"
                pe.wait_ge(sig("xq_ready"), i + 1)
                for t in range(T):
                    ins = tr(PA[:, 0, S * t:S * t + S].bitcast(bf16), xq[:, t, :], identb[:, :])
                ins.then_inc(sig("xqT_ps"), 1)
                yield "A29"
                pe.wait_ge(sig("xqT_ready"), i + 1)
                for t in range(T):
                    mm(PA[:, t, :], xqT[:, tile(t)], f1T[:, :], start=True, stop=True).then_inc(sig("f1_ps"), 1)
                yield "A31"
                for t in range(T):
                    if t:
                        yield "A31"
                    pe.wait_ge(sig("gq_ready"), i * 4 + t + 1)
                    if t >= 2:
                        pe.wait_ge(sig("gqT_ready"), i * 4 + t - 1)
                    for k in range(4):
                        ins = tr(PA[:, (0, 1)[t % 2], S * k:S * k + S].bitcast(bf16), gq[:, t, k * P:k * P + P], identb[:, :])
                    ins.then_inc(sig("gqT_ps"), 1)
                for t in range(T):
                    yield "A31"
                    pe.wait_ge(sig("gqT_ready"), i * 4 + t + 1)
                    for k in range(4):
                        ins = mm(PA[:, 3, tile(t)], gqT[:, t, k, :], f2T[:, k, :], start=(k == 0), stop=(k == 3))
                ins.then_inc(sig("f2_ps"), 1)
                yield "B01"
                b_norm_T(i, 0, PA)
                yield "B02"
                pe.wait_ge(sig("bhT_ready"), i * 3 + 1)
                for t in range(T):
                    ins = mm(PA[:, t // 2, 256 * (t % 2):256 * (t % 2) + 256], hT[:, tile(t)], wqkT[:, :], start=True, stop=True)
                    if t % 2:
                        ins.then_inc(sig("qk_ps"), 1)
                values(lambda t, b: hT[:, seq(t, b)], wv_par, PA)
                yield "B03"
                transposes(i, 0, 2, PA)

            def chain_b(i):
                def attend(k):
                    for r in range(2):
                        yield f"B{k}{4 + 3 * r}"
                        if r == 0:
                            pe.wait_ge(sig("augT_ready"), (i * 3 + k) * T + T)
                        n_ = (i * 3 + k) * 8 + 4 * r
                        if k == 0 and r == 0 and not first(i):
                            pe.wait_ge(sig("out_ready"), i * T)
                        if r:
                            pe.wait_ge(sig("cx_ready"), (i * 3 + k) * T + 2)
                        for j in range(4):
                            if j:
                                yield f"B{k}{4 + 3 * r}"
                            if k < 2:
                                mm(PB[:, j, :], identb[:, :], causalb[:, :].unsqueeze(1).broadcast_to([P, 8, S]),
                                   start=True, stop=False, skip_group_check=True)
                            rows_ = slice(32 * j, 32 * j + 32)
                            for t2 in range(2):
                                for c_ in range(4):
                                    for b in range(2):
                                        at = (4 * t2 + c_) * S
                                        ins = mm(PB[S * b:S * b + S, j, at:at + S], augT[rows_, 2 * r + t2, 0, c_, S * b:S * b + S],
                                                 augT[rows_, 2 * r + t2, 1, c_, S * b:S * b + S],
                                                 start=(k == 2), stop=True, skip_group_check=True)
                            ins.then_inc(sig("s_ps"), 1)
                        yield f"B{k}{5 + 3 * r}"
                        for j in range(4):
                            if j:
                                yield f"B{k}{5 + 3 * r}"
                            pe.wait_ge(sig("exp_ready"), n_ + j + 1)
                            for a_ in range(4):
                                ins = tr(PB[:, j, P * a_:P * a_ + P], Pr[:, j, 2 * a_:2 * a_ + 2, :].rearrange("p h s -> p (h s)"), ident[:, :])
                            ins.then_inc(sig("pT_ps"), 1)
                        yield f"B{k}{6 + 3 * r}"
                        for j in range(4):
                            if j == 2:
                                yield f"B{k}{6 + 3 * r}"
                            if j < 3:
                                pe.wait_ge(sig("PT_act"), (i * 3 + k) * 6 + 3 * r + j + 1)
                            else:
                                pe.wait_ge(sig("PT_dve"), (i * 3 + k) * 2 + r + 1)
                            for t2 in range(2):
                                for cc in range(2):
                                    for b in range(2):
                                        a_ = 2 * t2 + cc
                                        ins = mm(PB[S * b:S * b + S, j, VW * a_:VW * a_ + VW], PT[:, j, a_, S * b:S * b + S],
                                                 Vx[:, 2 * (2 * r + t2) + b, 2 * j + cc, :], start=True, stop=True)
                        ins.then_inc(sig("pv_ps"), 1)

                def context_T(bank, k):
                    for t in range(T):
                        pe.wait_ge(sig("cx_ready"), (i * 3 + k) * T + t + 1)
                        if t == 0:
                            pe.wait_ge(sig("cx_ready"), (i * 3 + k) * T + T)
                        ins = tr(PB[:, bank, tile(t)], cx[:, t, :], ident[:, :])
                    ins.then_inc(sig("cxo_ps"), 1)

                yield from attend(0)
                yield "C0"
                context_T(1, 0)
                yield "B12"
                pe.wait_ge(sig("cxT_shifted"), i * 2 + 2)
                for t in range(T):
                    for k in range(3):
                        ins = mm(PB[:, t // 2, P * (t % 2):P * (t % 2) + P], cxT[:, k, 2 * t:2 * t + 2, :].rearrange("p b s -> p (b s)"), cvT[:, k, :], start=(k == 0), stop=(k == 2))
                    if t % 2:
                        ins.then_inc(sig("qk_ps"), 1)
                yield "B13"
                transposes(i, 1, 1, PB)
                yield from attend(1)
                yield "C1"
                context_T(0, 1)
                pe.wait_ge(sig("cxT_ready"), i * 3 + 2)
                for t in range(T):
                    ins = mm(PB[:, 1, tile(t)], bhT[:, tile(t)], owT[:, :], start=True, stop=True)
                ins.then_inc(sig("o_ps"), 1)
                yield "B21"
                b_norm_T(i, 1, PB)
                yield "B22"
                pe.wait_ge(sig("bhT_ready"), i * 3 + 2)
                pe.wait_ge(sig("ctxTB_ready"), i + 1)
                pe.wait_ge(sig("xB_sum"), i * 2 + 1)
                for t in range(T):
                    at = 256 * (t % 2)
                    mm(PB[:, t // 2, at:at + P], bhT[:, tile(t)], ewq[:, :], start=True, stop=True)
                    ins = mm(PB[:, t // 2, at + P:at + 2 * P], ctxTB[:, t, :], ewk[:, :], start=True, stop=True)
                    if t % 2:
                        ins.then_inc(sig("qk_ps"), 1)
                values(lambda t, b: ctxTB[:, t, S * b:S * b + S], ewv_par, PB)
                yield "B23"
                transposes(i, 2, 2, PB)
                yield from attend(2)
                yield "C2"
                context_T(0, 2)
                pe.wait_ge(sig("cxT_ready"), i * 3 + 3)
                for t in range(T):
                    ins = mm(PB[:, 1, tile(t)], bhT[:, tile(t)], ewo[:, :], start=True, stop=True)
                ins.then_inc(sig("o_ps"), 1)
                yield "E01"
                b_norm_T(i, 2, PB)
                yield "E02"
                pe.wait_ge(sig("bhT_ready"), i * 3 + 3)
                for t in range(T):
                    ins = mm(PB[:, 3, E * t:E * t + E], bhT[:, tile(t)], gate[:, :], start=True, stop=True)
                ins.then_inc(sig("lg_ps"), 1)

                def up(e):
                    for c_ in range(2):
                        if e >= 1:
                            pe.wait_ge(sig(("hid_act", "hid_dve")[c_]), i * 8 + e)
                        hi, lo = mw1h[:, e, P * c_:P * c_ + P], mw1l[:, e, P * c_:P * c_ + P]
                        mm(PB[:, c_, :], hi, bhh[:, :], start=True, stop=False)
                        mm(PB[:, c_, :], hi, bhl[:, :], start=False, stop=False)
                        mm(PB[:, c_, :], lo, bhh[:, :], start=False, stop=True).then_inc(sig("w1_ps"), 1)

                yield "E02"
                pe.wait_ge(sig("bhl_ready"), i + 1)
                up(0)
                yield "E04"
                pe.wait_ge(sig("gates"), i * 11 + 11)
                for t in range(T):
                    ins = tr(PB[0:E, 2, tile(t)], cwt[:, t, :], ident[:, :])
                ins.then_inc(sig("cwT_ps"), 1)
                yield "E05"
                pe.wait_ge(sig("cwT_ready"), i + 1)
                for t in range(T):
                    ins = mm(PB[:, 3, tile(t)], cwT[:, tile(t)], mb2[:, :], start=True, stop=True)
                ins.then_inc(sig("b2_ps"), 1)
                for e in range(E):
                    yield f"X{e}"
                    if e + 1 < E:
                        up(e + 1)
                    yield f"X{e}"
                    pe.wait_ge(sig("hid_act"), i * 8 + e + 1)
                    pe.wait_ge(sig("hid_dve"), i * 8 + e + 1)
                    if e >= 1:
                        pe.wait_ge(sig("acc"), i * 8 + e)
                    for t in range(T):
                        for c_ in range(2):
                            ins = mm(PB[:, 2 + e % 2, tile(t)], hid[:, e % 2, c_, tile(t)], mw2[:, 2 * e + c_, :], start=(c_ == 0), stop=(c_ == 1))
                    ins.then_inc(sig("w2_ps"), 1)

            alone(chain_a(0))
            with pe.Fori(1, groups) as i:
                interleave(ORDER["tensor"], chain_a(i), chain_b(i - 1))
            alone(chain_b(groups - 1))


_INS = ['x', 'ctx_1024', 'itok_BxS_0_7', 'itok_BxS_0_4092', 'mask_Bx1xSxS2_ff0', 'L0_attn_norm1_w', 'L0_attn_W_in',
        'L0_attn_conv_w', 'L0_attn_conv_b', 'L0_attn_dt_bias', 'L0_attn_A_log', 'L0_attn_D', 'L0_attn_norm_gate_w',
        'L0_attn_W_out', 'L0_attn_norm2_w', 'L0_attn_mlp_w1', 'L0_attn_mlp_b1', 'L0_attn_mlp_w2', 'L0_attn_mlp_b2',
        'L0_xattn_Wqj', 'L0_xattn_Wkj', 'L0_xattn_Wvj', 'L0_xattn_Wqi', 'L0_xattn_Wki', 'L0_xattn_Wvi', 'L0_xattn_Wout',
        'L0_xattn_gain', 'L0_xattn_council_weights', 'L0_ffn_W1', 'L0_ffn_b1', 'L0_ffn_W2', 'L0_ffn_b2',
        'L1_attn_Wqkv_w', 'L1_attn_Wqkv_b', 'L1_attn_conv_w', 'L1_attn_conv_b', 'L1_attn_out_w', 'L1_attn_out_b',
        'L1_xattn_wq', 'L1_xattn_wk', 'L1_xattn_wv', 'L1_xattn_wo', 'L1_ffn_gate_W', 'L1_ffn_W1', 'L1_ffn_b1',
        'L1_ffn_W2', 'L1_ffn_b2']


def kernel(**inputs):
    import numpy as _np
    import concourse.bacc as _bacc
    from concourse import mybir as _mybir
    from concourse.bass_utils import run_bass_kernel_spmd as _run

    nc = _bacc.Bacc("TRN2", target_bir_lowering=False, num_devices=1)
    given = {name: _np.ascontiguousarray(inputs[name]) for name in _INS}
    given["L0_xattn_gain"] = given["L0_xattn_gain"].reshape(1, 1)
    given.update(shape_constants())
    arrays, args = {}, {}
    for name, arr in given.items():
        arrays[f"in_{name}_dram"] = arr
        args[name] = nc.dram_tensor(f"in_{name}_dram", arr.shape, _mybir.dt.from_np(arr.dtype), kind="ExternalInput").ap()
    out = nc.dram_tensor("out_0_dram", (BATCH, S, D), _mybir.dt.float32, kind="ExternalOutput").ap()
    program(nc, args, out)
    r = _run(nc, [arrays], core_ids=[0])
    return r.results[0]["out_0_dram"]
```
